# Optimizing a Trainium2 kernel written in Bass

```python
import numpy as np
import jax
import jax.numpy as jnp

def _softmax(x, axis=-1):
    return jax.nn.softmax(x, axis=axis)

def _gelu(x):
    return jax.nn.gelu(x, approximate=True)

def _silu(x):
    return jax.nn.silu(x)

def _sigmoid(x):
    return jax.nn.sigmoid(x)

def _layernorm(x, axis=-1, eps=1e-05):
    m = jnp.mean(x, axis=axis, keepdims=True)
    v = jnp.var(x, axis=axis, keepdims=True)
    return (x - m) / jnp.sqrt(v + eps)

def _scatter_add(tgt, idx, src, axis=0):
    return tgt.at[idx].add(src)

def _segment_sum(src, seg, n):
    return jax.ops.segment_sum(src, seg, n)
kernel_name = 'mk_macaron_d1_jaxref_r4_3e321f'

def setup_inputs(seed: int=0):
    np.random.seed(seed)
    _w = jnp.asarray

    def _L0_attn_setup():
        import jax, jax.numpy as jnp
        import numpy as np
        D_MODEL = 256
        N_HEADS = 16
        K_TOP = 64
        D_HEAD = D_MODEL // N_HEADS
        key = jax.random.key(seed)
        ks = jax.random.split(key, 9)
        B, L = (8, 1024)
        bound = 1.0 / np.sqrt(D_MODEL)
        lin = lambda k: jax.random.uniform(k, (D_MODEL, D_MODEL), jnp.float32, -bound, bound)
        vec = lambda k: jax.random.uniform(k, (D_MODEL,), jnp.float32, -bound, bound)
        return {'query': jax.random.normal(ks[0], (B, L, D_MODEL), jnp.float32), 'Wq': lin(ks[1]), 'bq': vec(ks[2]), 'Wk': lin(ks[3]), 'bk': vec(ks[4]), 'Wv': lin(ks[5]), 'bv': vec(ks[6]), 'Wo': lin(ks[7]), 'bo': vec(ks[8])}
    _L0_attn_in = _L0_attn_setup()

    def _L0_ffn_setup():
        import jax, jax.numpy as jnp
        import numpy as np
        B, S, H, E = (2, 2048, 256, 8)
        SCALE = 0.5
        key = jax.random.key(seed)
        k1, k2 = jax.random.split(key)
        x = jax.random.normal(k1, (B, S, H), dtype=jnp.float32)
        gate_w = jax.random.normal(k2, (E, H), dtype=jnp.float32) * 0.02
        coeff = SCALE * (1.0 + 0.05 * jnp.arange(E, dtype=jnp.float32))
        expert_w = coeff[:, None, None] * jnp.eye(H, dtype=jnp.float32)
        return {'x': x, 'gate_w': gate_w, 'expert_w': expert_w}
    _L0_ffn_in = _L0_ffn_setup()
    _d = {'L0_attn_query': _L0_attn_in['query'], 'L0_attn_Wq': _L0_attn_in['Wq'], 'L0_attn_bq': _L0_attn_in['bq'], 'L0_attn_Wk': _L0_attn_in['Wk'], 'L0_attn_bk': _L0_attn_in['bk'], 'L0_attn_Wv': _L0_attn_in['Wv'], 'L0_attn_bv': _L0_attn_in['bv'], 'L0_attn_Wo': _L0_attn_in['Wo'], 'L0_attn_bo': _L0_attn_in['bo'], 'L0_ffn_gate_w': _L0_ffn_in['gate_w'], 'L0_ffn_expert_w': _L0_ffn_in['expert_w']}
    _x0 = _d['L0_attn_query']
    _d['L0_attn_query'] = jax.random.normal(jax.random.fold_in(jax.random.key(seed), 1), (16, 1024, 256), dtype=_x0.dtype)
    del _x0
    return _d

def reference(L0_attn_query, L0_attn_Wq, L0_attn_bq, L0_attn_Wk, L0_attn_bk, L0_attn_Wv, L0_attn_bv, L0_attn_Wo, L0_attn_bo, L0_ffn_gate_w, L0_ffn_expert_w):

    def _L0_attn_ref(query, Wq, bq, Wk, bk, Wv, bv, Wo, bo):
        import jax, jax.numpy as jnp
        import numpy as np
        D_MODEL = 256
        N_HEADS = 16
        K_TOP = 64
        D_HEAD = D_MODEL // N_HEADS
        B, L_q, D = query.shape
        L_k = L_q
        F_q = L_q // 2 + 1
        F_k = L_k // 2 + 1
        k_top = min(K_TOP, F_q)

        def proj(x, W, b):
            return (x @ W + b).reshape(B, -1, N_HEADS, D_HEAD).transpose(0, 2, 1, 3)
        q = proj(query, Wq, bq)
        k = proj(query, Wk, bk)
        v = proj(query, Wv, bv)
        q_freq = jnp.fft.rfft(q, axis=2)
        k_freq = jnp.fft.rfft(k, axis=2)
        v_freq = jnp.fft.rfft(v, axis=2)
        q_energy = jnp.abs(q_freq).mean(axis=-1)
        _, idx = jax.lax.top_k(q_energy, k_top)
        mapped_idx = jnp.clip(jnp.round(idx.astype(jnp.float32) * (F_k - 1) / (F_q - 1)).astype(jnp.int32), 0, F_k - 1)
        gather = lambda x, i: jnp.take_along_axis(x, i[..., None], axis=2)
        q_top = gather(q_freq, idx)
        k_top_freq = gather(k_freq, mapped_idx)
        v_top = gather(v_freq, mapped_idx)
        eps = 1e-08
        attn_score = (q_top.real * k_top_freq.real).sum(-1) / (D_HEAD ** 0.5 + eps)
        attn = jax.nn.softmax(attn_score, axis=-1)[..., None]
        q_mean_freq = q_freq.mean(axis=2, keepdims=True)
        out_freq = jnp.broadcast_to(q_mean_freq, (B, N_HEADS, F_q, D_HEAD))
        src = (attn * v_top.real).astype(out_freq.dtype)
        bi = jnp.arange(B)[:, None, None]
        hi = jnp.arange(N_HEADS)[None, :, None]
        out_freq = out_freq.at[bi, hi, idx].set(src)
        out_time = jnp.fft.irfft(out_freq, n=L_q, axis=2)
        out = out_time.transpose(0, 2, 1, 3).reshape(B, L_q, D)
        return out @ Wo + bo

    def _L0_ffn_ref(x, gate_w, expert_w):
        import jax, jax.numpy as jnp
        import numpy as np
        B, S, H, E = (2, 2048, 256, 8)
        SCALE = 0.5
        scores = jnp.einsum('bsh,eh->bse', x, gate_w)
        chosen = jnp.argmax(scores, axis=-1)
        onehot = jax.nn.one_hot(chosen, gate_w.shape[0], dtype=x.dtype)
        expert_out = jnp.einsum('bsh,efh->bsef', x, expert_w)
        return x + jnp.einsum('bsef,bse->bsf', expert_out, onehot)
    x = L0_attn_query
    x = x + 0.5 * _L0_ffn_ref(_layernorm(x, axis=-1), L0_ffn_gate_w, L0_ffn_expert_w)
    x = x + _L0_attn_ref(_layernorm(x, axis=-1), L0_attn_Wq, L0_attn_bq, L0_attn_Wk, L0_attn_bk, L0_attn_Wv, L0_attn_bv, L0_attn_Wo, L0_attn_bo)
    x = x + 0.5 * _L0_ffn_ref(_layernorm(x, axis=-1), L0_ffn_gate_w, L0_ffn_expert_w)
    return x

_drawn_inputs = setup_inputs


def setup_inputs(seed=0):
    import zlib

    import numpy as np

    out = dict(_drawn_inputs(seed))
    spreads = {}
    factors = {'L0_attn_Wq': 5.775,
     'L0_attn_bq': 7.62,
     'L0_attn_Wk': 8.0,
     'L0_attn_bk': 8.0,
     'L0_attn_Wv': 8.0,
     'L0_attn_bv': 7.388,
     'L0_attn_Wo': 4.629,
     'L0_attn_bo': 2.874}
    for name, (base, spread) in spreads.items():
        noise = np.random.default_rng([zlib.crc32(name.encode()), seed]).standard_normal(out[name].shape)
        drawn = base * np.exp(spread * noise) if base else spread * noise
        out[name] = jnp.asarray(drawn.astype(out[name].dtype))
    for name, factor in factors.items():
        out[name] = (out[name] * factor).astype(out[name].dtype)
    return out
```

```python
import numpy as np
import concourse.bass as bass
from concourse import mybir
from contextlib import ExitStack

F32 = mybir.dt.float32
ALU = mybir.AluOpType
ACT = mybir.ActivationFunctionType
AX = mybir.AxisListType

P = 128
B, L, D = 16, 1024, 256
H = 16
DH = D // H
NF = L // 2 + 1
KTOP = 64
E = 8
KB = D // P
NJ = 4
HL = L // 2
EPS = 1e-5
NEG = -3.0e38
TILES = B * L // P


def constants():
    p = np.arange(P)
    w = 2 * np.pi / L
    fwd = np.zeros((P, 2, NJ, 512))
    for h in range(2):
        for j in range(NJ):
            t = (512 * h + 4 * p + j)[:, None]
            if j % 2 == 0:
                fwd[:, h, j] = np.concatenate([np.cos(w * ((t * np.arange(257)) % L)),
                                               np.sin(w * ((t * np.arange(1, 256)) % L))], 1)
            else:
                fwd[:, h, j] = np.concatenate([np.cos(w * ((t * np.arange(256)) % L)),
                                               np.sin(w * ((t * np.arange(1, 257)) % L))], 1)
    t = (4 * p[None, :] + np.arange(NJ)[:, None]).reshape(-1)
    cinv = np.zeros((P, 2, 2, 512))
    sinv = np.zeros((P, 2, 2, 512))
    for par in range(2):
        for qt in range(2):
            f = (2 * (128 * qt + p) + par)[:, None]
            wt = np.where(f == 0, 1.0, 2.0) / L
            cinv[:, par, qt] = wt * np.cos(w * ((f * t) % L))
            sinv[:, par, qt] = wt * np.sin(w * ((f * t) % L))
    cnyq = (np.where(t % 2 == 0, 1.0, -1.0) / L)[None, :]
    head = (np.arange(KB)[None, :] * P + p[:, None]) // DH
    ind = (head[:, :, None] == np.arange(H)).astype(np.float64)
    indt = ind.transpose(2, 1, 0)
    rowsel = ((p[:, None] % 64) // 16 == np.arange(4)).astype(np.float64)
    c = {"fwd": fwd.reshape(P, -1), "cinv": cinv.reshape(P, -1), "sinv": sinv.reshape(P, -1), "cnyq": cnyq,
         "ind": ind.reshape(P, -1), "indt": np.ascontiguousarray(indt).reshape(H, -1), "rowsel": rowsel,
         "ident": np.eye(P), "rank": np.broadcast_to(E - np.arange(E), (P, E))}
    return {k: np.ascontiguousarray(v, dtype=np.float32) for k, v in c.items()}


def start_at_one(nc, sems):
    with nc.Block() as block:
        @block.sync
        def _(sp):
            for s in sems:
                sp.sem_inc(s, 1)


class Chain:

    def __init__(self, eng, sem, before):
        self.eng, self.sem, self.before, self.k = eng, sem, before, 0

    def link(self, ins):
        self.k += 1
        ins.then_inc(self.sem, 1)
        self.eng.wait_ge(self.sem, self.before + self.k + 1)

    def link_hold(self, ins, turn):
        self.k += 1
        ins.then_inc(self.sem, 1)
        self.eng.wait_ge(self.sem, self.before + self.k + 1)
        self.eng.sem_inc(turn, 1)


def layer_norm_stats(nc, ch, turn, stats, mv, x3, n):
    for r in range(n):
        ins = nc.vector.bn_stats(stats[:, r, :], x3[:, r, :])
    ch.link_hold(ins, turn)
    for r in range(n):
        ins = nc.vector.bn_aggr(mv[:, r, :], stats[:, r, :])
    ch.link(ins)


def rsqrt_refine(nc, ch, var, root, r0, tmp):
    ch.link(nc.vector.reciprocal(r0, root))
    ch.link(nc.vector.tensor_tensor(tmp, r0, r0, ALU.mult))
    ch.link(nc.vector.tensor_tensor(tmp, tmp, var, ALU.mult))
    ch.link(nc.vector.tensor_scalar(tmp, tmp, -0.5, 1.5, ALU.mult, ALU.add))
    ch.link(nc.vector.tensor_tensor(r0, r0, tmp, ALU.mult))


LN_STEPS = 2 + 1 + 5


def setup_weights(nc, w, args, cst):
    with ExitStack() as ctx:
        raw = ctx.enter_context(nc.sbuf_tensor("raw_experts", [P, E, KB, D], F32))
        graw = ctx.enter_context(nc.sbuf_tensor("raw_gate", [E, D], F32))
        pt = [ctx.enter_context(nc.psum_tensor(f"setup_ps{i}", [P, 512], F32)) for i in range(2)]
        loaded = ctx.enter_context(nc.semaphore("setup_loaded"))
        transposed = ctx.enter_context(nc.semaphore("setup_transposed"))
        evacuated = ctx.enter_context(nc.semaphore("setup_evacuated"))
        scaled = ctx.enter_context(nc.semaphore("setup_scaled"))
        start_at_one(nc, [loaded, transposed, evacuated, scaled])
        block = ctx.enter_context(nc.Block())
        loads = [(raw[:, :, :, :], args["L0_ffn_expert_w"].rearrange("e (k p) h -> p e k h", p=P)),
                 (graw[:, :], args["L0_ffn_gate_w"])]
        for k in ("fwd", "cinv", "sinv", "cnyq", "ind", "indt", "rowsel", "ident", "rank"):
            loads.append((w[k][:, :], cst[k]))
        for k in ("Wq", "Wk", "Wv", "Wo"):
            loads.append((w[k][:, :, :], args["L0_attn_" + k].rearrange("(k p) n -> p k n", p=P)))
        for i, k in enumerate(("bq", "bk", "bv")):
            loads.append((w["bias"][:, i, :], args["L0_attn_" + k].rearrange("(k p) -> p k", p=P)))
        loads.append((w["bo"][0:1, :], args["L0_attn_bo"].rearrange("(a d) -> a d", a=1)))
        total = 16 * len(loads)
        groups = E * KB

        @block.sync
        def _(sp):
            with nc.allow_non_contiguous_dma(reason="three bias vectors, once"):
                for dst, src in loads:
                    sp.dma_start(dst, src).then_inc(loaded, 16)

        @block.tensor
        def _(pe):
            pe.wait_ge(loaded, total + 1)
            for g in range(groups):
                e, k = g // KB, g % KB
                if g >= 2:
                    pe.wait_ge(evacuated, g - 1 + 1)
                for fb in range(KB):
                    ins = nc.tensor.transpose(pt[g % 2][:, fb * P:(fb + 1) * P], raw[:, e, fb, k * P:(k + 1) * P],
                                              w["ident"][:, :])
                ins.then_inc(transposed, 1)
            pe.wait_ge(evacuated, groups - 1 + 1)
            for k in range(KB):
                ins = nc.tensor.transpose(pt[0][:, k * E:(k + 1) * E], graw[:, k * P:(k + 1) * P],
                                          w["ident"][0:E, 0:E])
            ins.then_inc(transposed, 1)

        @block.scalar
        def _(act):
            for g in range(groups):
                e, k = g // KB, g % KB
                act.wait_ge(transposed, g + 1 + 1)
                nc.scalar.copy(w["expert"][:, k, e * D:(e + 1) * D], pt[g % 2][:, 0:D]).then_inc(evacuated, 1)
            act.wait_ge(transposed, groups + 1 + 1)
            nc.scalar.copy(w["gate"][:, :], pt[0][:, 0:KB * E]).then_inc(evacuated, 1)
            act.wait_ge(evacuated, groups + 1 + 1)

        @block.vector
        def _(dve):
            dve.wait_ge(loaded, total + 1)
            nc.vector.tensor_scalar(w["bias"][:, :, :], w["bias"][:, :, :], float(L), None, ALU.mult).then_inc(scaled, 1)
            nc.vector.tensor_scalar(w["bo"][:, :], w["bo"][:, :], float(L), None, ALU.mult).then_inc(scaled, 1)
            dve.wait_ge(scaled, 2 + 1)


def expert_stage(nc, tag, w, src, dst):
    with ExitStack() as ctx:
        sb = lambda name, shape: ctx.enter_context(nc.sbuf_tensor(f"{tag}_{name}", shape, F32))
        sems = []
        sem = lambda name: sems.append(ctx.enter_context(nc.semaphore(f"{tag}_{name}"))) or sems[-1]
        x = [sb(f"x{u}", [P, D]) for u in range(2)]
        n = [sb(f"n{u}", [P, D]) for u in range(2)]
        nT = [sb(f"nT{u}", [P, D]) for u in range(2)]
        y = [sb(f"y{u}", [P, D]) for u in range(2)]
        stats = [sb(f"stats{u}", [P, 1, 6]) for u in range(2)]
        mv = [sb(f"mv{u}", [P, 1, 2]) for u in range(2)]
        small = [sb(f"small{u}", [P, 4]) for u in range(2)]
        pick = [sb(f"pick{u}", [P, 2, E]) for u in range(2)]
        psE = [ctx.enter_context(nc.psum_tensor(f"{tag}_psE{g}", [P, 512], F32)) for g in range(4)]
        psT = [ctx.enter_context(nc.psum_tensor(f"{tag}_psT{u}", [P, 512], F32)) for u in range(2)]
        psS = [ctx.enter_context(nc.psum_tensor(f"{tag}_psS{u}", [P, 512], F32)) for u in range(2)]
        x_in = [sem(f"x_in{u}") for u in range(2)]
        y_out = [sem(f"y_out{u}") for u in range(2)]
        var_ready, root_ready, n_ready = sem("var_ready"), sem("root_ready"), sem("n_ready")
        nT_in_psum, nT_ready = sem("nT_in_psum"), sem("nT_ready")
        scores_ready, experts_ready, bank_used = sem("scores_ready"), sem("experts_ready"), sem("bank_used")
        y_ready, ln_step, pick_step = sem("y_ready"), sem("ln_step"), sem("pick_step")
        turn = sem("turn")
        start_at_one(nc, sems)
        block = ctx.enter_context(nc.Block())
        PAIRS = TILES // 2
        PICK_STEPS = 1 + 4 + E
        rows = lambda ap, t: ap[bass.ds(t * P, P), :]

        @block.sync
        def _(sp):
            def load(i, u):
                sp.dma_start(x[u][:, :], rows(src, 2 * i + u)).then_inc(x_in[u], 16)

            def store(i, u):
                sp.wait_ge(y_ready, 2 * i + u + 1 + 1)
                sp.sem_inc(turn, 1)
                sp.dma_start(rows(dst, 2 * i + u), y[u][:, :]).then_inc(y_out[u], 16)

            for u in range(2):
                load(0, u)
            with sp.Fori(0, PAIRS - 1) as i:
                for u in range(2):
                    store(i, u)
                    load(i + 1, u)
            for u in range(2):
                store(PAIRS - 1, u)
            for u in range(2):
                sp.wait_ge(y_out[u], 16 * PAIRS + 1)
                sp.sem_inc(turn, 1)

        @block.scalar
        def _(act):
            def root(t, u):
                act.wait_ge(var_ready, t + 1 + 1)
                nc.scalar.activation(small[u][:, 1:2], small[u][:, 0:1], ACT.Sqrt).then_inc(root_ready, 1)

            def evacuate(t, u):
                act.wait_ge(nT_in_psum, t + 1 + 1)
                nc.scalar.copy(nT[u][:, :], psT[u][:, 0:D]).then_inc(nT_ready, 1)

            root(0, 0)
            evacuate(0, 0)
            with act.Fori(0, PAIRS - 1) as i:
                for u in range(2):
                    root(2 * i + u + 1, 1 - u)
                    evacuate(2 * i + u + 1, 1 - u)
            root(TILES - 1, 1)
            evacuate(TILES - 1, 1)

        @block.vector
        def _(dve):
            def normalise(i, t, u):
                dve.wait_ge(x_in[u], 16 * (i + 1) + 1)
                ch = Chain(dve, ln_step, t * LN_STEPS)
                layer_norm_stats(nc, ch, turn, stats[u], mv[u], x[u][:, :].rearrange("p (a d) -> p a d", a=1), 1)
                ch.link(nc.vector.tensor_scalar(small[u][:, 0:1], mv[u][:, 0, 1:2], EPS, None, ALU.add))
                dve.sem_inc(var_ready, 1)
                dve.wait_ge(root_ready, t + 1 + 1)
                rsqrt_refine(nc, ch, small[u][:, 0:1], small[u][:, 1:2], small[u][:, 2:3], small[u][:, 3:4])
                nc.vector.tensor_scalar(n[u][:, :], x[u][:, :], mv[u][:, 0, 0:1], small[u][:, 2:3],
                                        ALU.subtract, ALU.mult).then_inc(n_ready, 1)

            def choose(i, t, u):
                ch = Chain(dve, pick_step, t * PICK_STEPS)
                dve.wait_ge(n_ready, t + 1 + 1)
                dve.wait_ge(y_out[u], 16 * i + 1)
                ch.link(nc.vector.scalar_tensor_tensor(out=y[u][:, :], in0=n[u][:, :], scalar=0.5, in1=x[u][:, :],
                                                       op0=ALU.mult, op1=ALU.add))
                dve.wait_ge(scores_ready, t + 1 + 1)
                m, one = pick[u][:, 0, :], pick[u][:, 1, :]
                ch.link(nc.vector.reduce_max(small[u][:, 0:1], psS[u][:, 0:E], AX.X))
                ch.link(nc.vector.scalar_tensor_tensor(out=m, in0=psS[u][:, 0:E], scalar=small[u][:, 0:1],
                                                       in1=w["rank"][:, :], op0=ALU.is_equal, op1=ALU.mult))
                ch.link(nc.vector.reduce_max(small[u][:, 1:2], m, AX.X))
                ch.link(nc.vector.tensor_scalar(one, w["rank"][:, :], small[u][:, 1:2], 0.5,
                                                ALU.is_equal, ALU.mult))
                for e in range(E):
                    g = e // 2
                    if e % 2 == 0:
                        dve.wait_ge(experts_ready, 4 * t + g + 1 + 1)
                    ins = nc.vector.scalar_tensor_tensor(out=y[u][:, :], in0=psE[g][:, (e % 2) * D:(e % 2 + 1) * D],
                                                         scalar=one[:, e:e + 1], in1=y[u][:, :],
                                                         op0=ALU.mult, op1=ALU.add)
                    ch.link(ins)
                    if e % 2 == 1:
                        dve.sem_inc(bank_used, 1)
                dve.sem_inc(y_ready, 1)

            normalise(0, 0, 0)
            with dve.Fori(0, PAIRS - 1) as i:
                normalise(i, 2 * i + 1, 1)
                choose(i, 2 * i, 0)
                normalise(i + 1, 2 * i + 2, 0)
                choose(i, 2 * i + 1, 1)
            normalise(PAIRS - 1, TILES - 1, 1)
            choose(PAIRS - 1, TILES - 2, 0)
            choose(PAIRS - 1, TILES - 1, 1)

        @block.tensor
        def _(pe):
            def transpose(t, u):
                pe.wait_ge(n_ready, t + 1 + 1)
                for k in range(KB):
                    ins = nc.tensor.transpose(psT[u][:, k * P:(k + 1) * P], n[u][:, k * P:(k + 1) * P],
                                              w["ident"][:, :])
                ins.then_inc(nT_in_psum, 1)

            def products(t, u):
                pe.wait_ge(nT_ready, t + 1 + 1)
                for k in range(KB):
                    ins = nc.tensor.matmul(psS[u][:, 0:E], nT[u][:, k * P:(k + 1) * P],
                                           w["gate"][:, k * E:(k + 1) * E], start=(k == 0), stop=(k == KB - 1))
                ins.then_inc(scores_ready, 1)
                for g in range(4):
                    pe.wait_ge(bank_used, 4 * t + g + 1 + 1)
                    for k in range(KB):
                        ins = nc.tensor.matmul(psE[g][:, :], nT[u][:, k * P:(k + 1) * P],
                                               w["expert"][:, k, g * 512:(g + 1) * 512],
                                               start=(k == 0), stop=(k == KB - 1))
                    ins.then_inc(experts_ready, 1)

            pe.sem_inc(bank_used, 4)
            transpose(0, 0)
            with pe.Fori(0, PAIRS - 1) as i:
                for u in range(2):
                    transpose(2 * i + u + 1, 1 - u)
                    products(2 * i + u, u)
            transpose(TILES - 1, 1)
            products(TILES - 2, 0)
            products(TILES - 1, 1)


def spectra_stage(nc, w, src, es, means, vspec):
    with ExitStack() as ctx:
        sb = lambda name, shape: ctx.enter_context(nc.sbuf_tensor(f"sp_{name}", shape, F32))
        sems = []
        sem = lambda name: sems.append(ctx.enter_context(nc.semaphore(f"sp_{name}"))) or sems[-1]
        x = [sb(f"x{u}", [P, 2 * NJ, D]) for u in range(2)]
        n = [sb(f"n{u}", [P, 2 * NJ, D]) for u in range(2)]
        stats = sb("stats", [P, 2 * NJ, 6])
        mv = sb("mv", [P, 2 * NJ, 2])
        var, root, rstd, tmp = (sb(k, [P, 2 * NJ]) for k in ("var", "root", "rstd", "tmp"))
        even = sb("even", [P, KB, 512])
        X = sb("X", [P, KB, 2 * L // 2])
        q = sb("q", [P, KB, L])
        sq = sb("sq", [P, KB, L])
        mag = sb("mag", [P, KB, NF])
        qk = sb("qk", [P, KB, NF])
        acc = sb("acc", [P, 2, KB])
        esb = [sb(f"es{u}", [H, 2 * NF]) for u in range(2)]
        ps = [ctx.enter_context(nc.psum_tensor(f"sp_ps{i}", [P, 512], F32)) for i in range(8)]
        x_in = [sem(f"x_in{u}") for u in range(2)]
        es_out = [sem(f"es_out{u}") for u in range(2)]
        names = ("var_ready root_ready n_ready dft_ready even_ready X_ready proj_ready q_ready v_ready k_used "
                 "nyq_ready nyq_used sq_ready mag_in mag_ready qk_ready sums_ready es_ready ln_step dve_step pool_step").split()
        S = {k: sem(k) for k in names}
        turn = sem("turn")
        start_at_one(nc, sems)
        block = ctx.enter_context(nc.Block())
        PAIRS = B // 2
        seq = src.rearrange("(b h p j) c -> b p h (j c)", b=B, h=2, j=NJ)
        c0 = 4 * KB

        @block.sync
        def _(sp):
            def load(i, u):
                sp.dma_start(x[u][:, :, :].rearrange("p (h j) c -> p h (j c)", h=2),
                             seq[bass.ds(2 * i + u, 1), :, :, :].rearrange("a p h c -> (a p) h c")).then_inc(x_in[u], 16)

            def store(i, u):
                b = 2 * i + u
                sp.wait_ge(S["es_ready"], 4 * (b + 1) + 1)
                sp.sem_inc(turn, 1)
                sp.dma_start(es[bass.ds(b * H, H), :], esb[u][:, :]).then_inc(es_out[u], 16)

            for u in range(2):
                load(0, u)
            with sp.Fori(0, PAIRS - 1) as i:
                for u in range(2):
                    sp.wait_ge(S["n_ready"], 2 * i + u + 1 + 1)
                    sp.sem_inc(turn, 1)
                    load(i + 1, u)
                    store(i, u)
            for u in range(2):
                store(PAIRS - 1, u)
            for u in range(2):
                sp.wait_ge(es_out[u], 16 * PAIRS + 1)
                sp.sem_inc(turn, 1)

        @block.vector
        def _(dve):
            def normalise(i, b, u):
                dve.wait_ge(x_in[u], 16 * (i + 1) + 1)
                ch = Chain(dve, S["ln_step"], b * LN_STEPS)
                layer_norm_stats(nc, ch, turn, stats, mv, x[u], 2 * NJ)
                ch.link(nc.vector.tensor_scalar(var[:, :], mv[:, :, 1], EPS, None, ALU.add))
                dve.sem_inc(S["var_ready"], 1)
                dve.wait_ge(S["root_ready"], b + 1 + 1)
                rsqrt_refine(nc, ch, var[:, :], root[:, :], rstd[:, :], tmp[:, :])
                for r in range(2 * NJ):
                    ins = nc.vector.tensor_scalar(n[u][:, r, :], x[u][:, r, :], mv[:, r, 0:1], rstd[:, r:r + 1],
                                                  ALU.subtract, ALU.mult)
                ins.then_inc(S["n_ready"], 1)

            def combine(b):
                for k in range(KB):
                    dve.wait_ge(S["even_ready"], KB * b + k + 1 + 1)
                    dve.wait_ge(S["dft_ready"], 4 * b + 2 * k + 2 + 1)
                    ev, od, xk = even[:, k, :], ps[2 * k + 1], X[:, k, :]
                    nc.vector.tensor_tensor(xk[:, 0:256], ev[:, 0:256], od[:, 0:256], ALU.add)
                    nc.vector.tensor_tensor(xk[:, 512:256:-1], ev[:, 0:256], od[:, 0:256], ALU.subtract)
                    nc.vector.tensor_copy(xk[:, 256:257], ev[:, 256:257])
                    nc.vector.tensor_tensor(xk[:, 513:768], ev[:, 257:512], od[:, 256:511], ALU.add)
                    nc.vector.tensor_copy(xk[:, 768:769], od[:, 511:512])
                    nc.vector.scalar_tensor_tensor(out=xk[:, 1023:768:-1], in0=ev[:, 257:512], scalar=-1.0,
                                                   in1=od[:, 256:511], op0=ALU.mult,
                                                   op1=ALU.add).then_inc(S["X_ready"], 1)

            def scores(b):
                for m in range(KB):
                    dve.wait_ge(S["proj_ready"], 8 * b + 4 * m + 3 + 1)
                    dve.wait_ge(S["q_ready"], KB * b + m + 1 + 1)
                    nc.vector.scalar_tensor_tensor(out=qk[:, m, 0:1], in0=ps[6][:, 0:1], scalar=w["bias"][:, 1, m:m + 1],
                                                   in1=q[:, m, 0:1], op0=ALU.add, op1=ALU.mult)
                    nc.vector.tensor_tensor(qk[:, m, 1:512], ps[6][:, 1:512], q[:, m, 1:512],
                                            ALU.mult).then_inc(S["k_used"], 1)
                    ch = Chain(dve, S["dve_step"], (KB * b + m))
                    ch.link(nc.vector.tensor_tensor(acc[:, 0, m:m + 1], acc[:, 0, m:m + 1], q[:, m, 0:1], ALU.add))
                    nc.vector.tensor_tensor(means[:, 0, m, bass.ds(b, 1)], acc[:, 0, m:m + 1], q[:, m, 512:513], ALU.add)
                    nc.vector.tensor_copy(means[:, 1, m, bass.ds(b, 1)], acc[:, 1, m:m + 1])
                dve.wait_ge(S["nyq_ready"], b + 1 + 1)
                nc.vector.tensor_tensor(qk[:, :, 512], ps[4][:, 0:2], q[:, :, 512], ALU.mult).then_inc(S["qk_ready"], 1)

            normalise(0, 0, 0)
            with dve.Fori(0, PAIRS - 1) as i:
                combine(2 * i)
                normalise(i, 2 * i + 1, 1)
                scores(2 * i)
                combine(2 * i + 1)
                normalise(i + 1, 2 * i + 2, 0)
                scores(2 * i + 1)
            combine(B - 2)
            normalise(PAIRS - 1, B - 1, 1)
            scores(B - 2)
            combine(B - 1)
            scores(B - 1)

        @block.scalar
        def _(act):
            def even_out(b):
                for k in range(KB):
                    act.wait_ge(S["dft_ready"], 4 * b + 2 * k + 1 + 1)
                    nc.scalar.copy(even[:, k, :], ps[2 * k][:, :]).then_inc(S["even_ready"], 1)

            def ln_root(b):
                act.wait_ge(S["var_ready"], b + 1 + 1)
                nc.scalar.activation(root[:, :], var[:, :], ACT.Sqrt).then_inc(S["root_ready"], 1)

            def project_out(b):
                for m in range(KB):
                    if m == 0:
                        act.wait_ge(S["sums_ready"], 4 * b + 1)
                        act.wait_ge(S["qk_ready"], b + 1)
                        act.wait_ge(S["sq_ready"], KB * b + 1)
                    act.wait_ge(S["proj_ready"], 8 * b + 4 * m + 1 + 1)
                    nc.scalar.activation(q[:, m, 0:1], ps[4][:, 0:1], ACT.Identity, bias=w["bias"][:, 0, m:m + 1])
                    nc.scalar.activation(q[:, m, 1:512], ps[4][:, 1:512], ACT.Identity, accum_out=acc[:, 0, m:m + 1])
                    act.wait_ge(S["proj_ready"], 8 * b + 4 * m + 2 + 1)
                    nc.scalar.copy(q[:, m, 512:513], ps[5][:, 0:1])
                    nc.scalar.activation(q[:, m, 513:1024], ps[5][:, 1:512], ACT.Identity,
                                         accum_out=acc[:, 1, m:m + 1]).then_inc(S["q_ready"], 1)
                    act.wait_ge(S["proj_ready"], 8 * b + 4 * m + 4 + 1)
                    nc.scalar.activation(vspec[:, m, bass.ds(b * NF, 1)], ps[7][:, 0:1], ACT.Identity,
                                         bias=w["bias"][:, 2, m:m + 1])
                    nc.scalar.copy(vspec[:, m, bass.ds(b * NF + 1, 511)], ps[7][:, 1:512]).then_inc(S["v_ready"], 1)
                act.wait_ge(S["qk_ready"], b + 1 + 1)
                for m in range(KB):
                    ins = nc.scalar.copy(vspec[:, m, bass.ds(b * NF + 512, 1)], ps[4][:, 2 + m:3 + m])
                ins.then_inc(S["nyq_used"], 1)
                for m in range(KB):
                    act.wait_ge(S["mag_in"], KB * b + m + 1 + 1)
                    nc.scalar.activation(mag[:, m, :], sq[:, m, 0:NF], ACT.Sqrt).then_inc(S["mag_ready"], 1)

            def sums_out(b, i, u):
                act.wait_ge(es_out[u], 16 * i + 1)
                for r, (bank, lo, hi) in enumerate(((5, 0, 512), (6, NF, NF + 512))):
                    act.wait_ge(S["sums_ready"], 4 * b + r + 1 + 1)
                    nc.scalar.copy(esb[u][:, lo:hi], ps[bank][0:H, :]).then_inc(S["es_ready"], 1)
                for r, at in enumerate((512, 2 * NF - 1)):
                    act.wait_ge(S["sums_ready"], 4 * b + 4 + 1)
                    nc.scalar.copy(esb[u][:, at:at + 1], ps[7][0:H, r:r + 1]).then_inc(S["es_ready"], 1)

            ln_root(0)
            with act.Fori(0, PAIRS - 1) as i:
                for u in range(2):
                    even_out(2 * i + u)
                    ln_root(2 * i + u + 1)
                    project_out(2 * i + u)
                    sums_out(2 * i + u, i, u)
            even_out(B - 2)
            ln_root(B - 1)
            project_out(B - 2)
            sums_out(B - 2, PAIRS - 1, 0)
            even_out(B - 1)
            project_out(B - 1)
            sums_out(B - 1, PAIRS - 1, 1)

        @block.gpsimd
        def _(pool):
            def squares(b):
                for m in range(KB):
                    if m == 0:
                        pool.wait_ge(S["mag_ready"], KB * b + 1)
                    pool.wait_ge(S["q_ready"], KB * b + m + 1 + 1)
                    nc.gpsimd.tensor_tensor(sq[:, m, :], q[:, m, :], q[:, m, :], ALU.mult).then_inc(S["sq_ready"], 1)
                    pool.wait_ge(S["sq_ready"], KB * b + m + 1 + 1)
                    nc.gpsimd.tensor_tensor(sq[:, m, 1:512], sq[:, m, 1:512], sq[:, m, 513:1024],
                                            ALU.add).then_inc(S["mag_in"], 1)

            with pool.Fori(0, B) as b:
                squares(b)

        @block.tensor
        def _(pe):
            def dft(b, u):
                pe.wait_ge(S["n_ready"], b + 1 + 1)
                pe.wait_ge(S["X_ready"], KB * b + 1)
                for k in range(KB):
                    for odd in range(2):
                        slots = [h * NJ + j for h in range(2) for j in (odd, odd + 2)]
                        for c, s in enumerate(slots):
                            ins = nc.tensor.matmul(ps[2 * k + odd][:, :], n[u][:, s, k * P:(k + 1) * P],
                                                   w["fwd"][:, s * 512:(s + 1) * 512], start=(c == 0), stop=(c == 3))
                        ins.then_inc(S["dft_ready"], 1)

            def project(b):
                pe.wait_ge(S["es_ready"], 4 * b + 1)
                for m in range(KB):
                    for r, (wt, lo, bank) in enumerate((("Wq", 0, 4), ("Wq", 512, 5), ("Wk", 0, 6), ("Wv", 0, 7))):
                        if r < 2:
                            pe.wait_ge(S["q_ready"], KB * b + m + 1)
                        elif r == 2:
                            pe.wait_ge(S["k_used"], KB * b + m + 1)
                        else:
                            pe.wait_ge(S["v_ready"], KB * b + m + 1)
                        if r == 0 and m == 0:
                            pe.wait_ge(S["nyq_used"], b + 1)
                            pe.wait_ge(S["qk_ready"], b + 1)
                        for k in range(KB):
                            if m == 0 and r == 0:
                                pe.wait_ge(S["X_ready"], KB * b + k + 1 + 1)
                            ins = nc.tensor.matmul(ps[bank][:, :], w[wt][:, k, m * P:(m + 1) * P],
                                                   X[:, k, lo:lo + 512], start=(k == 0), stop=(k == KB - 1))
                        ins.then_inc(S["proj_ready"], 1)
                pe.wait_ge(S["q_ready"], KB * (b + 1) + 1)
                for r, wt in enumerate(("Wk", "Wv")):
                    for m in range(KB):
                        for k in range(KB):
                            ins = nc.tensor.matmul(ps[4][:, 2 * r + m:2 * r + m + 1], w[wt][:, k, m * P:(m + 1) * P],
                                                   X[:, k, 512:513], start=(k == 0), stop=(k == KB - 1))
                ins.then_inc(S["nyq_ready"], 1)

            def sums(b):
                pe.wait_ge(S["mag_ready"], KB * (b + 1) + 1)
                pe.wait_ge(S["qk_ready"], b + 1 + 1)
                pe.wait_ge(S["v_ready"], KB * (b + 1) + 1)
                for out, val, lo, n_ in ((ps[5][0:H, :], mag, 0, 512), (ps[6][0:H, :], qk, 0, 512),
                                         (ps[7][0:H, 0:1], mag, 512, 1), (ps[7][0:H, 1:2], qk, 512, 1)):
                    for m in range(KB):
                        ins = nc.tensor.matmul(out, w["ind"][:, m * H:(m + 1) * H], val[:, m, lo:lo + n_],
                                               start=(m == 0), stop=(m == KB - 1))
                    ins.then_inc(S["sums_ready"], 1)

            dft(0, 0)
            with pe.Fori(0, PAIRS - 1) as i:
                for u in range(2):
                    project(2 * i + u)
                    dft(2 * i + u + 1, 1 - u)
                    sums(2 * i + u)
            project(B - 2)
            dft(B - 1, 1)
            sums(B - 2)
            project(B - 1)
            sums(B - 1)


def selection_stage(nc, es, attn, outside):
    with ExitStack() as ctx:
        sb = lambda name, shape: ctx.enter_context(nc.sbuf_tensor(f"sel_{name}", shape, F32))
        sems = []
        sem = lambda name: sems.append(ctx.enter_context(nc.semaphore(f"sel_{name}"))) or sems[-1]
        G = B * H // P
        row = [sb(f"row{g}", [P, 2 * NF]) for g in range(G)]
        top = [sb(f"top{g}", [P, 8]) for g in range(G)]
        outs = [sb(f"outside{g}", [P, NF]) for g in range(G)]
        prob = [sb(f"prob{g}", [P, NF]) for g in range(G)]
        col = [sb(f"col{g}", [P, 4]) for g in range(G)]
        row_in = [sem(f"row_in{g}") for g in range(G)]
        step, max_ready, exp_ready, out_ready, stored = (sem(k) for k in ("step", "max_ready", "exp_ready", "out_ready", "stored"))
        turn = sem("turn")
        start_at_one(nc, sems)
        block = ctx.enter_context(nc.Block())

        @block.sync
        def _(sp):
            for g in range(G):
                sp.dma_start(row[g][:, :], es[g * P:(g + 1) * P, :]).then_inc(row_in[g], 16)
            for g in range(G):
                sp.wait_ge(out_ready, g + 1 + 1)
                sp.sem_inc(turn, 1)
                sp.dma_start(attn[g * P:(g + 1) * P, :], prob[g][:, :]).then_inc(stored, 16)
                sp.dma_start(outside[g * P:(g + 1) * P, :], outs[g][:, :]).then_inc(stored, 16)
            sp.wait_ge(stored, 32 * G + 1)
            sp.sem_inc(turn, 1)

        @block.vector
        def _(dve):
            ch = Chain(dve, step, 0)
            for g in range(G):
                dve.wait_ge(row_in[g], 16 + 1)
                energy, score = row[g][:, 0:NF], row[g][:, NF:2 * NF]
                for _ in range(KTOP // 8):
                    ch.link(nc.vector.max(out=top[g][:, :], in_=energy))
                    ch.link(nc.vector.match_replace(out=energy, in_to_replace=top[g][:, :], in_values=energy,
                                                    imm_value=-1.0))
                ch.link(nc.vector.tensor_scalar(outs[g][:, :], energy, 0.0, None, ALU.is_ge))
                ch.link(nc.vector.scalar_tensor_tensor(out=score, in0=outs[g][:, :], scalar=NEG, in1=score,
                                                       op0=ALU.mult, op1=ALU.add))
                ch.link(nc.vector.reduce_max(col[g][:, 0:1], score, AX.X))
                nc.vector.tensor_scalar(col[g][:, 1:2], col[g][:, 0:1], -1.0 / DH ** 0.5, None,
                                        ALU.mult).then_inc(max_ready, 1)
            for g in range(G):
                dve.wait_ge(exp_ready, g + 1 + 1)
                ch.link(nc.vector.reciprocal(col[g][:, 3:4], col[g][:, 2:3]))
                nc.vector.tensor_scalar(prob[g][:, :], prob[g][:, :], col[g][:, 3:4], None,
                                        ALU.mult).then_inc(out_ready, 1)

        @block.scalar
        def _(act):
            for g in range(G):
                act.wait_ge(max_ready, g + 1 + 1)
                nc.scalar.activation(prob[g][:, :], row[g][:, NF:2 * NF], ACT.Exp, bias=col[g][:, 1:2],
                                     scale=1.0 / DH ** 0.5, accum_out=col[g][:, 2:3]).then_inc(exp_ready, 1)


def synthesis_stage(nc, w, src, attn, outside, means, vspec, dst):
    with ExitStack() as ctx:
        sb = lambda name, shape: ctx.enter_context(nc.sbuf_tensor(f"sy_{name}", shape, F32))
        sems = []
        sem = lambda name: sems.append(ctx.enter_context(nc.semaphore(f"sy_{name}"))) or sems[-1]
        GS = 4
        R = GS * H
        G = B // GS
        x = [sb(f"x{u}", [P, 2, NJ * D]) for u in range(2)]
        at = [sb(f"at{u}", [H, NF]) for u in range(2)]
        out_rows = sb("out_rows", [R, NF])
        outT = sb("outT", [P, 4, R])
        outT_nyq = sb("outT_nyq", [1, R])
        kc = sb("kc", [P, 2, 512])
        cind = sb("cind", [P, 2, KB, R])
        z = sb("z", [P, D])
        zb = sb("zb", [P, GS, D])
        av = sb("av", [P, KB, NF])
        meansc = sb("meansc", [P, 2, KB, B])
        y = sb("y", [P, 5, D])
        y0 = sb("y0", [1, D])
        pa = [ctx.enter_context(nc.psum_tensor(f"sy_pa{i}", [P, 512], F32)) for i in range(2)]
        py = [ctx.enter_context(nc.psum_tensor(f"sy_py{i}", [P, 512], F32)) for i in range(2)]
        po = [ctx.enter_context(nc.psum_tensor(f"sy_po{i}", [P, 512], F32)) for i in range(4)]
        x_in = [sem(f"x_in{u}") for u in range(2)]
        at_in = [sem(f"at_in{u}") for u in range(2)]
        x_out = [sem(f"x_out{u}") for u in range(2)]
        names = ("rows_in mean_ready cind_ready outT_in_psum outT_ready kc_in_psum kc_ready z_in_psum z_ready zb_ready "
                 "spread_ready av_ready y_in_psum y_copied y_ready p_ready p_used inv_done o_ready row_step acc_step").split()
        S = {k: sem(k) for k in names}
        turn = sem("turn")
        start_at_one(nc, sems)
        block = ctx.enter_context(nc.Block())
        seq = src.rearrange("(b h p j) c -> b p h (j c)", b=B, h=2, j=NJ)
        oseq = dst.rearrange("(b h p j) c -> b p h (j c)", b=B, h=2, j=NJ)
        one = lambda ap, b: ap[bass.ds(b, 1), :, :, :].rearrange("a p h c -> (a p) h c")

        @block.sync
        def _(sp):
            with sp.Fori(0, G) as g:
                sp.wait_ge(S["outT_ready"], 5 * g + 1)
                sp.sem_inc(turn, 1)
                sp.dma_start(out_rows[:, :], outside[bass.ds(g * R, R), :]).then_inc(S["rows_in"], 16)
                for s in range(GS):
                    b, u = GS * g + s, s % 2
                    if s >= 2:
                        sp.wait_ge(x_out[u], 16 * (2 * g + s // 2) + 1)
                        sp.sem_inc(turn, 1)
                        sp.wait_ge(S["av_ready"], (KB + 1) * (b - 1) + 1)
                        sp.sem_inc(turn, 1)
                    else:
                        sp.wait_ge(x_out[u], 16 * 2 * g + 1)
                        sp.sem_inc(turn, 1)
                        sp.wait_ge(S["av_ready"], (KB + 1) * GS * g + 1)
                        sp.sem_inc(turn, 1)
                    sp.dma_start(x[u][:, :, :], one(seq, b)).then_inc(x_in[u], 16)
                    sp.dma_start(at[u][:, :], attn[bass.ds(b * H, H), :]).then_inc(at_in[u], 16)
            for u in range(2):
                sp.wait_ge(x_out[u], 16 * (B // 2) + 1)
                sp.sem_inc(turn, 1)

        @block.vector
        def _(dve):
            def group(g):
                if g is None:
                    return
                dve.wait_ge(S["z_in_psum"], g + 1)
                for c in range(2):
                    for m in range(KB):
                        ins = nc.vector.tensor_tensor(
                            cind[:, c, m, :].rearrange("p (s h) -> p s h", s=GS),
                            w["ind"][:, m * H:(m + 1) * H].unsqueeze(1).broadcast_to([P, GS, H]),
                            meansc[:, c, m, bass.ds(GS * g, GS)].unsqueeze(2).broadcast_to([P, GS, H]), ALU.mult)
                ins.then_inc(S["cind_ready"], 1)
                dve.wait_ge(S["z_ready"], g + 1 + 1)
                for s in range(GS):
                    ins = nc.vector.tensor_scalar(zb[:, s, :], z[:, :], w["rowsel"][:, s:s + 1], None, ALU.mult)
                ins.then_inc(S["zb_ready"], 1)

            def attend(g, b, s):
                for m in range(KB):
                    dve.wait_ge(S["spread_ready"], 3 * b + m + 1 + 1)
                    nc.vector.tensor_tensor(av[:, m, 0:512], pa[m][:, :], vspec[:, m, bass.ds(b * NF, 512)],
                                            ALU.mult).then_inc(S["av_ready"], 1)
                dve.wait_ge(S["spread_ready"], 3 * b + 3 + 1)
                for m in range(KB):
                    ins = nc.vector.tensor_tensor(av[:, m, 512:513], py[0][:, m:m + 1],
                                                  vspec[:, m, bass.ds(b * NF + 512, 1)], ALU.mult)
                ins.then_inc(S["av_ready"], 1)

            def frequency0(b):
                ch = Chain(dve, S["row_step"], 3 * b)
                dve.wait_ge(S["y_copied"], 3 * b + 3 + 1)
                ch.link(nc.vector.tensor_tensor(y0[0:1, :], y[0:1, 0, :], w["bo"][0:1, :], ALU.add))
                ch.link(nc.vector.tensor_tensor(y[0:1, 0, :], y0[0:1, :], pa[0][0:1, 0:D], ALU.add))
                ch.link(nc.vector.tensor_tensor(y[0:1, 4, :], y0[0:1, :], pa[0][0:1, 0:D], ALU.subtract))
                dve.sem_inc(S["y_ready"], 1)

            def residual(g, b, s):
                u = s % 2
                dve.wait_ge(x_in[u], 16 * (2 * g + s // 2 + 1) + 1)
                ch = Chain(dve, S["acc_step"], 4 * b)
                for jj in range(2):
                    cols = slice(jj * 512, (jj + 1) * 512)
                    x0, x1 = x[u][:, 0, cols], x[u][:, 1, cols]
                    dve.wait_ge(S["p_ready"], 4 * b + 2 * jj + 1 + 1)
                    nc.vector.tensor_tensor(x0, x0, po[2 * jj][:, :], ALU.add)
                    ch.link(nc.vector.tensor_tensor(x1, x1, po[2 * jj][:, :], ALU.add))
                    dve.sem_inc(S["p_used"], 1)
                    dve.wait_ge(S["p_ready"], 4 * b + 2 * jj + 2 + 1)
                    nc.vector.tensor_tensor(x0, x0, po[2 * jj + 1][:, :], ALU.add)
                    ch.link(nc.vector.tensor_tensor(x1, x1, po[2 * jj + 1][:, :], ALU.subtract))
                    dve.sem_inc(S["p_used"], 1)
                dve.sem_inc(S["o_ready"], 1)

            nc.vector.tensor_scalar(meansc[:, :, :, :], means[:, :, :, :], 1.0 / NF, None, ALU.mult).then_inc(S["mean_ready"], 1)
            dve.wait_ge(S["mean_ready"], 1 + 1)
            with dve.Fori(0, G) as g:
                group(g)
                attend(g, GS * g, 0)
                frequency0(GS * g)
                for s in range(GS):
                    b = GS * g + s
                    if s + 1 < GS:
                        attend(g, b + 1, s + 1)
                    residual(g, b, s)
                    if s + 1 < GS:
                        frequency0(b + 1)

        @block.scalar
        def _(act):
            def group(g):
                act.wait_ge(S["outT_in_psum"], 5 * g + 5 + 1)
                for i in range(4):
                    nc.scalar.copy(outT[:, i, :], pa[0][:, i * R:(i + 1) * R]).then_inc(S["outT_ready"], 1)
                nc.scalar.copy(outT_nyq[:, :], pa[0][0:1, 4 * R:5 * R]).then_inc(S["outT_ready"], 1)
                act.wait_ge(S["z_in_psum"], g + 1 + 1)
                nc.scalar.copy(z[:, :], pa[1][:, 0:D]).then_inc(S["z_ready"], 1)
                for par in range(2):
                    act.wait_ge(S["kc_in_psum"], 2 * g + par + 1 + 1)
                    nc.scalar.copy(kc[:, par, :], py[par][:, :]).then_inc(S["kc_ready"], 1)

            def spectrum_out(b):
                act.wait_ge(S["y_in_psum"], 3 * b + 1 + 1)
                nc.scalar.copy(y[:, 0:2, :].rearrange("p a d -> p (a d)"), py[0][:, :]).then_inc(S["y_copied"], 1)
                nc.scalar.copy(y[:, 4, :], py[0][:, 0:D]).then_inc(S["y_copied"], 1)
                act.wait_ge(S["y_in_psum"], 3 * b + 3 + 1)
                nc.scalar.copy(y[:, 2:4, :].rearrange("p a d -> p (a d)"), py[1][:, :]).then_inc(S["y_copied"], 1)

            with act.Fori(0, G) as g:
                group(g)
                spectrum_out(GS * g)
                for s in range(GS):
                    b = GS * g + s
                    if s + 1 < GS:
                        spectrum_out(b + 1)
                    act.wait_ge(S["o_ready"], b + 1 + 1)
                    act.sem_inc(turn, 1)
                    act.dma_start(one(oseq, b), x[s % 2][:, :, :]).then_inc(x_out[s % 2], 16)

        @block.tensor
        def _(pe):
            def group(g):
                pe.wait_ge(S["rows_in"], 16 * (g + 1) + 1)
                pe.sem_inc(turn, 1)
                for par in range(2):
                    for qt in range(2):
                        i = 2 * par + qt
                        lo = 256 * qt + par
                        nc.tensor.transpose(pa[0][:, i * R:(i + 1) * R], out_rows[:, lo:lo + 255:2],
                                            w["ident"][0:R, 0:R]).then_inc(S["outT_in_psum"], 1)
                nc.tensor.transpose(pa[0][0:1, 4 * R:5 * R], out_rows[:, 512:513],
                                    w["ident"][0:R, 0:R]).then_inc(S["outT_in_psum"], 1)
                pe.wait_ge(S["cind_ready"], g + 1 + 1)
                for c in range(2):
                    for m in range(KB):
                        ins = nc.tensor.matmul(pa[1][c * R:(c + 1) * R, 0:D], cind[:, c, m, :], w["Wo"][:, m, :],
                                               start=(m == 0), stop=(m == KB - 1))
                ins.then_inc(S["z_in_psum"], 1)
                pe.wait_ge(S["outT_ready"], 5 * (g + 1) + 1)
                for par in range(2):
                    for c, tab in ((0, "cinv"), (1, "sinv")):
                        nyq = par == 0 and c == 0
                        for qt in range(2):
                            i = 2 * par + qt
                            ins = nc.tensor.matmul(py[par][c * R:(c + 1) * R, :], outT[:, i, :],
                                                   w[tab][:, i * 512:(i + 1) * 512], start=(qt == 0),
                                                   stop=(qt == 1 and not nyq))
                        if nyq:
                            ins = nc.tensor.matmul(py[par][0:R, :], outT_nyq[:, :], w["cnyq"][:, :],
                                                   start=False, stop=True)
                    ins.then_inc(S["kc_in_psum"], 1)
                pe.wait_ge(S["kc_ready"], 2 * (g + 1) + 1)
                pe.wait_ge(S["z_ready"], g + 1 + 1)

            def spread(g, b, s):
                u = s % 2
                pe.wait_ge(at_in[u], 16 * (2 * g + s // 2 + 1) + 1)
                if s > 0:
                    pe.wait_ge(S["y_ready"], b + 1)
                for m in range(KB):
                    nc.tensor.matmul(pa[m][:, :], w["indt"][:, m * P:(m + 1) * P], at[u][:, 0:512],
                                     start=True, stop=True).then_inc(S["spread_ready"], 1)
                for m in range(KB):
                    ins = nc.tensor.matmul(py[0][:, m:m + 1], w["indt"][:, m * P:(m + 1) * P], at[u][:, 512:513],
                                           start=True, stop=True)
                ins.then_inc(S["spread_ready"], 1)

            def project(b):
                pe.wait_ge(S["av_ready"], (KB + 1) * (b + 1) + 1)
                for par in range(2):
                    for qt in range(2):
                        lo = 256 * qt + par
                        for m in range(KB):
                            ins = nc.tensor.matmul(py[par][:, qt * D:(qt + 1) * D], av[:, m, lo:lo + 255:2],
                                                   w["Wo"][:, m, :], start=(m == 0), stop=(m == KB - 1))
                    if par == 0:
                        ins.then_inc(S["y_in_psum"], 1)
                        for m in range(KB):
                            ins = nc.tensor.matmul(pa[0][0:1, 0:D], av[:, m, 512:513], w["Wo"][:, m, :],
                                                   start=(m == 0), stop=(m == KB - 1))
                        ins.then_inc(S["y_in_psum"], 1)
                    else:
                        ins.then_inc(S["y_in_psum"], 1)

            def inverse(g, b, s):
                pe.wait_ge(S["y_ready"], b + 1 + 1)
                pe.wait_ge(S["zb_ready"], g + 1 + 1)
                for jj in range(2):
                    for par in range(2):
                        pe.wait_ge(S["p_used"], 4 * b + 1)
                        for j in (2 * jj, 2 * jj + 1):
                            out = po[2 * jj + par][:, (j % 2) * D:(j % 2 + 1) * D]
                            for qt in range(2):
                                i = 2 * par + qt
                                yt = 4 if (par == 0 and qt == 0 and j % 2 == 1) else i
                                nc.tensor.matmul(out, w["cinv"][:, i * 512 + j * P:i * 512 + (j + 1) * P],
                                                 y[:, yt, :], start=(qt == 0), stop=False)
                            ins = nc.tensor.matmul(out, kc[:, par, j * P:(j + 1) * P], zb[:, s, :],
                                                   start=False, stop=True)
                        ins.then_inc(S["p_ready"], 1)

            with pe.Fori(0, G) as g:
                group(g)
                spread(g, GS * g, 0)
                project(GS * g)
                for s in range(GS):
                    b = GS * g + s
                    if s + 1 < GS:
                        spread(g, b + 1, s + 1)
                    inverse(g, b, s)
                    if s + 1 < GS:
                        project(b + 1)


def build(nc, args, cst, out):
    x1 = nc.dram_tensor("x1", (B * L, D), F32, kind="Internal").ap()
    x2 = nc.dram_tensor("x2", (B * L, D), F32, kind="Internal").ap()
    es = nc.dram_tensor("energy_score", (B * H, 2 * NF), F32, kind="Internal").ap()
    attn = nc.dram_tensor("attn", (B * H, NF), F32, kind="Internal").ap()
    outside = nc.dram_tensor("outside", (B * H, NF), F32, kind="Internal").ap()
    query = args["L0_attn_query"].rearrange("b l d -> (b l) d")
    out = out.rearrange("b l d -> (b l) d")
    with ExitStack() as ctx:
        w = {}
        for k, a in cst.items():
            w[k] = ctx.enter_context(nc.sbuf_tensor(f"w_{k}", list(a.shape), F32))
        for k in ("Wq", "Wk", "Wv", "Wo"):
            w[k] = ctx.enter_context(nc.sbuf_tensor(f"w_{k}", [P, KB, D], F32))
        w["bias"] = ctx.enter_context(nc.sbuf_tensor("w_bias", [P, 3, KB], F32))
        w["bo"] = ctx.enter_context(nc.sbuf_tensor("w_bo", [1, D], F32))
        w["gate"] = ctx.enter_context(nc.sbuf_tensor("w_gate", [P, KB * E], F32))
        w["expert"] = ctx.enter_context(nc.sbuf_tensor("w_expert", [P, KB, E * D], F32))
        setup_weights(nc, w, args, cst)
        expert_stage(nc, "ffn1", w, query, x1)
        with ExitStack() as mid:
            means = mid.enter_context(nc.sbuf_tensor("means", [P, 2, KB, B], F32))
            vspec = mid.enter_context(nc.sbuf_tensor("vspec", [P, KB, B * NF], F32))
            spectra_stage(nc, w, x1, es, means, vspec)
            selection_stage(nc, es, attn, outside)
            synthesis_stage(nc, w, x1, attn, outside, means, vspec, x2)
        expert_stage(nc, "ffn2", w, x2, out)


_INS = ["L0_attn_query", "L0_attn_Wq", "L0_attn_bq", "L0_attn_Wk", "L0_attn_bk", "L0_attn_Wv", "L0_attn_bv",
        "L0_attn_Wo", "L0_attn_bo", "L0_ffn_gate_w", "L0_ffn_expert_w"]


def kernel(**inputs):
    import concourse.bacc as bacc
    from concourse.bass_utils import run_bass_kernel_spmd

    nc = bacc.Bacc("TRN2", target_bir_lowering=False, num_devices=1)
    arrays, args, cst = {}, {}, {}
    for name in _INS:
        a = np.ascontiguousarray(inputs[name])
        arrays[name + "_dram"] = a
        args[name] = nc.dram_tensor(name + "_dram", a.shape, mybir.dt.from_np(a.dtype), kind="ExternalInput").ap()
    for name, a in constants().items():
        arrays["c_" + name] = a
        cst[name] = nc.dram_tensor("c_" + name, a.shape, F32, kind="ExternalInput").ap()
    out = nc.dram_tensor("out_dram", (B, L, D), F32, kind="ExternalOutput").ap()
    build(nc, args, cst, out)
    r = run_bass_kernel_spmd(nc, [arrays], core_ids=[0])
    return r.results[0]["out_dram"]
```

```python
import numpy as np
import concourse.bass as bass
from concourse import mybir
from contextlib import ExitStack

F32 = mybir.dt.float32
ALU = mybir.AluOpType
ACT = mybir.ActivationFunctionType
AX = mybir.AxisListType

P = 128
B, L, D = 16, 1024, 256
H = 16
DH = D // H
NF = L // 2 + 1
KTOP = 64
E = 8
KB = D // P
NJ = 4
HL = L // 2
EPS = 1e-5
NEG = -3.0e38
TILES = B * L // P
SLOTS = TILES + E
BIG = 2000000
F16 = mybir.dt.float16
I32 = mybir.dt.int32
U32 = mybir.dt.uint32


def constants():
    p = np.arange(P)
    w = 2 * np.pi / L
    fwd = np.zeros((P, 2, NJ, 256))
    for kind in range(2):
        for j in range(NJ):
            t = (4 * p + j)[:, None]
            f = 2 * np.arange(128)[None, :] + kind
            c, sn = np.cos(w * ((t * f) % L)), np.sin(w * ((t * f) % L))
            if kind == 0:
                sn[:, 0:1] = np.cos(w * ((256 * t) % L)) if j % 2 == 0 else np.sin(w * ((256 * t) % L))
            fwd[:, kind, j] = np.concatenate([c, sn], 1)
    t = (4 * p[None, :] + np.arange(NJ)[:, None]).reshape(-1)
    cinv = np.zeros((P, 2, 2, 512))
    sinv = np.zeros((P, 2, 2, 512))
    for par in range(2):
        for qt in range(2):
            f = (2 * (128 * qt + p) + par)[:, None]
            wt = np.where(f == 0, 1.0, 2.0) / L
            cinv[:, par, qt] = wt * np.cos(w * ((f * t) % L))
            sinv[:, par, qt] = wt * np.sin(w * ((f * t) % L))
    cnyq = (np.where(t % 2 == 0, 1.0, -1.0) / L)[None, :]
    head = (np.arange(KB)[None, :] * P + p[:, None]) // DH
    ind = (head[:, :, None] == np.arange(H)).astype(np.float64)
    indt = ind.transpose(2, 1, 0)
    rowsel = ((p[:, None] % 64) // 16 == np.arange(4)).astype(np.float64)
    c = {"fwd": fwd.reshape(P, -1), "cinv": cinv.reshape(P, -1), "sinv": sinv.reshape(P, -1), "cnyq": cnyq,
         "ind": ind.reshape(P, -1), "indt": np.ascontiguousarray(indt).reshape(H, -1), "rowsel": rowsel,
         "ident": np.eye(P), "rank": np.broadcast_to(E - np.arange(E), (P, E)),
         "low": 4 * p[:, None] + np.arange(NJ) + 1, "high": np.broadcast_to(np.arange(2 * B), (P, 2 * B))}
    half = {"before": p[:, None] < p[None, :], "ones": np.ones((P, P)),
            "iota": np.broadcast_to(np.arange(SLOTS), (P, SLOTS))}
    c = {k: np.ascontiguousarray(v, dtype=np.float32) for k, v in c.items()}
    c.update({k: np.ascontiguousarray(v, dtype=np.float16) for k, v in half.items()})
    return c


def start_at_one(nc, sems):
    with nc.Block() as block:
        @block.sync
        def _(sp):
            for s in sems:
                sp.sem_inc(s, 1)


def back_to_zero(nc, sems):
    with nc.Block() as block:
        @block.sync
        def _(sp):
            for s in sems:
                sp.sem_clear(s)


class Chain:

    def __init__(self, eng, sem, before):
        self.eng, self.sem, self.before, self.k = eng, sem, before, 0

    def link(self, ins):
        self.k += 1
        ins.then_inc(self.sem, 1)
        self.eng.wait_ge(self.sem, self.before + self.k + 1)

    def link_hold(self, ins, turn):
        self.k += 1
        ins.then_inc(self.sem, 1)
        self.eng.wait_ge(self.sem, self.before + self.k + 1)
        self.eng.sem_inc(turn, 1)


def layer_norm_stats(nc, ch, turn, stats, mv, x3, n):
    for r in range(n):
        ins = nc.vector.bn_stats(stats[:, r, :], x3[:, r, :])
    ch.link_hold(ins, turn)
    for r in range(n):
        ins = nc.vector.bn_aggr(mv[:, r, :], stats[:, r, :])
    ch.link(ins)


def rsqrt_refine(nc, ch, var, root, r0, tmp):
    ch.link(nc.vector.reciprocal(r0, root))
    ch.link(nc.vector.tensor_tensor(tmp, r0, r0, ALU.mult))
    ch.link(nc.vector.tensor_tensor(tmp, tmp, var, ALU.mult))
    ch.link(nc.vector.tensor_scalar(tmp, tmp, -0.5, 1.5, ALU.mult, ALU.add))
    ch.link(nc.vector.tensor_tensor(r0, r0, tmp, ALU.mult))


LN_STEPS = 2 + 1 + 5


def setup_weights(nc, w, args, cst):
    with ExitStack() as ctx:
        raw = ctx.enter_context(nc.sbuf_tensor("raw_experts", [P, E, KB, D], F32))
        graw = ctx.enter_context(nc.sbuf_tensor("raw_gate", [E, D], F32))
        gmean = ctx.enter_context(nc.sbuf_tensor("gate_mean", [E, 1], F32))
        rmean = ctx.enter_context(nc.sbuf_tensor("expert_mean", [P, E * KB], F32))
        pt = [ctx.enter_context(nc.psum_tensor(f"setup_ps{i}", [P, 512], F32)) for i in range(2)]
        loaded = ctx.enter_context(nc.semaphore("setup_loaded"))
        transposed = ctx.enter_context(nc.semaphore("setup_transposed"))
        evacuated = ctx.enter_context(nc.semaphore("setup_evacuated"))
        scaled = ctx.enter_context(nc.semaphore("setup_scaled"))
        start_at_one(nc, [loaded, transposed, evacuated, scaled])
        ctx.callback(back_to_zero, nc, [loaded, transposed, evacuated, scaled])
        block = ctx.enter_context(nc.Block())
        loads = [(raw[:, :, :, :], args["L0_ffn_expert_w"].rearrange("e (k p) h -> p e k h", p=P)),
                 (graw[:, :], args["L0_ffn_gate_w"])]
        for k in ("fwd", "cinv", "sinv", "cnyq", "ind", "indt", "rowsel", "ident", "rank", "low", "high", "before",
                  "ones", "iota"):
            loads.append((w[k][:, :], cst[k]))
        for k in ("Wq", "Wk", "Wv", "Wo"):
            loads.append((w[k][:, :, :], args["L0_attn_" + k].rearrange("(k p) n -> p k n", p=P)))
        for i, k in enumerate(("bq", "bk", "bv")):
            loads.append((w["bias"][:, i, :], args["L0_attn_" + k].rearrange("(k p) -> p k", p=P)))
        loads.append((w["bo"][0:1, :], args["L0_attn_bo"].rearrange("(a d) -> a d", a=1)))
        total = 16 * len(loads)
        groups = E * KB

        @block.sync
        def _(sp):
            with nc.allow_non_contiguous_dma(reason="three bias vectors, once"):
                for dst, src in loads:
                    sp.dma_start(dst, src).then_inc(loaded, 16)

        @block.tensor
        def _(pe):
            pe.wait_ge(loaded, total + 1)
            pe.wait_ge(scaled, 8 + 1)
            for g in range(groups):
                e, k = g // KB, g % KB
                if g >= 2:
                    pe.wait_ge(evacuated, g - 1 + 1)
                for fb in range(KB):
                    ins = nc.tensor.transpose(pt[g % 2][:, fb * P:(fb + 1) * P], raw[:, e, fb, k * P:(k + 1) * P],
                                              w["ident"][:, :])
                ins.then_inc(transposed, 1)
            pe.wait_ge(evacuated, groups - 1 + 1)
            for k in range(KB):
                ins = nc.tensor.transpose(pt[0][:, k * E:(k + 1) * E], graw[:, k * P:(k + 1) * P],
                                          w["ident"][0:E, 0:E])
            ins.then_inc(transposed, 1)

        @block.scalar
        def _(act):
            for g in range(groups):
                e, k = g // KB, g % KB
                act.wait_ge(transposed, g + 1 + 1)
                nc.scalar.copy(w["expert"][:, k, e * D:(e + 1) * D], pt[g % 2][:, 0:D]).then_inc(evacuated, 1)
            act.wait_ge(transposed, groups + 1 + 1)
            nc.scalar.copy(w["gate"][:, :], pt[0][:, 0:KB * E]).then_inc(evacuated, 1)
            act.wait_ge(evacuated, groups + 1 + 1)

        @block.vector
        def _(dve):
            dve.wait_ge(loaded, total + 1)
            nc.vector.tensor_scalar(w["bias"][:, :, :], w["bias"][:, :, :], float(L), None, ALU.mult).then_inc(scaled, 1)
            nc.vector.tensor_scalar(w["bo"][:, :], w["bo"][:, :], float(L), None, ALU.mult).then_inc(scaled, 1)
            nc.vector.reduce_sum(gmean[:, :], graw[:, :], AX.X).then_inc(scaled, 1)
            dve.wait_ge(scaled, 3 + 1)
            nc.vector.scalar_tensor_tensor(out=graw[:, :], in0=gmean[:, 0:1].broadcast_to([E, D]), scalar=-1.0 / D,
                                           in1=graw[:, :], op0=ALU.mult, op1=ALU.add).then_inc(scaled, 1)
            for fb in range(KB):
                part = raw[:, :, fb, fb * P:(fb + 1) * P]
                ins = nc.vector.tensor_tensor(part, part, w["ident"][:, :].unsqueeze(1).broadcast_to([P, E, P]), ALU.add)
            ins.then_inc(scaled, 1)
            dve.wait_ge(scaled, 5 + 1)
            rows = raw[:, :, :, :].rearrange("p e k h -> p (e k) h")
            nc.vector.reduce_sum(rmean[:, :], rows, AX.X).then_inc(scaled, 1)
            dve.wait_ge(scaled, 6 + 1)
            nc.vector.tensor_scalar(rmean[:, :], rmean[:, :], -0.5 / D, None, ALU.mult).then_inc(scaled, 1)
            dve.wait_ge(scaled, 7 + 1)
            nc.vector.scalar_tensor_tensor(out=rows, in0=rows, scalar=0.5,
                                           in1=rmean[:, :].unsqueeze(2).broadcast_to([P, E * KB, D]),
                                           op0=ALU.mult, op1=ALU.add).then_inc(scaled, 1)
            dve.wait_ge(scaled, 8 + 1)


def score_stage(nc, tag, w, src, chosen):
    with ExitStack() as ctx:
        sb = lambda name, shape: ctx.enter_context(nc.sbuf_tensor(f"{tag}_{name}", shape, F32))
        sems = []
        sem = lambda name: sems.append(ctx.enter_context(nc.semaphore(f"{tag}_{name}"))) or sems[-1]
        NX = 4
        R = 2 * NJ // 2
        x = [sb(f"x{u}", [P, 2 * NJ, D]) for u in range(NX)]
        xT = [sb(f"xT{r}", [P, 2, KB, P]) for r in range(R)]
        best, code = sb("best", [P, 2 * NJ]), sb("code", [P, 2 * NJ])
        hit = sb("hit", [P, 2 * NJ, E])
        psT = [ctx.enter_context(nc.psum_tensor(f"{tag}_psT{r}", [P, 512], F32)) for r in range(R)]
        psS = [ctx.enter_context(nc.psum_tensor(f"{tag}_psS{u}", [P, 512], F32)) for u in range(2)]
        x_in = [sem(f"x_in{u}") for u in range(NX)]
        xT_in_psum, xT_ready, scores_ready, chosen_ready, step, turn = (
            sem(k) for k in ("xT_in_psum", "xT_ready", "scores_ready", "chosen_ready", "step", "turn"))
        start_at_one(nc, sems)
        ctx.callback(back_to_zero, nc, sems)
        block = ctx.enter_context(nc.Block())
        seq = src.rearrange("(b h p j) c -> b p h (j c)", b=B, h=2, j=NJ)

        @block.sync
        def _(sp):
            def load(i, u):
                sp.dma_start(x[u][:, :, :].rearrange("p (h j) c -> p h (j c)", h=2),
                             seq[bass.ds(NX * i + u, 1), :, :, :].rearrange("a p h c -> (a p) h c")).then_inc(x_in[u], 16)

            for u in range(NX):
                load(0, u)
            with sp.Fori(0, B // NX - 1) as i:
                for u in range(NX):
                    sp.wait_ge(xT_in_psum, R * (NX * i + u + 1) + 1)
                    sp.sem_inc(turn, 1)
                    load(i + 1, u)

        @block.tensor
        def _(pe):
            def transpose(b, u, r):
                for c in range(2):
                    for k in range(KB):
                        ins = nc.tensor.transpose(psT[r][:, (2 * c + k) * P:(2 * c + k + 1) * P],
                                                  x[u][:, 2 * r + c, k * P:(k + 1) * P], w["ident"][:, :])
                ins.then_inc(xT_in_psum, 1)

            def scores(b, u, r):
                pe.wait_ge(xT_ready, R * b + r + 1 + 1)
                for c in range(2):
                    at = (2 * r + c) * E
                    for k in range(KB):
                        ins = nc.tensor.matmul(psS[u % 2][:, at:at + E], xT[r][:, c, k, :],
                                               w["gate"][:, k * E:(k + 1) * E], start=(k == 0), stop=(k == KB - 1))
                if r == R - 1:
                    ins.then_inc(scores_ready, 1)

            pe.sem_inc(chosen_ready, 2)
            with pe.Fori(0, B // NX) as i:
                for u in range(NX):
                    b = NX * i + u
                    pe.wait_ge(x_in[u], 16 * (i + 1) + 1)
                    transpose(b, u, 0)
                    transpose(b, u, 1)
                    pe.wait_ge(chosen_ready, b + 1 + 1)
                    scores(b, u, 0)
                    for r in range(2, R):
                        transpose(b, u, r)
                        scores(b, u, r - 1)
                    scores(b, u, R - 1)

        @block.scalar
        def _(act):
            with act.Fori(0, B) as b:
                for r in range(R):
                    act.wait_ge(xT_in_psum, R * b + r + 1 + 1)
                    nc.scalar.copy(xT[r][:, :, :, :].rearrange("p a k q -> p (a k q)"),
                                   psT[r][:, :]).then_inc(xT_ready, 1)

        @block.vector
        def _(dve):
            with dve.Fori(0, B // 2) as i:
                for u in range(2):
                    b = 2 * i + u
                    ch = Chain(dve, step, 5 * b)
                    dve.wait_ge(scores_ready, b + 1 + 1)
                    sc = psS[u][:, 0:2 * NJ * E].rearrange("p (t e) -> p t e", e=E)
                    rank = w["rank"][:, :].unsqueeze(1).broadcast_to([P, 2 * NJ, E])
                    wide = [P, 2 * NJ, E]
                    ch.link(nc.vector.reduce_max(best[:, :], sc, AX.X))
                    ch.link(nc.vector.tensor_tensor(hit[:, :, :], sc, best[:, :].unsqueeze(2).broadcast_to(wide),
                                                    ALU.is_equal))
                    ch.link(nc.vector.tensor_tensor(hit[:, :, :], hit[:, :, :], rank, ALU.mult))
                    ch.link(nc.vector.reduce_max(code[:, :], hit[:, :, :], AX.X))
                    ch.link(nc.vector.tensor_scalar(code[:, :], code[:, :], 1.0, None, ALU.max))
                    nc.vector.tensor_tensor(chosen[:, bass.ds(b * 2 * NJ * E, 2 * NJ * E)].rearrange("p (t e) -> p t e", e=E),
                                            rank, code[:, :].unsqueeze(2).broadcast_to(wide),
                                            ALU.is_equal).then_inc(chosen_ready, 1)
            dve.wait_ge(chosen_ready, B + 2 + 1)


def routing_stage(nc, tag, w, chosen, index, expert_at):
    with ExitStack() as ctx:
        sb = lambda name, shape, dt=F32: ctx.enter_context(nc.sbuf_tensor(f"{tag}_{name}", shape, dt))
        sems = []
        sem = lambda name: sems.append(ctx.enter_context(nc.semaphore(f"{tag}_{name}"))) or sems[-1]
        T = TILES
        count = [sb(f"count{i}", [P, E, T]) for i in range(2)]
        first = sb("first", [P, E, T])
        where = sb("where", [P, T, E])
        slot, tile_of, row_of = sb("slot", [P, T]), sb("tile_of", [P, T]), sb("row_of", [P, T])
        ints = sb("ints", [P, T], I32)
        ints2 = sb("ints2", [P, T], I32)
        pad_i = sb("pad_i", [P, E], I32)
        padded = sb("padded", [P, E])
        ends = [sb(f"ends{i}", [P, E]) for i in range(2)]
        base = sb("base", [P, E])
        at_row = [sb(f"at_row{j}", [P, P], F16) for j in range(NJ)]
        at_tile = [sb(f"at_tile{j}", [P, 2, SLOTS], F16) for j in range(NJ)]
        low, empty = sb("low", [P, SLOTS]), sb("empty", [P, SLOTS])
        past = sb("past", [1, SLOTS, E])
        past_sum = sb("past_sum", [1, SLOTS])
        ps_rank = ctx.enter_context(nc.psum_tensor(f"{tag}_rank", [P, T * E], F32))
        ps_tot = ctx.enter_context(nc.psum_tensor(f"{tag}_tot", [P, T * E], F32))
        ps_index = ctx.enter_context(nc.psum_tensor(f"{tag}_index", [P, 2 * SLOTS], F32))
        counted, step, placed, used, hot = (sem(k) for k in ("counted", "step", "placed", "used", "hot"))
        start_at_one(nc, sems)
        ctx.callback(back_to_zero, nc, sems)
        block = ctx.enter_context(nc.Block())
        QS = TILES // NJ

        @block.tensor
        def _(pe):
            for tab, out in (("before", ps_rank), ("ones", ps_tot)):
                for c in range(0, T * E, 512):
                    ins = nc.tensor.matmul(out[:, c:c + 512], w[tab][:, :], chosen[:, c:c + 512], start=True, stop=True)
            ins.then_inc(counted, 1)

            def place(q, first_, last_):
                for j in range(NJ):
                    pe.wait_ge(hot, NJ * q + j + 1 + 1)
                    nc.tensor.matmul(ps_index[:, :], at_row[j][:, :], at_tile[j][:, :, :].rearrange("p a s -> p (a s)"),
                                     start=(first_ and j == 0), stop=(last_ and j == NJ - 1)).then_inc(used, 1)

            place(0, True, False)
            with pe.Fori(1, QS - 1) as q:
                place(q, False, False)
            place(QS - 1, False, True)

        @block.vector
        def _(dve):
            ch = Chain(dve, step, 0)
            V = nc.vector
            dve.wait_ge(counted, 1 + 1)
            tot = ps_tot[:, :].rearrange("p (t e) -> p e t", e=E)
            ch.link(V.tensor_copy(count[0][:, :, :], tot))
            src, dst = count
            d = 1
            while d < T:
                V.tensor_copy(dst[:, :, 0:d], src[:, :, 0:d])
                ch.link(V.tensor_tensor(dst[:, :, d:T], src[:, :, d:T], src[:, :, 0:T - d], ALU.add))
                src, dst, d = dst, src, 2 * d
            ch.link(V.tensor_scalar(pad_i[:, :], src[:, :, T - 1], float(P - 1), None, ALU.add))
            ch.link(V.tensor_scalar(pad_i[:, :], pad_i[:, :], 7, 7, ALU.logical_shift_right, ALU.logical_shift_left))
            ch.link(V.tensor_copy(padded[:, :], pad_i[:, :]))
            ch.link(V.tensor_copy(ends[0][:, :], padded[:, :]))
            esrc, edst = ends
            d = 1
            while d < E:
                V.tensor_copy(edst[:, 0:d], esrc[:, 0:d])
                ch.link(V.tensor_tensor(edst[:, d:E], esrc[:, d:E], esrc[:, 0:E - d], ALU.add))
                esrc, edst, d = edst, esrc, 2 * d
            ch.link(V.tensor_tensor(base[:, :], esrc[:, :], padded[:, :], ALU.subtract))
            ch.link(V.tensor_tensor(first[:, :, :], src[:, :, :], tot, ALU.subtract))
            ch.link(V.tensor_tensor(first[:, :, :], first[:, :, :],
                                    base[:, :].unsqueeze(2).broadcast_to([P, E, T]), ALU.add))
            ch.link(V.tensor_tensor(where[:, :, :], ps_rank[:, :].rearrange("p (t e) -> p t e", e=E),
                                    first[:, :, :].rearrange("p e t -> p t e"), ALU.add))
            ch.link(V.tensor_tensor(where[:, :, :], where[:, :, :], chosen[:, :].rearrange("p (t e) -> p t e", e=E),
                                    ALU.mult))
            ch.link(V.reduce_sum(slot[:, :], where[:, :, :], AX.X))
            ch.link(V.tensor_copy(ints[:, :], slot[:, :]))
            ch.link(V.tensor_scalar(ints2[:, :], ints[:, :], 7, None, ALU.logical_shift_right))
            V.tensor_copy(tile_of[:, :], ints2[:, :])
            ch.link(V.tensor_scalar(ints[:, :], ints[:, :], P - 1, None, ALU.bitwise_and))
            ch.link(V.tensor_copy(row_of[:, :], ints[:, :]))
            ch.link(V.tensor_scalar(base[:, :], esrc[:, :], 1.0 / P, None, ALU.mult))
            ch.link(V.tensor_tensor(past[:, :, :], w["iota"][0:1, :].unsqueeze(2).broadcast_to([1, SLOTS, E]),
                                    base[0:1, :].unsqueeze(1).broadcast_to([1, SLOTS, E]), ALU.is_ge))
            ch.link(V.reduce_sum(past_sum[:, :], past[:, :, :], AX.X))
            ch.link(V.tensor_scalar(expert_at[:, :], past_sum[:, :], float(E - 1), float(D), ALU.min, ALU.mult))

            def one_hots(q):
                for j in range(NJ):
                    t = NJ * q + j
                    if not (isinstance(q, int) and q == 0):
                        dve.wait_ge(used, NJ * (q - 1) + j + 1 + 1)
                    row, tile = row_of[:, bass.ds(t, 1)], tile_of[:, bass.ds(t, 1)]
                    V.tensor_scalar(at_row[j][:, :], w["iota"][:, 0:P], row, None, ALU.is_equal)
                    V.tensor_scalar(at_tile[j][:, 0, :], w["iota"][:, :], tile, w["low"][:, j:j + 1],
                                    ALU.is_equal, ALU.mult)
                    V.tensor_scalar(at_tile[j][:, 1, :], w["iota"][:, :], tile, w["high"][:, bass.ds(q, 1)],
                                    ALU.is_equal, ALU.mult).then_inc(hot, 1)

            one_hots(0)
            with dve.Fori(1, QS) as q:
                one_hots(q)
            dve.wait_ge(used, TILES + 1)
            ch.link(V.tensor_copy(low[:, :], ps_index[:, 0:SLOTS]))
            V.tensor_scalar(empty[:, :], low[:, :], 0.0, float(BIG), ALU.is_equal, ALU.mult)
            ch.link(V.scalar_tensor_tensor(out=low[:, :], in0=ps_index[:, SLOTS:2 * SLOTS], scalar=512.0,
                                           in1=low[:, :], op0=ALU.mult, op1=ALU.add))
            ch.link(V.scalar_tensor_tensor(out=index[:, :], in0=low[:, :], scalar=-1.0, in1=empty[:, :],
                                           op0=ALU.add, op1=ALU.add))


def expert_stage(nc, tag, w, index, expert_at, src, dst):
    with ExitStack() as ctx:
        sb = lambda name, shape, dt=F32: ctx.enter_context(nc.sbuf_tensor(f"{tag}_{name}", shape, dt))
        sems = []
        sem = lambda name: sems.append(ctx.enter_context(nc.semaphore(f"{tag}_{name}"))) or sems[-1]
        NB, AHEAD, GT = 16, 12, 4
        ROUNDS = SLOTS // NB
        TAIL = SLOTS - NB * ROUNDS
        GR = NB // GT
        x = [sb(f"x{k}", [P, D]) for k in range(NB)]
        y = [sb(f"y{k}", [P, D]) for k in range(NB)]
        xT = [sb(f"xT{k}", [P, 2, KB, P]) for k in range(4)]
        gather_at = [sb(f"gather_at{k}", [P, 1], I32) for k in range(NB)]
        scatter_at = [sb(f"scatter_at{k}", [P, 1], I32) for k in range(NB)]
        stats, mv = sb("stats", [P, GT, 6]), sb("mv", [P, GT, 2])
        var, root, r0, tmp = (sb(k, [P, GT]) for k in ("var", "root", "r0", "tmp"))
        rstd = [sb(f"rstd{k}", [P, GT]) for k in range(2)]
        psT = [ctx.enter_context(nc.psum_tensor(f"{tag}_psT{k}", [P, 512], F32)) for k in range(4)]
        psY = [ctx.enter_context(nc.psum_tensor(f"{tag}_psY{k}", [P, 512], F32)) for k in range(4)]
        gathered = [ctx.enter_context(nc.semaphore(f"{tag}_gathered{k}")) for k in range(NB)]
        scattered = [ctx.enter_context(nc.semaphore(f"{tag}_scattered{k}")) for k in range(NB)]
        from_zero = gathered + scattered
        cleared, gather_at_ready, scatter_at_ready, var_ready, root_ready = (
            sem(k) for k in ("cleared", "gather_at_ready", "scatter_at_ready", "var_ready", "root_ready"))
        xT_in_psum, xT_ready, product_ready, y_ready, ln_step, turn = (
            sem(k) for k in ("xT_in_psum", "xT_ready", "product_ready", "y_ready", "ln_step", "turn"))
        start_at_one(nc, sems)
        ctx.callback(back_to_zero, nc, sems + from_zero)
        block = ctx.enter_context(nc.Block())
        is_first = lambda i: isinstance(i, int) and i == 0
        exists = lambda i, k: not isinstance(i, int) or NB * i + k < SLOTS

        @block.gpsimd
        def _(pool):
            def gather(i, k):
                pool.wait_ge(gather_at_ready, NB * i + k + 1 + 1)
                pool.sem_inc(turn, 1)
                pool.indirect_dma_start(out=x[k][:, :], out_offset=None, in_=src,
                                        in_offset=bass.IndirectOffsetOnAxis(ap=gather_at[k][:, 0:1], axis=0),
                                        bounds_check=B * L - 1, oob_is_err=False).then_inc(gathered[k], 16)

            def scatter(i, k):
                pool.wait_ge(y_ready, NB * i + k + 1 + 1)
                pool.sem_inc(turn, 1)
                pool.wait_ge(scatter_at_ready, NB * i + k + 1 + 1)
                pool.sem_inc(turn, 1)
                pool.indirect_dma_start(out=dst, out_offset=bass.IndirectOffsetOnAxis(ap=scatter_at[k][:, 0:1], axis=0),
                                        in_=y[k][:, :], in_offset=None,
                                        bounds_check=B * L - 1, oob_is_err=False).then_inc(scattered[k], 16)

            def round_(i, tiles=NB, last=False):
                for k in range(tiles):
                    a = k + AHEAD
                    if a < NB:
                        if exists(i, a):
                            gather(i, a)
                    elif not last and exists(i + 1, a - NB):
                        gather(i + 1, a - NB)
                    scatter(i, k)

            pool.wait_ge(cleared, 1 + 1)
            for k in range(AHEAD):
                gather(0, k)
            with pool.Fori(0, ROUNDS - 1) as i:
                round_(i)
            round_(ROUNDS - 1)
            round_(ROUNDS, TAIL, last=True)
            for k in range(NB):
                pool.wait_ge(scattered[k], 16 * (ROUNDS + (k < TAIL)))

        @block.scalar
        def _(act):
            def place_gather(i, k):
                if not is_first(i):
                    act.wait_ge(gathered[k], 16 * i)
                    act.sem_inc(turn, 1)
                nc.scalar.copy(gather_at[k][:, :], index[:, bass.ds(NB * i + k, 1)]).then_inc(gather_at_ready, 1)

            def place_scatter(i, k):
                if not is_first(i):
                    act.wait_ge(scattered[k], 16 * i)
                    act.sem_inc(turn, 1)
                nc.scalar.copy(scatter_at[k][:, :], index[:, bass.ds(NB * i + k, 1)]).then_inc(scatter_at_ready, 1)

            def transposed(i, h):
                act.wait_ge(xT_in_psum, NB // 2 * i + h + 1 + 1)
                nc.scalar.copy(xT[h % 4][:, :, :, :].rearrange("p a k q -> p (a k q)"),
                               psT[h % 4][:, :]).then_inc(xT_ready, 1)

            def group_root(i, g):
                act.wait_ge(var_ready, GR * i + g + 1 + 1)
                nc.scalar.activation(root[:, :], var[:, :], ACT.Sqrt).then_inc(root_ready, 1)

            def round_(i, tiles=NB, last=False):
                for g in range(tiles // GT):
                    for k in range(GT * g, GT * (g + 1)):
                        a = k + AHEAD
                        if a < NB:
                            if exists(i, a):
                                place_gather(i, a)
                        elif not last and exists(i + 1, a - NB):
                            place_gather(i + 1, a - NB)
                        place_scatter(i, k)
                        if k % 2:
                            transposed(i, k // 2)
                            if k % GT == 1:
                                if g + 1 < tiles // GT:
                                    group_root(i, g + 1)
                                elif not last:
                                    group_root(i + 1, 0)

            for k in range(AHEAD):
                place_gather(0, k)
            group_root(0, 0)
            round_(0)
            with act.Fori(1, ROUNDS - 1) as i:
                round_(i)
            round_(ROUNDS - 1)
            round_(ROUNDS, TAIL, last=True)

        @block.vector
        def _(dve):
            STEPS = 2 + 1 + 5

            def finish(i, k):
                dve.wait_ge(product_ready, NB * i + k + 1 + 1)
                if not is_first(i):
                    dve.wait_ge(scattered[k], 16 * i)
                nc.vector.scalar_tensor_tensor(out=y[k][:, :], in0=psY[k % 4][:, 0:D],
                                               scalar=rstd[k // GT % 2][:, k % GT:k % GT + 1], in1=x[k][:, :],
                                               op0=ALU.mult, op1=ALU.add).then_inc(y_ready, 1)

            def group(i, g, fi=None, fg=None):
                at = GR * i + g
                r = rstd[g % 2][:, :]
                step = STEPS * at + 1
                done = [0]

                def finish_next():
                    if fi is not None and done[0] < GT:
                        finish(fi, GT * fg + done[0])
                        done[0] += 1

                for c in range(GT):
                    dve.wait_ge(gathered[GT * g + c], 16 * (i + 1))
                    ins = nc.vector.bn_stats(stats[:, c, :], x[GT * g + c][:, :])
                ins.then_inc(ln_step, 1)
                finish_next()
                dve.wait_ge(ln_step, step + 1)
                dve.sem_inc(turn, 1)
                for c in range(GT):
                    ins = nc.vector.bn_aggr(mv[:, c, :], stats[:, c, :])
                ins.then_inc(ln_step, 1)
                finish_next()
                dve.wait_ge(ln_step, step + 2)
                nc.vector.tensor_scalar(var[:, :], mv[:, :, 1], EPS, None, ALU.add).then_inc(var_ready, 1)
                finish_next()
                dve.wait_ge(root_ready, at + 1 + 1)
                nc.vector.reciprocal(r0[:, :], root[:, :]).then_inc(ln_step, 1)
                finish_next()
                dve.wait_ge(ln_step, step + 3)
                nc.vector.tensor_tensor(tmp[:, :], r0[:, :], r0[:, :], ALU.mult).then_inc(ln_step, 1)
                dve.wait_ge(ln_step, step + 4)
                nc.vector.tensor_tensor(tmp[:, :], tmp[:, :], var[:, :], ALU.mult).then_inc(ln_step, 1)
                dve.wait_ge(ln_step, step + 5)
                nc.vector.tensor_scalar(tmp[:, :], tmp[:, :], -0.5, 1.5, ALU.mult, ALU.add).then_inc(ln_step, 1)
                dve.wait_ge(ln_step, step + 6)
                nc.vector.tensor_tensor(r, r0[:, :], tmp[:, :], ALU.mult).then_inc(ln_step, 1)
                dve.wait_ge(ln_step, step + 7)
                dve.sem_inc(ln_step, 1)

            def round_(i, tiles=NB, last=False):
                n = tiles // GT
                for g in range(n):
                    if g + 1 < n:
                        group(i, g + 1, i, g)
                    elif not last:
                        group(i + 1, 0, i, g)
                    else:
                        for c in range(GT):
                            finish(i, GT * g + c)

            for k in range(NB):
                ins = nc.vector.memset(x[k][:, :], 0.0)
            ins.then_inc(cleared, 1)
            group(0, 0)
            round_(0)
            with dve.Fori(1, ROUNDS - 1) as i:
                round_(i)
            round_(ROUNDS - 1)
            round_(ROUNDS, TAIL, last=True)

        @block.tensor
        def _(pe):
            def transpose(i, h):
                for c in range(2):
                    pe.wait_ge(gathered[2 * h + c], 16 * (i + 1))
                    for k in range(KB):
                        ins = nc.tensor.transpose(psT[h % 4][:, (2 * c + k) * P:(2 * c + k + 1) * P],
                                                  x[2 * h + c][:, k * P:(k + 1) * P], w["ident"][:, :])
                ins.then_inc(xT_in_psum, 1)

            def product(i, h):
                pe.wait_ge(xT_ready, NB // 2 * i + h + 1 + 1)
                if not (is_first(i) and h < 2):
                    pe.wait_ge(y_ready, NB * i + 2 * h - 2 + 1)
                for c in range(2):
                    s = NB * i + 2 * h + c
                    col = pe.value_load(expert_at[0:1, bass.ds(s, 1)], min_val=0, max_val=(E - 1) * D)
                    for k in range(KB):
                        ins = nc.tensor.matmul(psY[(2 * h + c) % 4][:, 0:D], xT[h % 4][:, c, k, :],
                                               w["expert"][:, k, bass.ds(col, D)], start=(k == 0), stop=(k == KB - 1))
                    ins.then_inc(product_ready, 1)

            def round_(i, tiles=NB, last=False):
                n = tiles // 2
                for h in range(n):
                    if h + 1 < n:
                        transpose(i, h + 1)
                    elif not last:
                        transpose(i + 1, 0)
                    product(i, h)

            transpose(0, 0)
            round_(0)
            with pe.Fori(1, ROUNDS - 1) as i:
                round_(i)
            round_(ROUNDS - 1)
            round_(ROUNDS, TAIL, last=True)


def routed_experts(nc, tag, w, src, dst):
    with ExitStack() as ctx:
        index = ctx.enter_context(nc.sbuf_tensor(f"{tag}_index_of_slots", [P, SLOTS], I32))
        expert_at = ctx.enter_context(nc.sbuf_tensor(f"{tag}_expert_of_tile", [1, SLOTS], I32))
        chosen = ctx.enter_context(nc.sbuf_tensor(f"{tag}_chosen", [P, TILES * E], F16))
        score_stage(nc, tag + "s", w, src, chosen)
        routing_stage(nc, tag + "r", w, chosen, index, expert_at)
        expert_stage(nc, tag + "e", w, index, expert_at, src, dst)


def spectra_stage(nc, w, src, es, means, vspec):
    with ExitStack() as ctx:
        sb = lambda name, shape: ctx.enter_context(nc.sbuf_tensor(f"sp_{name}", shape, F32))
        sems = []
        sem = lambda name: sems.append(ctx.enter_context(nc.semaphore(f"sp_{name}"))) or sems[-1]
        HF = NF - 1
        x = [sb(f"x{u}", [P, 2 * NJ, D]) for u in range(2)]
        n = sb("n", [P, 2, NJ * D])
        sd = [sb(f"sd{u}", [P, 2, NJ * D]) for u in range(2)]
        stats = sb("stats", [P, 2 * NJ, 6])
        mv = sb("mv", [P, 2 * NJ, 2])
        var, root, rstd, tmp = (sb(k, [P, 2 * NJ]) for k in ("var", "root", "rstd", "tmp"))
        even = sb("even", [P, KB, 512])
        X = sb("X", [P, KB, L + 4])
        XN = sb("XN", [P, KB, B])
        q = sb("q", [P, KB, L])
        sq = sb("sq", [P, KB, L])
        mag = sb("mag", [P, KB, HF])
        qk = sb("qk", [P, KB, HF])
        acc = sb("acc", [P, 2, KB])
        esb = [sb(f"es{u}", [H, 2, HF]) for u in range(2)]
        qn, kn, magn, qkn = (sb(k, [P, KB, B]) for k in ("qn", "kn", "magn", "qkn"))
        esn = sb("esn", [H, 2, B])
        ps = [ctx.enter_context(nc.psum_tensor(f"sp_ps{i}", [P, 512], F32)) for i in range(8)]
        x_in = [sem(f"x_in{u}") for u in range(2)]
        es_out = [sem(f"es_out{u}") for u in range(2)]
        names = ("var_ready root_ready x_used n_ready dft_ready even_ready X_ready proj_ready q_ready v_ready k_used "
                 "sq_ready mag_in mag_ready qk_ready sums_ready es_ready ln_step dve_step nyq_ready nyq_step turn").split()
        S = {k: sem(k) for k in names}
        turn = S["turn"]
        start_at_one(nc, sems)
        ctx.callback(back_to_zero, nc, sems)
        block = ctx.enter_context(nc.Block())
        PAIRS = B // 2
        seq = src.rearrange("(b h p j) c -> b p h (j c)", b=B, h=2, j=NJ)
        es3 = es.rearrange("r (c n) -> r c n", c=2)

        @block.sync
        def _(sp):
            def load(i, u):
                sp.dma_start(x[u][:, :, :].rearrange("p (h j) c -> p h (j c)", h=2),
                             seq[bass.ds(2 * i + u, 1), :, :, :].rearrange("a p h c -> (a p) h c")).then_inc(x_in[u], 16)

            def store(i, u):
                b = 2 * i + u
                sp.wait_ge(S["es_ready"], 2 * (b + 1) + 1)
                sp.sem_inc(turn, 1)
                sp.dma_start(es3[bass.ds(b * H, H), :, 0:HF], esb[u][:, :, :]).then_inc(es_out[u], 16)

            for u in range(2):
                load(0, u)
            with sp.Fori(0, PAIRS - 1) as i:
                for u in range(2):
                    sp.wait_ge(S["x_used"], 2 * i + u + 1 + 1)
                    sp.sem_inc(turn, 1)
                    load(i + 1, u)
                    store(i, u)
            for u in range(2):
                store(PAIRS - 1, u)
            sp.wait_ge(S["nyq_ready"], 3 + 1)
            with nc.allow_non_contiguous_dma(reason="one frequency of every row, once"):
                for c in range(2):
                    sp.dma_start(es.rearrange("(b h) n -> h b n", h=H)[:, :, c * NF + HF:c * NF + HF + 1],
                                 esn[:, c, :].unsqueeze(2)).then_inc(es_out[c], 16)
            for u in range(2):
                sp.wait_ge(es_out[u], 16 * (PAIRS + 1) + 1)

        @block.vector
        def _(dve):
            def statistics(i, b, u):
                dve.wait_ge(x_in[u], 16 * (i + 1) + 1)
                ch = Chain(dve, S["ln_step"], b * (LN_STEPS + 1))
                layer_norm_stats(nc, ch, turn, stats, mv, x[u], 2 * NJ)
                ch.link(nc.vector.tensor_scalar(var[:, :], mv[:, :, 1], EPS, None, ALU.add))
                dve.sem_inc(S["var_ready"], 1)
                return ch

            def normalise(ch, b, u):
                dve.wait_ge(S["root_ready"], b + 1 + 1)
                rsqrt_refine(nc, ch, var[:, :], root[:, :], rstd[:, :], tmp[:, :])
                for r in range(2 * NJ):
                    ins = nc.vector.tensor_scalar(n[:, r // NJ, r % NJ * D:(r % NJ + 1) * D], x[u][:, r, :],
                                                  mv[:, r, 0:1], rstd[:, r:r + 1], ALU.subtract, ALU.mult)
                ch.link(ins)
                dve.sem_inc(S["x_used"], 1)
                nc.vector.tensor_tensor(sd[u][:, 0, :], n[:, 0, :], n[:, 1, :], ALU.add)
                nc.vector.tensor_tensor(sd[u][:, 1, :], n[:, 0, :], n[:, 1, :], ALU.subtract).then_inc(S["n_ready"], 1)

            def combine(b):
                for k in range(KB):
                    dve.wait_ge(S["even_ready"], KB * b + k + 1 + 1)
                    dve.wait_ge(S["dft_ready"], 4 * b + 2 * k + 2 + 1)
                    ev = even[:, k, :].rearrange("p (d c g) -> p c g d", d=2, c=2)
                    od = ps[2 * k + 1][:, :].rearrange("p (d c g) -> p c g d", d=2, c=2)
                    view = lambda lo, hi, step: X[:, k, lo:hi:step].rearrange("p (g d) -> p g d", d=2)
                    nc.vector.tensor_tensor(view(0, 256, 1), ev[:, 0], od[:, 0], ALU.add)
                    nc.vector.tensor_tensor(view(512, 256, -1), ev[:, 0], od[:, 0], ALU.subtract)
                    nc.vector.tensor_tensor(view(514, 770, 1), ev[:, 1], od[:, 1], ALU.add)
                    nc.vector.tensor_tensor(view(1026, 770, -1), od[:, 1], ev[:, 1], ALU.subtract)
                    nc.vector.tensor_tensor(XN[:, k, bass.ds(b, 1)], even[:, k, 0:1], ps[2 * k + 1][:, 0:1],
                                            ALU.subtract)
                    nc.vector.tensor_copy(X[:, k, 256:257], even[:, k, 128:129])
                    nc.vector.tensor_copy(X[:, k, 770:771], ps[2 * k + 1][:, 128:129]).then_inc(S["X_ready"], 1)

            def scores(b, m):
                dve.wait_ge(S["proj_ready"], 8 * b + 4 * m + 3 + 1)
                dve.wait_ge(S["q_ready"], KB * b + m + 1 + 1)
                nc.vector.scalar_tensor_tensor(out=qk[:, m, 0:1], in0=ps[6][:, 0:1], scalar=w["bias"][:, 1, m:m + 1],
                                               in1=q[:, m, 0:1], op0=ALU.add, op1=ALU.mult)
                nc.vector.tensor_tensor(qk[:, m, 1:512], ps[6][:, 1:512], q[:, m, 1:512],
                                        ALU.mult).then_inc(S["k_used"], 1)
                nc.vector.tensor_tensor(means[:, 0, m, bass.ds(b, 1)], acc[:, 0, m:m + 1], q[:, m, 0:1], ALU.add)
                nc.vector.tensor_copy(means[:, 1, m, bass.ds(b, 1)], acc[:, 1, m:m + 1]).then_inc(S["qk_ready"], 1)

            def turn_of(b, following):
                combine(b)
                if following:
                    ch = statistics(*following)
                scores(b, 0)
                if following:
                    normalise(ch, *following[1:])
                scores(b, 1)

            normalise(statistics(0, 0, 0), 0, 0)
            with dve.Fori(0, PAIRS - 1) as i:
                turn_of(2 * i, (i, 2 * i + 1, 1))
                turn_of(2 * i + 1, (i + 1, 2 * i + 2, 0))
            turn_of(B - 2, (PAIRS - 1, B - 1, 1))
            turn_of(B - 1, None)
            ch = Chain(dve, S["nyq_step"], 0)
            dve.wait_ge(S["nyq_ready"], 1 + 1)
            ch.link(nc.vector.tensor_copy(qn[:, :, :], ps[0][:, 0:KB * B].rearrange("p (m b) -> p m b", m=KB)))
            nc.vector.tensor_tensor(qkn[:, :, :], ps[0][:, KB * B:2 * KB * B].rearrange("p (m b) -> p m b", m=KB),
                                    qn[:, :, :], ALU.mult)
            nc.vector.tensor_copy(vspec[:, :, HF:B * NF:NF], ps[0][:, 2 * KB * B:3 * KB * B].rearrange("p (m b) -> p m b", m=KB))
            nc.vector.tensor_tensor(means[:, 0, :, :], means[:, 0, :, :], qn[:, :, :], ALU.add)
            ch.link(nc.vector.scalar_tensor_tensor(out=magn[:, :, :], in0=qn[:, :, :], scalar=-1.0, in1=qn[:, :, :],
                                                   op0=ALU.mult, op1=ALU.max))
            dve.wait_ge(S["nyq_ready"], 2 + 1)
            nc.vector.tensor_copy(esn[:, :, :], ps[1][0:H, 0:2 * B].rearrange("p (c b) -> p c b", c=2)).then_inc(S["nyq_ready"], 1)

        @block.scalar
        def _(act):
            def even_out(b):
                for k in range(KB):
                    act.wait_ge(S["dft_ready"], 4 * b + 2 * k + 1 + 1)
                    nc.scalar.copy(even[:, k, :], ps[2 * k][:, :]).then_inc(S["even_ready"], 1)

            def ln_root(b):
                act.wait_ge(S["var_ready"], b + 1 + 1)
                nc.scalar.activation(root[:, :], var[:, :], ACT.Sqrt).then_inc(S["root_ready"], 1)

            def project_out(b, following):
                act.wait_ge(S["qk_ready"], KB * b + 1)
                act.wait_ge(S["sq_ready"], KB * b + 1)
                for m in range(KB):
                    act.wait_ge(S["proj_ready"], 8 * b + 4 * m + 1 + 1)
                    nc.scalar.activation(q[:, m, 0:1], ps[4][:, 0:1], ACT.Identity, bias=w["bias"][:, 0, m:m + 1])
                    nc.scalar.activation(q[:, m, 1:512], ps[4][:, 1:512], ACT.Identity, accum_out=acc[:, 0, m:m + 1])
                    act.wait_ge(S["proj_ready"], 8 * b + 4 * m + 2 + 1)
                    nc.scalar.activation(q[:, m, 513:1024], ps[5][:, 1:512], ACT.Identity,
                                         accum_out=acc[:, 1, m:m + 1]).then_inc(S["q_ready"], 1)
                    if m == 0 and following is not None:
                        ln_root(following)
                    act.wait_ge(S["proj_ready"], 8 * b + 4 * m + 4 + 1)
                    nc.scalar.activation(vspec[:, m, bass.ds(b * NF, 1)], ps[7][:, 0:1], ACT.Identity,
                                         bias=w["bias"][:, 2, m:m + 1])
                    nc.scalar.copy(vspec[:, m, bass.ds(b * NF + 1, 511)], ps[7][:, 1:512]).then_inc(S["v_ready"], 1)
                for m in range(KB):
                    if m == 0:
                        act.wait_ge(S["sums_ready"], 2 * b + 1)
                    act.wait_ge(S["mag_in"], KB * b + m + 1 + 1)
                    nc.scalar.activation(mag[:, m, :], sq[:, m, 0:512], ACT.Sqrt).then_inc(S["mag_ready"], 1)

            def sums_out(b, i, u):
                act.wait_ge(es_out[u], 16 * i + 1)
                for r in range(2):
                    act.wait_ge(S["sums_ready"], 2 * b + r + 1 + 1)
                    nc.scalar.copy(esb[u][:, r, :], ps[5 + r][0:H, :]).then_inc(S["es_ready"], 1)

            ln_root(0)
            even_out(0)
            with act.Fori(0, PAIRS - 1) as i:
                for u in range(2):
                    b = 2 * i + u
                    project_out(b, b + 1)
                    even_out(b + 1)
                    sums_out(b, i, u)
            project_out(B - 2, B - 1)
            even_out(B - 1)
            sums_out(B - 2, PAIRS - 1, 0)
            project_out(B - 1, None)
            sums_out(B - 1, PAIRS - 1, 1)

        @block.gpsimd
        def _(pool):
            def squares(b):
                for m in range(KB):
                    if m == 0:
                        pool.wait_ge(S["mag_ready"], KB * b + 1)
                    pool.wait_ge(S["q_ready"], KB * b + m + 1 + 1)
                    nc.gpsimd.tensor_tensor(sq[:, m, 0:512], q[:, m, 0:512], q[:, m, 0:512], ALU.mult)
                    nc.gpsimd.tensor_tensor(sq[:, m, 513:1024], q[:, m, 513:1024], q[:, m, 513:1024],
                                            ALU.mult).then_inc(S["sq_ready"], 1)
                    pool.wait_ge(S["sq_ready"], KB * b + m + 1 + 1)
                    nc.gpsimd.tensor_tensor(sq[:, m, 1:512], sq[:, m, 1:512], sq[:, m, 513:1024],
                                            ALU.add).then_inc(S["mag_in"], 1)

            with pool.Fori(0, B) as b:
                squares(b)

        @block.tensor
        def _(pe):
            def dft(b, u):
                pe.wait_ge(S["n_ready"], b + 1 + 1)
                pe.wait_ge(S["X_ready"], KB * b + 1)
                for k in range(KB):
                    for odd in range(2):
                        for kind in range(2):
                            for c, j in enumerate((odd, odd + 2)):
                                at = (kind * NJ + j) * 256
                                ins = nc.tensor.matmul(ps[2 * k + odd][:, kind * 256:(kind + 1) * 256],
                                                       sd[u][:, kind, j * D + k * P:j * D + (k + 1) * P],
                                                       w["fwd"][:, at:at + 256], start=(c == 0), stop=(c == 1))
                        ins.then_inc(S["dft_ready"], 1)

            def project(b):
                pe.wait_ge(S["es_ready"], 2 * b + 1)
                for m in range(KB):
                    for r, (wt, lo, bank) in enumerate((("Wq", 0, 4), ("Wq", 514, 5), ("Wk", 0, 6), ("Wv", 0, 7))):
                        if r < 2:
                            pe.wait_ge(S["q_ready"], KB * b + m + 1)
                        elif r == 2:
                            pe.wait_ge(S["k_used"], KB * b + m + 1)
                        else:
                            pe.wait_ge(S["v_ready"], KB * b + m + 1)
                        for k in range(KB):
                            if m == 0 and r == 0:
                                pe.wait_ge(S["X_ready"], KB * b + k + 1 + 1)
                            ins = nc.tensor.matmul(ps[bank][:, :], w[wt][:, k, m * P:(m + 1) * P],
                                                   X[:, k, lo:lo + 512], start=(k == 0), stop=(k == KB - 1))
                        ins.then_inc(S["proj_ready"], 1)

            def sums(b):
                pe.wait_ge(S["qk_ready"], KB * (b + 1) + 1)
                for out, val, ready in ((ps[5], mag, "mag_ready"), (ps[6], qk, "qk_ready")):
                    for m in range(KB):
                        pe.wait_ge(S[ready], KB * b + m + 1 + 1)
                        ins = nc.tensor.matmul(out[0:H, :], w["ind"][:, m * H:(m + 1) * H], val[:, m, :],
                                               start=(m == 0), stop=(m == KB - 1))
                    ins.then_inc(S["sums_ready"], 1)

            dft(0, 0)
            with pe.Fori(0, PAIRS - 1) as i:
                for u in range(2):
                    project(2 * i + u)
                    dft(2 * i + u + 1, 1 - u)
                    sums(2 * i + u)
            project(B - 2)
            dft(B - 1, 1)
            sums(B - 2)
            project(B - 1)
            sums(B - 1)
            for c, wt in enumerate(("Wq", "Wk", "Wv")):
                for m in range(KB):
                    at = (c * KB + m) * B
                    for k in range(KB):
                        ins = nc.tensor.matmul(ps[0][:, at:at + B], w[wt][:, k, m * P:(m + 1) * P], XN[:, k, :],
                                               start=(k == 0), stop=(k == KB - 1))
            ins.then_inc(S["nyq_ready"], 1)
            pe.wait_ge(S["nyq_step"], 2 + 1)
            for c, val in enumerate((magn, qkn)):
                for m in range(KB):
                    ins = nc.tensor.matmul(ps[1][0:H, c * B:(c + 1) * B], w["ind"][:, m * H:(m + 1) * H], val[:, m, :],
                                           start=(m == 0), stop=(m == KB - 1))
            ins.then_inc(S["nyq_ready"], 1)


def selection_stage(nc, es, attn, outside):
    with ExitStack() as ctx:
        sb = lambda name, shape: ctx.enter_context(nc.sbuf_tensor(f"sel_{name}", shape, F32))
        sems = []
        sem = lambda name: sems.append(ctx.enter_context(nc.semaphore(f"sel_{name}"))) or sems[-1]
        G = B * H // P
        row = [sb(f"row{g}", [P, 2 * NF]) for g in range(G)]
        top = [sb(f"top{g}", [P, 8]) for g in range(G)]
        outs = [sb(f"outside{g}", [P, NF]) for g in range(G)]
        prob = [sb(f"prob{g}", [P, NF]) for g in range(G)]
        col = [sb(f"col{g}", [P, 4]) for g in range(G)]
        row_in = [sem(f"row_in{g}") for g in range(G)]
        step, max_ready, exp_ready, out_ready, stored = (sem(k) for k in ("step", "max_ready", "exp_ready", "out_ready", "stored"))
        turn = sem("turn")
        start_at_one(nc, sems)
        ctx.callback(back_to_zero, nc, sems)
        block = ctx.enter_context(nc.Block())

        @block.sync
        def _(sp):
            for g in range(G):
                sp.dma_start(row[g][:, :], es[g * P:(g + 1) * P, :]).then_inc(row_in[g], 16)
            for g in range(G):
                sp.wait_ge(out_ready, g + 1 + 1)
                sp.sem_inc(turn, 1)
                sp.dma_start(attn[g * P:(g + 1) * P, :], prob[g][:, :]).then_inc(stored, 16)
                sp.dma_start(outside[g * P:(g + 1) * P, :], outs[g][:, :]).then_inc(stored, 16)
            sp.wait_ge(stored, 32 * G + 1)
            sp.sem_inc(turn, 1)

        @block.vector
        def _(dve):
            ch = Chain(dve, step, 0)
            for g in range(G):
                dve.wait_ge(row_in[g], 16 + 1)
                energy, score = row[g][:, 0:NF], row[g][:, NF:2 * NF]
                for _ in range(KTOP // 8):
                    ch.link(nc.vector.max(out=top[g][:, :], in_=energy))
                    ch.link(nc.vector.match_replace(out=energy, in_to_replace=top[g][:, :], in_values=energy,
                                                    imm_value=-1.0))
                ch.link(nc.vector.tensor_scalar(outs[g][:, :], energy, 0.0, None, ALU.is_ge))
                ch.link(nc.vector.scalar_tensor_tensor(out=score, in0=outs[g][:, :], scalar=NEG, in1=score,
                                                       op0=ALU.mult, op1=ALU.add))
                ch.link(nc.vector.reduce_max(col[g][:, 0:1], score, AX.X))
                nc.vector.tensor_scalar(col[g][:, 1:2], col[g][:, 0:1], -1.0 / DH ** 0.5, None,
                                        ALU.mult).then_inc(max_ready, 1)
            for g in range(G):
                dve.wait_ge(exp_ready, g + 1 + 1)
                ch.link(nc.vector.reciprocal(col[g][:, 3:4], col[g][:, 2:3]))
                nc.vector.tensor_scalar(prob[g][:, :], prob[g][:, :], col[g][:, 3:4], None,
                                        ALU.mult).then_inc(out_ready, 1)

        @block.scalar
        def _(act):
            for g in range(G):
                act.wait_ge(max_ready, g + 1 + 1)
                nc.scalar.activation(prob[g][:, :], row[g][:, NF:2 * NF], ACT.Exp, bias=col[g][:, 1:2],
                                     scale=1.0 / DH ** 0.5, accum_out=col[g][:, 2:3]).then_inc(exp_ready, 1)


def synthesis_stage(nc, w, src, attn, outside, means, vspec, dst):
    with ExitStack() as ctx:
        sb = lambda name, shape: ctx.enter_context(nc.sbuf_tensor(f"sy_{name}", shape, F32))
        sems = []
        sem = lambda name: sems.append(ctx.enter_context(nc.semaphore(f"sy_{name}"))) or sems[-1]
        GS = 4
        R = GS * H
        G = B // GS
        x = [sb(f"x{u}", [P, 2, NJ * D]) for u in range(2)]
        at = [sb(f"at{u}", [H, NF]) for u in range(2)]
        out_rows = sb("out_rows", [R, NF])
        outT = sb("outT", [P, 4, R])
        outT_nyq = sb("outT_nyq", [1, R])
        kc = sb("kc", [P, 2, 512])
        cind = sb("cind", [P, 2, KB, R])
        z = sb("z", [P, D])
        zb = sb("zb", [P, GS, D])
        av = sb("av", [P, KB, NF])
        meansc = sb("meansc", [P, 2, KB, B])
        y = sb("y", [P, 5, D])
        y0 = sb("y0", [1, D])
        pa = [ctx.enter_context(nc.psum_tensor(f"sy_pa{i}", [P, 512], F32)) for i in range(2)]
        py = [ctx.enter_context(nc.psum_tensor(f"sy_py{i}", [P, 512], F32)) for i in range(2)]
        po = [ctx.enter_context(nc.psum_tensor(f"sy_po{i}", [P, 512], F32)) for i in range(4)]
        x_in = [sem(f"x_in{u}") for u in range(2)]
        at_in = [sem(f"at_in{u}") for u in range(2)]
        x_out = [sem(f"x_out{u}") for u in range(2)]
        names = ("rows_in mean_ready cind_ready outT_in_psum outT_ready kc_in_psum kc_ready z_in_psum z_ready zb_ready "
                 "spread_ready av_ready y_in_psum y_copied y_ready p_ready p_used inv_done o_ready row_step acc_step").split()
        S = {k: sem(k) for k in names}
        turn = sem("turn")
        start_at_one(nc, sems)
        ctx.callback(back_to_zero, nc, sems)
        block = ctx.enter_context(nc.Block())
        seq = src.rearrange("(b h p j) c -> b p h (j c)", b=B, h=2, j=NJ)
        oseq = dst.rearrange("(b h p j) c -> b p h (j c)", b=B, h=2, j=NJ)
        one = lambda ap, b: ap[bass.ds(b, 1), :, :, :].rearrange("a p h c -> (a p) h c")

        @block.sync
        def _(sp):
            with sp.Fori(0, G) as g:
                sp.wait_ge(S["outT_ready"], 5 * g + 1)
                sp.sem_inc(turn, 1)
                sp.dma_start(out_rows[:, :], outside[bass.ds(g * R, R), :]).then_inc(S["rows_in"], 16)
                for s in range(GS):
                    b, u = GS * g + s, s % 2
                    if s >= 2:
                        sp.wait_ge(x_out[u], 16 * (2 * g + s // 2) + 1)
                        sp.sem_inc(turn, 1)
                        sp.wait_ge(S["av_ready"], (KB + 1) * (b - 1) + 1)
                        sp.sem_inc(turn, 1)
                    else:
                        sp.wait_ge(x_out[u], 16 * 2 * g + 1)
                        sp.sem_inc(turn, 1)
                        sp.wait_ge(S["av_ready"], (KB + 1) * GS * g + 1)
                        sp.sem_inc(turn, 1)
                    sp.dma_start(x[u][:, :, :], one(seq, b)).then_inc(x_in[u], 16)
                    sp.dma_start(at[u][:, :], attn[bass.ds(b * H, H), :]).then_inc(at_in[u], 16)
            for u in range(2):
                sp.wait_ge(x_out[u], 16 * (B // 2) + 1)
                sp.sem_inc(turn, 1)

        @block.vector
        def _(dve):
            def group(g):
                if g is None:
                    return
                dve.wait_ge(S["z_in_psum"], g + 1)
                for c in range(2):
                    for m in range(KB):
                        ins = nc.vector.tensor_tensor(
                            cind[:, c, m, :].rearrange("p (s h) -> p s h", s=GS),
                            w["ind"][:, m * H:(m + 1) * H].unsqueeze(1).broadcast_to([P, GS, H]),
                            meansc[:, c, m, bass.ds(GS * g, GS)].unsqueeze(2).broadcast_to([P, GS, H]), ALU.mult)
                ins.then_inc(S["cind_ready"], 1)
                dve.wait_ge(S["z_ready"], g + 1 + 1)
                for s in range(GS):
                    ins = nc.vector.tensor_scalar(zb[:, s, :], z[:, :], w["rowsel"][:, s:s + 1], None, ALU.mult)
                ins.then_inc(S["zb_ready"], 1)

            def attend(g, b, s):
                for m in range(KB):
                    dve.wait_ge(S["spread_ready"], 3 * b + m + 1 + 1)
                    nc.vector.tensor_tensor(av[:, m, 0:512], pa[m][:, :], vspec[:, m, bass.ds(b * NF, 512)],
                                            ALU.mult).then_inc(S["av_ready"], 1)
                dve.wait_ge(S["spread_ready"], 3 * b + 3 + 1)
                for m in range(KB):
                    ins = nc.vector.tensor_tensor(av[:, m, 512:513], py[0][:, m:m + 1],
                                                  vspec[:, m, bass.ds(b * NF + 512, 1)], ALU.mult)
                ins.then_inc(S["av_ready"], 1)

            def frequency0(b):
                ch = Chain(dve, S["row_step"], 3 * b)
                dve.wait_ge(S["y_copied"], 3 * b + 3 + 1)
                ch.link(nc.vector.tensor_tensor(y0[0:1, :], y[0:1, 0, :], w["bo"][0:1, :], ALU.add))
                ch.link(nc.vector.tensor_tensor(y[0:1, 0, :], y0[0:1, :], pa[0][0:1, 0:D], ALU.add))
                ch.link(nc.vector.tensor_tensor(y[0:1, 4, :], y0[0:1, :], pa[0][0:1, 0:D], ALU.subtract))
                dve.sem_inc(S["y_ready"], 1)

            def residual(g, b, s):
                u = s % 2
                dve.wait_ge(x_in[u], 16 * (2 * g + s // 2 + 1) + 1)
                ch = Chain(dve, S["acc_step"], 4 * b)
                for jj in range(2):
                    cols = slice(jj * 512, (jj + 1) * 512)
                    x0, x1 = x[u][:, 0, cols], x[u][:, 1, cols]
                    dve.wait_ge(S["p_ready"], 4 * b + 2 * jj + 1 + 1)
                    nc.vector.tensor_tensor(x0, x0, po[2 * jj][:, :], ALU.add)
                    ch.link(nc.vector.tensor_tensor(x1, x1, po[2 * jj][:, :], ALU.add))
                    dve.sem_inc(S["p_used"], 1)
                    dve.wait_ge(S["p_ready"], 4 * b + 2 * jj + 2 + 1)
                    nc.vector.tensor_tensor(x0, x0, po[2 * jj + 1][:, :], ALU.add)
                    ch.link(nc.vector.tensor_tensor(x1, x1, po[2 * jj + 1][:, :], ALU.subtract))
                    dve.sem_inc(S["p_used"], 1)
                dve.sem_inc(S["o_ready"], 1)

            nc.vector.tensor_scalar(meansc[:, :, :, :], means[:, :, :, :], 1.0 / NF, None, ALU.mult).then_inc(S["mean_ready"], 1)
            dve.wait_ge(S["mean_ready"], 1 + 1)
            with dve.Fori(0, G) as g:
                group(g)
                attend(g, GS * g, 0)
                frequency0(GS * g)
                for s in range(GS):
                    b = GS * g + s
                    if s + 1 < GS:
                        attend(g, b + 1, s + 1)
                    residual(g, b, s)
                    if s + 1 < GS:
                        frequency0(b + 1)

        @block.scalar
        def _(act):
            def group(g):
                act.wait_ge(S["outT_in_psum"], 5 * g + 5 + 1)
                for i in range(4):
                    nc.scalar.copy(outT[:, i, :], pa[0][:, i * R:(i + 1) * R]).then_inc(S["outT_ready"], 1)
                nc.scalar.copy(outT_nyq[:, :], pa[0][0:1, 4 * R:5 * R]).then_inc(S["outT_ready"], 1)
                act.wait_ge(S["z_in_psum"], g + 1 + 1)
                nc.scalar.copy(z[:, :], pa[1][:, 0:D]).then_inc(S["z_ready"], 1)
                for par in range(2):
                    act.wait_ge(S["kc_in_psum"], 2 * g + par + 1 + 1)
                    nc.scalar.copy(kc[:, par, :], py[par][:, :]).then_inc(S["kc_ready"], 1)

            def spectrum_out(b):
                act.wait_ge(S["y_in_psum"], 3 * b + 1 + 1)
                nc.scalar.copy(y[:, 0:2, :].rearrange("p a d -> p (a d)"), py[0][:, :]).then_inc(S["y_copied"], 1)
                nc.scalar.copy(y[:, 4, :], py[0][:, 0:D]).then_inc(S["y_copied"], 1)
                act.wait_ge(S["y_in_psum"], 3 * b + 3 + 1)
                nc.scalar.copy(y[:, 2:4, :].rearrange("p a d -> p (a d)"), py[1][:, :]).then_inc(S["y_copied"], 1)

            with act.Fori(0, G) as g:
                group(g)
                spectrum_out(GS * g)
                for s in range(GS):
                    b = GS * g + s
                    if s + 1 < GS:
                        spectrum_out(b + 1)
                    act.wait_ge(S["o_ready"], b + 1 + 1)
                    act.sem_inc(turn, 1)
                    act.dma_start(one(oseq, b), x[s % 2][:, :, :]).then_inc(x_out[s % 2], 16)

        @block.tensor
        def _(pe):
            def group(g):
                pe.wait_ge(S["rows_in"], 16 * (g + 1) + 1)
                pe.sem_inc(turn, 1)
                for par in range(2):
                    for qt in range(2):
                        i = 2 * par + qt
                        lo = 256 * qt + par
                        nc.tensor.transpose(pa[0][:, i * R:(i + 1) * R], out_rows[:, lo:lo + 255:2],
                                            w["ident"][0:R, 0:R]).then_inc(S["outT_in_psum"], 1)
                nc.tensor.transpose(pa[0][0:1, 4 * R:5 * R], out_rows[:, 512:513],
                                    w["ident"][0:R, 0:R]).then_inc(S["outT_in_psum"], 1)
                pe.wait_ge(S["cind_ready"], g + 1 + 1)
                for c in range(2):
                    for m in range(KB):
                        ins = nc.tensor.matmul(pa[1][c * R:(c + 1) * R, 0:D], cind[:, c, m, :], w["Wo"][:, m, :],
                                               start=(m == 0), stop=(m == KB - 1))
                ins.then_inc(S["z_in_psum"], 1)
                pe.wait_ge(S["outT_ready"], 5 * (g + 1) + 1)
                for par in range(2):
                    for c, tab in ((0, "cinv"), (1, "sinv")):
                        nyq = par == 0 and c == 0
                        for qt in range(2):
                            i = 2 * par + qt
                            ins = nc.tensor.matmul(py[par][c * R:(c + 1) * R, :], outT[:, i, :],
                                                   w[tab][:, i * 512:(i + 1) * 512], start=(qt == 0),
                                                   stop=(qt == 1 and not nyq))
                        if nyq:
                            ins = nc.tensor.matmul(py[par][0:R, :], outT_nyq[:, :], w["cnyq"][:, :],
                                                   start=False, stop=True)
                    ins.then_inc(S["kc_in_psum"], 1)
                pe.wait_ge(S["kc_ready"], 2 * (g + 1) + 1)
                pe.wait_ge(S["z_ready"], g + 1 + 1)

            def spread(g, b, s):
                u = s % 2
                pe.wait_ge(at_in[u], 16 * (2 * g + s // 2 + 1) + 1)
                if s > 0:
                    pe.wait_ge(S["y_ready"], b + 1)
                for m in range(KB):
                    nc.tensor.matmul(pa[m][:, :], w["indt"][:, m * P:(m + 1) * P], at[u][:, 0:512],
                                     start=True, stop=True).then_inc(S["spread_ready"], 1)
                for m in range(KB):
                    ins = nc.tensor.matmul(py[0][:, m:m + 1], w["indt"][:, m * P:(m + 1) * P], at[u][:, 512:513],
                                           start=True, stop=True)
                ins.then_inc(S["spread_ready"], 1)

            def project(b):
                pe.wait_ge(S["av_ready"], (KB + 1) * (b + 1) + 1)
                for par in range(2):
                    for qt in range(2):
                        lo = 256 * qt + par
                        for m in range(KB):
                            ins = nc.tensor.matmul(py[par][:, qt * D:(qt + 1) * D], av[:, m, lo:lo + 255:2],
                                                   w["Wo"][:, m, :], start=(m == 0), stop=(m == KB - 1))
                    if par == 0:
                        ins.then_inc(S["y_in_psum"], 1)
                        for m in range(KB):
                            ins = nc.tensor.matmul(pa[0][0:1, 0:D], av[:, m, 512:513], w["Wo"][:, m, :],
                                                   start=(m == 0), stop=(m == KB - 1))
                        ins.then_inc(S["y_in_psum"], 1)
                    else:
                        ins.then_inc(S["y_in_psum"], 1)

            def inverse(g, b, s):
                pe.wait_ge(S["y_ready"], b + 1 + 1)
                pe.wait_ge(S["zb_ready"], g + 1 + 1)
                for jj in range(2):
                    for par in range(2):
                        pe.wait_ge(S["p_used"], 4 * b + 1)
                        for j in (2 * jj, 2 * jj + 1):
                            out = po[2 * jj + par][:, (j % 2) * D:(j % 2 + 1) * D]
                            for qt in range(2):
                                i = 2 * par + qt
                                yt = 4 if (par == 0 and qt == 0 and j % 2 == 1) else i
                                nc.tensor.matmul(out, w["cinv"][:, i * 512 + j * P:i * 512 + (j + 1) * P],
                                                 y[:, yt, :], start=(qt == 0), stop=False)
                            ins = nc.tensor.matmul(out, kc[:, par, j * P:(j + 1) * P], zb[:, s, :],
                                                   start=False, stop=True)
                        ins.then_inc(S["p_ready"], 1)

            with pe.Fori(0, G) as g:
                group(g)
                spread(g, GS * g, 0)
                project(GS * g)
                for s in range(GS):
                    b = GS * g + s
                    if s + 1 < GS:
                        spread(g, b + 1, s + 1)
                    inverse(g, b, s)
                    if s + 1 < GS:
                        project(b + 1)


def build(nc, args, cst, out):
    x1 = nc.dram_tensor("x1", (B * L, D), F32, kind="Internal").ap()
    x2 = nc.dram_tensor("x2", (B * L, D), F32, kind="Internal").ap()
    es = nc.dram_tensor("energy_score", (B * H, 2 * NF), F32, kind="Internal").ap()
    attn = nc.dram_tensor("attn", (B * H, NF), F32, kind="Internal").ap()
    outside = nc.dram_tensor("outside", (B * H, NF), F32, kind="Internal").ap()
    query = args["L0_attn_query"].rearrange("b l d -> (b l) d")
    out = out.rearrange("b l d -> (b l) d")
    with ExitStack() as ctx:
        w = {}
        for k, a in cst.items():
            w[k] = ctx.enter_context(nc.sbuf_tensor(f"w_{k}", list(a.shape), a.dtype))
        for k in ("Wq", "Wk", "Wv", "Wo"):
            w[k] = ctx.enter_context(nc.sbuf_tensor(f"w_{k}", [P, KB, D], F32))
        w["bias"] = ctx.enter_context(nc.sbuf_tensor("w_bias", [P, 3, KB], F32))
        w["bo"] = ctx.enter_context(nc.sbuf_tensor("w_bo", [1, D], F32))
        w["gate"] = ctx.enter_context(nc.sbuf_tensor("w_gate", [P, KB * E], F32))
        w["expert"] = ctx.enter_context(nc.sbuf_tensor("w_expert", [P, KB, E * D], F32))
        setup_weights(nc, w, args, cst)
        routed_experts(nc, "ffn1", w, query, x1)
        with ExitStack() as mid:
            means = mid.enter_context(nc.sbuf_tensor("means", [P, 2, KB, B], F32))
            vspec = mid.enter_context(nc.sbuf_tensor("vspec", [P, KB, B * NF], F32))
            spectra_stage(nc, w, x1, es, means, vspec)
            selection_stage(nc, es, attn, outside)
            synthesis_stage(nc, w, x1, attn, outside, means, vspec, x2)
        routed_experts(nc, "ffn2", w, x2, out)


_INS = ["L0_attn_query", "L0_attn_Wq", "L0_attn_bq", "L0_attn_Wk", "L0_attn_bk", "L0_attn_Wv", "L0_attn_bv",
        "L0_attn_Wo", "L0_attn_bo", "L0_ffn_gate_w", "L0_ffn_expert_w"]


def kernel(**inputs):
    import concourse.bacc as bacc
    from concourse.bass_utils import run_bass_kernel_spmd

    nc = bacc.Bacc("TRN2", target_bir_lowering=False, num_devices=1)
    arrays, args, cst = {}, {}, {}
    for name in _INS:
        a = np.ascontiguousarray(inputs[name])
        arrays[name + "_dram"] = a
        args[name] = nc.dram_tensor(name + "_dram", a.shape, mybir.dt.from_np(a.dtype), kind="ExternalInput").ap()
    for name, a in constants().items():
        arrays["c_" + name] = a
        cst[name] = nc.dram_tensor("c_" + name, a.shape, mybir.dt.from_np(a.dtype), kind="ExternalInput").ap()
    out = nc.dram_tensor("out_dram", (B, L, D), F32, kind="ExternalOutput").ap()
    build(nc, args, cst, out)
    r = run_bass_kernel_spmd(nc, [arrays], core_ids=[0])
    return r.results[0]["out_dram"]
```

```python
import numpy as np
import concourse.bass as bass
from concourse import mybir
from contextlib import ExitStack

F32 = mybir.dt.float32
F32R = mybir.dt.float32r
ALU = mybir.AluOpType
ACT = mybir.ActivationFunctionType
AX = mybir.AxisListType

P = 128
B, L, D = 16, 1024, 256
H = 16
DH = D // H
NF = L // 2 + 1
KTOP = 64
E = 8
KB = D // P
NJ = 4
HL = L // 2
EPS = 1e-5
NEG = -3.0e38
TILES = B * L // P
SLOTS = TILES + E
BIG = 2000000
F16 = mybir.dt.float16
I32 = mybir.dt.int32


def constants():
    p = np.arange(P)
    w = 2 * np.pi / L
    fwd = np.zeros((P, 2, NJ, 256))
    for kind in range(2):
        for j in range(NJ):
            t = (4 * p + j)[:, None]
            f = 2 * np.arange(128)[None, :] + kind
            c, sn = np.cos(w * ((t * f) % L)), np.sin(w * ((t * f) % L))
            if kind == 0:
                sn[:, 0:1] = np.cos(w * ((256 * t) % L)) if j % 2 == 0 else np.sin(w * ((256 * t) % L))
            fwd[:, kind, j] = np.concatenate([c, sn], 1)
    t = (4 * p[None, :] + np.arange(NJ)[:, None]).reshape(-1)
    cinv = np.zeros((P, 2, 2, 512))
    sinv = np.zeros((P, 2, 2, 512))
    for par in range(2):
        for qt in range(2):
            f = (2 * (128 * qt + p) + par)[:, None]
            wt = np.where(f == 0, 1.0, 2.0) / L
            cinv[:, par, qt] = wt * np.cos(w * ((f * t) % L))
            sinv[:, par, qt] = wt * np.sin(w * ((f * t) % L))
    cnyq = (np.where(t % 2 == 0, 1.0, -1.0) / L)[None, :]
    head = (np.arange(KB)[None, :] * P + p[:, None]) // DH
    ind = (head[:, :, None] == np.arange(H)).astype(np.float64)
    indt = ind.transpose(2, 1, 0)
    rowsel = ((p[:, None] % 64) // 16 == np.arange(4)).astype(np.float64)
    c = {"fwd": fwd.reshape(P, -1), "cinv": cinv.reshape(P, -1), "sinv": sinv.reshape(P, -1), "cnyq": cnyq,
         "ind": ind.reshape(P, -1), "indt": np.ascontiguousarray(indt).reshape(H, -1), "rowsel": rowsel,
         "ident": np.eye(P), "rank": np.broadcast_to(E - np.arange(E), (P, E)),
         "low": 4 * p[:, None] + np.arange(NJ) + 1, "high": np.broadcast_to(np.arange(2 * B), (P, 2 * B))}
    half = {"before": p[:, None] < p[None, :], "ones": np.ones((P, P)),
            "iota": np.broadcast_to(np.arange(SLOTS), (P, SLOTS))}
    c = {k: np.ascontiguousarray(v, dtype=np.float32) for k, v in c.items()}
    c.update({k: np.ascontiguousarray(v, dtype=np.float16) for k, v in half.items()})
    return c


EXPERT_BUFFERS = 16
KEPT = ("ind", "ident", "rank", "low", "high", "before", "ones", "iota")


def start_at_one(nc, sems):
    with nc.Block() as block:
        @block.sync
        def _(sp):
            for s in sems[0::4]:
                sp.sem_inc(s, 1)

        @block.scalar
        def _(act):
            for s in sems[1::4]:
                act.sem_inc(s, 1)

        @block.vector
        def _(dve):
            for s in sems[2::4]:
                dve.sem_inc(s, 1)

        @block.tensor
        def _(pe):
            for s in sems[3::4]:
                pe.sem_inc(s, 1)


def back_to_zero(nc, sems):
    with nc.Block() as block:
        @block.sync
        def _(sp):
            for s in sems[0::4]:
                sp.sem_clear(s)

        @block.scalar
        def _(act):
            for s in sems[1::4]:
                act.sem_clear(s)

        @block.vector
        def _(dve):
            for s in sems[2::4]:
                dve.sem_clear(s)

        @block.tensor
        def _(pe):
            for s in sems[3::4]:
                pe.sem_clear(s)


class Chain:

    def __init__(self, eng, sem, before):
        self.eng, self.sem, self.before, self.k = eng, sem, before, 0

    def link(self, ins):
        self.k += 1
        ins.then_inc(self.sem, 1)
        self.eng.wait_ge(self.sem, self.before + self.k + 1)

    def behind(self, ins, n):
        self.k += 1
        ins.then_inc(self.sem, 1)
        if self.k >= n:
            self.eng.wait_ge(self.sem, self.before + self.k - n + 1 + 1)

    def link_hold(self, ins, turn):
        self.k += 1
        ins.then_inc(self.sem, 1)
        self.eng.wait_ge(self.sem, self.before + self.k + 1)
        self.eng.sem_inc(turn, 1)


def split_product(nc, out, a, b, start, stop):
    nc.tensor.matmul(out, a[0], b[0], start=start, stop=False)
    nc.tensor.matmul(out, a[0], b[1], start=False, stop=False)
    return nc.tensor.matmul(out, a[1], b[0], start=False, stop=stop)


def layer_norm_stats(nc, ch, turn, stats, mv, x3, n):
    for r in range(n):
        ins = nc.vector.bn_stats(stats[:, r, :], x3[:, r, :])
    ch.link_hold(ins, turn)
    for r in range(n):
        ins = nc.vector.bn_aggr(mv[:, r, :], stats[:, r, :])
    ch.link(ins)


def rsqrt_refine(nc, ch, var, root, r0, tmp):
    ch.link(nc.vector.reciprocal(r0, root))
    ch.link(nc.vector.tensor_tensor(tmp, r0, r0, ALU.mult))
    ch.link(nc.vector.tensor_tensor(tmp, tmp, var, ALU.mult))
    ch.link(nc.vector.tensor_scalar(tmp, tmp, -0.5, 1.5, ALU.mult, ALU.add))
    ch.link(nc.vector.tensor_tensor(r0, r0, tmp, ALU.mult))


LN_STEPS = 2 + 1 + 5


class Experts:

    def __init__(self, nc, ctx, w):
        self.nc, self.w = nc, w
        self.raw = ctx.enter_context(nc.sbuf_tensor("raw_experts", [P, E, KB, D], F32))
        self.mean = ctx.enter_context(nc.sbuf_tensor("expert_mean", [P, E * KB], F32))
        self.loaded, self.folded, self.transposed, self.placed = (
            ctx.enter_context(nc.semaphore(f"experts_{k}")) for k in ("loaded", "folded", "transposed", "placed"))

    def fold(self, dve, e):
        V, folded = self.nc.vector, self.folded
        rows, mean = self.raw[:, e, :, :], self.mean[:, e * KB:(e + 1) * KB]
        dve.wait_ge(self.loaded, 16)
        for fb in range(KB):
            part = rows[:, fb, fb * P:(fb + 1) * P]
            ins = V.tensor_tensor(part, part, self.w["ident"][:, :], ALU.add)
        ins.then_inc(folded, 1)
        dve.wait_ge(folded, 4 * e + 1)
        V.reduce_sum(mean, rows, AX.X).then_inc(folded, 1)
        dve.wait_ge(folded, 4 * e + 2)
        V.tensor_scalar(mean, mean, -0.5 / D, None, ALU.mult).then_inc(folded, 1)
        dve.wait_ge(folded, 4 * e + 3)
        V.scalar_tensor_tensor(out=rows, in0=rows, scalar=0.5, in1=mean.unsqueeze(2).broadcast_to([P, KB, D]),
                               op0=ALU.mult, op1=ALU.add).then_inc(folded, 1)

    def transpose(self, pe, pt):
        pe.wait_ge(self.folded, 4 * E)
        for g in range(E * KB):
            e, k = g // KB, g % KB
            if g >= len(pt):
                pe.wait_ge(self.placed, g - len(pt) + 1)
            for fb in range(KB):
                ins = self.nc.tensor.transpose(pt[g % len(pt)][:, fb * P:(fb + 1) * P],
                                               self.raw[:, e, fb, k * P:(k + 1) * P], self.w["ident"][:, :])
            ins.then_inc(self.transposed, 1)

    def place(self, act, pt):
        for g in range(E * KB):
            e, k = g // KB, g % KB
            act.wait_ge(self.transposed, g + 1)
            self.nc.scalar.copy(self.w["expert"][:, k, e * D:(e + 1) * D], pt[g % len(pt)][:, 0:D]).then_inc(self.placed, 1)


def setup_weights(nc, w, args, cst, experts):
    with ExitStack() as ctx:
        graw = ctx.enter_context(nc.sbuf_tensor("raw_gate", [E, D], F32))
        gmean = ctx.enter_context(nc.sbuf_tensor("gate_mean", [E, 1], F32))
        pt = ctx.enter_context(nc.psum_tensor("setup_ps", [P, 512], F32))
        loaded = ctx.enter_context(nc.semaphore("setup_loaded"))
        transposed = ctx.enter_context(nc.semaphore("setup_transposed"))
        evacuated = ctx.enter_context(nc.semaphore("setup_evacuated"))
        scaled = ctx.enter_context(nc.semaphore("setup_scaled"))
        start_at_one(nc, [loaded, transposed, evacuated, scaled])
        ctx.callback(back_to_zero, nc, [loaded, transposed, evacuated, scaled])
        block = ctx.enter_context(nc.Block())
        loads = [(graw[:, :], args["L0_ffn_gate_w"])]
        for k in KEPT:
            loads.append((w[k][:, :], cst[k]))
        loads.append((w["Wo"][:, :, :], args["L0_attn_Wo"].rearrange("(k p) n -> p k n", p=P)))
        for i, k in enumerate(("bq", "bk", "bv")):
            loads.append((w["bias"][:, i, :], args["L0_attn_" + k].rearrange("(k p) -> p k", p=P)))
        loads.append((w["bo"][0:1, :], args["L0_attn_bo"].rearrange("(a d) -> a d", a=1)))
        total = 16 * len(loads)

        @block.sync
        def _(sp):
            with nc.allow_non_contiguous_dma(reason="three bias vectors, once"):
                for dst, src in loads[:len(loads) // 2]:
                    sp.dma_start(dst, src).then_inc(loaded, 16)
            sp.dma_start(experts.raw[:, :, :, :],
                         args["L0_ffn_expert_w"].rearrange("e (k p) h -> p e k h", p=P)).then_inc(experts.loaded, 16)

        @block.tensor
        def _(pe):
            pe.wait_ge(loaded, total + 1)
            pe.wait_ge(scaled, 4 + 1)
            for k in range(KB):
                ins = nc.tensor.transpose(pt[:, k * E:(k + 1) * E], graw[:, k * P:(k + 1) * P],
                                          w["ident"][0:E, 0:E])
            ins.then_inc(transposed, 1)

        @block.scalar
        def _(act):
            with nc.allow_non_contiguous_dma(reason="three bias vectors, once"):
                for dst, src in loads[len(loads) // 2:]:
                    act.dma_start(dst, src).then_inc(loaded, 16)
            act.wait_ge(transposed, 1 + 1)
            nc.scalar.copy(w["gate"][:, :], pt[:, 0:KB * E]).then_inc(evacuated, 1)
            act.wait_ge(evacuated, 1 + 1)

        @block.vector
        def _(dve):
            dve.wait_ge(loaded, total + 1)
            nc.vector.tensor_scalar(w["bias"][:, :, :], w["bias"][:, :, :], float(L), None, ALU.mult).then_inc(scaled, 1)
            nc.vector.tensor_scalar(w["bo"][:, :], w["bo"][:, :], float(L), None, ALU.mult).then_inc(scaled, 1)
            nc.vector.reduce_sum(gmean[:, :], graw[:, :], AX.X).then_inc(scaled, 1)
            dve.wait_ge(scaled, 3 + 1)
            nc.vector.scalar_tensor_tensor(out=graw[:, :], in0=gmean[:, 0:1].broadcast_to([E, D]), scalar=-1.0 / D,
                                           in1=graw[:, :], op0=ALU.mult, op1=ALU.add).then_inc(scaled, 1)


def score_stage(nc, tag, w, src, chosen, experts=None):
    with ExitStack() as ctx:
        sb = lambda name, shape: ctx.enter_context(nc.sbuf_tensor(f"{tag}_{name}", shape, F32))
        sems = []
        sem = lambda name: sems.append(ctx.enter_context(nc.semaphore(f"{tag}_{name}"))) or sems[-1]
        NX = 4
        NG = P // E
        SEQS = NG // 2
        PARTS = B // SEQS
        PT = NG * NJ
        x = [sb(f"x{u}", [P, 2 * NJ, D]) for u in range(NX)]
        pair = lambda name, shape: tuple(
            ctx.enter_context(nc.sbuf_tensor(f"{tag}_{name}_{part}", shape, F32R)) for part in ("high", "low"))
        xT_s = [pair(f"xT{c}", [P, KB, NJ * P]) for c in range(2)]
        gate_s = pair("gate", [P, KB, 2 * P])
        wide_gate = sb("wide_gate", [P, KB, 2 * P])
        scoresT = sb("scoresT", [P, NJ * P])
        best, code = sb("best", [P, PT]), sb("code", [P, PT])
        hit = sb("hit", [P, PT, E])
        psT = [[ctx.enter_context(nc.psum_tensor(f"{tag}_psT{c}{k}", [P, NJ * P], F32)) for k in range(KB)]
               for c in range(2)]
        psS = ctx.enter_context(nc.psum_tensor(f"{tag}_psS", [P, NJ * P], F32))
        psB = ctx.enter_context(nc.psum_tensor(f"{tag}_psB", [P, NJ * P], F32))
        x_in = [sem(f"x_in{u}") for u in range(NX)]
        xT_in_psum, xT_high, xT_ready, gate_ready, scores_in_psum, scoresT_ready, scores_ready, chosen_ready, step, turn = (
            sem(k) for k in ("xT_in_psum", "xT_high", "xT_ready", "gate_ready", "scores_in_psum", "scoresT_ready",
                             "scores_ready", "chosen_ready", "step", "turn"))
        start_at_one(nc, sems)
        ctx.callback(back_to_zero, nc, sems)
        block = ctx.enter_context(nc.Block())
        seq = src.rearrange("(b h p j) c -> b p h (j c)", b=B, h=2, j=NJ)

        @block.sync
        def _(sp):
            def load(i, u):
                sp.dma_start(x[u][:, :, :].rearrange("p (h j) c -> p h (j c)", h=2),
                             seq[bass.ds(NX * i + u, 1), :, :, :].rearrange("a p h c -> (a p) h c")).then_inc(x_in[u], 16)

            for u in range(NX):
                load(0, u)
            with sp.Fori(0, B // NX - 1) as i:
                for u in range(NX):
                    sp.wait_ge(xT_in_psum, 2 * KB * (NX * i + u + 1) + 1)
                    sp.sem_inc(turn, 1)
                    load(i + 1, u)

        @block.tensor
        def _(pe):
            def transpose(g, s, h):
                for k in range(KB):
                    for j in range(NJ):
                        ins = nc.tensor.transpose(psT[h][k][:, j * P:(j + 1) * P],
                                                  x[s % NX][:, NJ * h + j, k * P:(k + 1) * P], w["ident"][:, :])
                    ins.then_inc(xT_in_psum, 1)

            def scores(i, s, h):
                g = 2 * s + h
                for k in range(KB):
                    pe.wait_ge(xT_ready, KB * (NG * i + g) + k + 1 + 1)
                    at = P - E - E * g
                    first_, last_ = g == 0 and k == 0, g == NG - 1 and k == KB - 1
                    ins = split_product(nc, psS[:, :], [v[:, k, at:at + P] for v in gate_s],
                                        [v[:, k, :] for v in xT_s[h]], first_, last_)
                if g == NG - 1:
                    ins.then_inc(scores_in_psum, 1)

            pe.wait_ge(gate_ready, KB + 3 + 1)
            with pe.Fori(0, PARTS) as i:
                for s in range(SEQS):
                    pe.wait_ge(x_in[s % NX], 16 * (SEQS // NX * i + s // NX + 1) + 1)
                    pe.sem_inc(turn, 1)
                    transpose(i, s, 0)
                    if s > 0:
                        scores(i, s - 1, 1)
                    transpose(i, s, 1)
                    scores(i, s, 0)
                scores(i, SEQS - 1, 1)
                pe.wait_ge(scoresT_ready, i + 1 + 1)
                pe.sem_inc(turn, 1)
                pe.wait_ge(chosen_ready, i + 1)
                pe.sem_inc(turn, 1)
                for j in range(NJ):
                    ins = nc.tensor.transpose(psB[:, j * P:(j + 1) * P], scoresT[:, j * P:(j + 1) * P], w["ident"][:, :])
                ins.then_inc(scores_ready, 1)

        @block.scalar
        def _(act):
            with act.Fori(0, PARTS) as i:
                for g in range(NG):
                    for k in range(KB):
                        act.wait_ge(xT_in_psum, KB * (NG * i + g) + k + 1 + 1)
                        nc.scalar.copy(xT_s[g % 2][0][:, k, :], psT[g % 2][k][:, :]).then_inc(xT_high, 1)
                act.wait_ge(scores_in_psum, i + 1 + 1)
                nc.scalar.copy(scoresT[:, :], psS[:, :]).then_inc(scoresT_ready, 1)

        @block.vector
        def _(dve):
            nc.vector.memset(wide_gate[:, :, :], 0.0).then_inc(gate_ready, 1)
            dve.wait_ge(gate_ready, 1 + 1)
            for k in range(KB):
                nc.vector.tensor_copy(wide_gate[:, k, P - E:P], w["gate"][:, k * E:(k + 1) * E]).then_inc(gate_ready, 1)
            dve.wait_ge(gate_ready, KB + 1 + 1)
            nc.vector.tensor_copy(gate_s[0][:, :, :], wide_gate[:, :, :]).then_inc(gate_ready, 1)
            dve.wait_ge(gate_ready, KB + 2 + 1)
            nc.vector.tensor_tensor(gate_s[1][:, :, :], wide_gate[:, :, :], gate_s[0][:, :, :],
                                    ALU.subtract).then_inc(gate_ready, 1)
            def part_of(i, fold=False):
                for g in range(NG):
                    for k in range(KB):
                        dve.wait_ge(xT_high, KB * (NG * i + g) + k + 1 + 1)
                        nc.vector.tensor_tensor(xT_s[g % 2][1][:, k, :], psT[g % 2][k][:, :], xT_s[g % 2][0][:, k, :],
                                                ALU.subtract).then_inc(xT_ready, 1)
                    if fold and g % 2 == 1:
                        experts.fold(dve, g // 2)
                ch = Chain(dve, step, 5 * i)
                dve.wait_ge(scores_ready, i + 1 + 1)
                sc = psB[:, :].rearrange("p (t e) -> p t e", e=E)
                rank = w["rank"][:, :].unsqueeze(1).broadcast_to([P, PT, E])
                wide = [P, PT, E]
                ch.link(nc.vector.reduce_max(best[:, :], sc, AX.X))
                ch.link(nc.vector.tensor_tensor(hit[:, :, :], sc, best[:, :].unsqueeze(2).broadcast_to(wide),
                                                ALU.is_equal))
                ch.link(nc.vector.tensor_tensor(hit[:, :, :], hit[:, :, :], rank, ALU.mult))
                ch.link(nc.vector.reduce_max(code[:, :], hit[:, :, :], AX.X))
                ch.link(nc.vector.tensor_scalar(code[:, :], code[:, :], 1.0, None, ALU.max))
                part = chosen[:, bass.ds(i * PT * E, PT * E)].rearrange("p (g j e) -> p j g e", j=NJ, e=E)
                for j in range(NJ):
                    ins = nc.vector.tensor_tensor(part[:, j], w["rank"][:, :].unsqueeze(1).broadcast_to([P, NG, E]),
                                                  code[:, j * NG:(j + 1) * NG].unsqueeze(2).broadcast_to([P, NG, E]),
                                                  ALU.is_equal)
                ins.then_inc(chosen_ready, 1)

            if experts is None:
                with dve.Fori(0, PARTS) as i:
                    part_of(i)
            else:
                part_of(0, fold=True)
                with dve.Fori(1, PARTS) as i:
                    part_of(i)
            dve.wait_ge(chosen_ready, PARTS + 1)


def routing_stage(nc, tag, w, chosen, index, expert_at, experts=None):
    with ExitStack() as ctx:
        sb = lambda name, shape, dt=F32: ctx.enter_context(nc.sbuf_tensor(f"{tag}_{name}", shape, dt))
        sems = []
        sem = lambda name: sems.append(ctx.enter_context(nc.semaphore(f"{tag}_{name}"))) or sems[-1]
        T = TILES
        NU = 4
        in_tile = sb("in_tile", [P, E], F16)
        earlier = sb("earlier", [P, T, E], F16)
        where = sb("where", [P, T, E])
        slot, tile_of, row_of = sb("slot", [P, T]), sb("tile_of", [P, T]), sb("row_of", [P, T])
        ints = sb("ints", [P, T], I32)
        ints2 = sb("ints2", [P, T], I32)
        pad_i = sb("pad_i", [P, E], I32)
        padded = sb("padded", [P, E])
        ends = [sb(f"ends{i}", [P, E]) for i in range(2)]
        base = sb("base", [P, E])
        at_row = [sb(f"at_row{u}", [P, NJ, P], F16) for u in range(NU)]
        hot_tile = [sb(f"hot_tile{u}", [P, NJ, SLOTS], F16) for u in range(NU)]
        at_tile = [sb(f"at_tile{u}", [P, 2, NJ, SLOTS], F16) for u in range(NU)]
        low, empty = sb("low", [P, SLOTS]), sb("empty", [P, SLOTS])
        past = sb("past", [1, SLOTS, E])
        past_sum = sb("past_sum", [1, SLOTS])
        ps_rank = ctx.enter_context(nc.psum_tensor(f"{tag}_rank", [P, T * E], F32))
        ps_count = ctx.enter_context(nc.psum_tensor(f"{tag}_count", [P, 2 * E], F32))
        ps_experts = [ctx.enter_context(nc.psum_tensor(f"{tag}_experts{i}", [P, 512], F32)) for i in range(4)]
        ps_index = ctx.enter_context(nc.psum_tensor(f"{tag}_index", [P, 2 * SLOTS], F32))
        counted, step, used, hot, scaled, turn = (
            sem(k) for k in ("counted", "step", "used", "hot", "scaled", "turn"))
        start_at_one(nc, sems)
        ctx.callback(back_to_zero, nc, sems)
        block = ctx.enter_context(nc.Block())
        QS = TILES // NJ

        @block.tensor
        def _(pe):
            for e in range(E):
                ins = nc.tensor.matmul(ps_count[:, e:e + 1], chosen[:, e:T * E:E], w["ones"][:, 0:1], start=True, stop=True)
            ins.then_inc(counted, 1)
            for c in range(0, T * E, 512):
                nc.tensor.matmul(ps_rank[:, c:c + 512], w["before"][:, :], chosen[:, c:c + 512], start=True, stop=False)
            pe.wait_ge(step, 1 + 1)
            nc.tensor.matmul(ps_count[:, E:2 * E], w["ones"][:, :], in_tile[:, :], start=True, stop=True).then_inc(counted, 1)
            pe.wait_ge(step, 2 + 1)
            for c in range(0, T * E, 512):
                ins = nc.tensor.matmul(ps_rank[:, c:c + 512], w["ones"][:, :],
                                       earlier[:, :, :].rearrange("p t e -> p (t e)")[:, c:c + 512],
                                       start=False, stop=True)
            ins.then_inc(counted, 1)

            if experts is not None:
                experts.transpose(pe, ps_experts)

            def place(q, u, first_=False, last_=False):
                pe.wait_ge(scaled, q + 1 + 1)
                for j in range(NJ):
                    ins = nc.tensor.matmul(ps_index[:, :].rearrange("p (a s) -> p a s", a=2), at_row[u][:, j, :],
                                           at_tile[u][:, :, j, :], start=(first_ and j == 0),
                                           stop=(last_ and j == NJ - 1))
                ins.then_inc(used, 1)

            for u in range(NU):
                place(u, u, first_=(u == 0))
            with pe.Fori(1, QS // NU - 1) as i:
                for u in range(NU):
                    place(NU * i + u, u)
            for u in range(NU):
                place(QS - NU + u, u, last_=(u == NU - 1))

        @block.scalar
        def _(act):
            def scale(q, u):
                act.wait_ge(hot, q + 1 + 1)
                act.sem_inc(turn, 1)
                for j in range(NJ - 1):
                    nc.scalar.activation(at_tile[u][:, 0, j, :], hot_tile[u][:, j, :], ACT.Identity,
                                         scale=w["low"][:, j:j + 1])
                nc.scalar.activation(at_tile[u][:, 1, :, :], hot_tile[u][:, :, :], ACT.Identity,
                                     scale=w["high"][:, bass.ds(q, 1)]).then_inc(scaled, 1)

            if experts is not None:
                experts.place(act, ps_experts)
            with act.Fori(0, QS // NU) as i:
                for u in range(NU):
                    scale(NU * i + u, u)

        @block.vector
        def _(dve):
            ch = Chain(dve, step, 0)
            V = nc.vector
            dve.wait_ge(counted, 1 + 1)
            ch.link(V.tensor_copy(in_tile[:, :], ps_count[:, 0:E]))
            ch.link(V.tensor_tensor(earlier[:, :, :], w["before"][:, :].unsqueeze(2).broadcast_to([P, T, E]),
                                    in_tile[:, :].unsqueeze(1).broadcast_to([P, T, E]), ALU.mult))
            dve.wait_ge(counted, 2 + 1)
            ch.link(V.tensor_scalar(pad_i[:, :], ps_count[:, E:2 * E], float(P - 1), None, ALU.add))
            ch.link(V.tensor_scalar(pad_i[:, :], pad_i[:, :], 7, 7, ALU.logical_shift_right, ALU.logical_shift_left))
            ch.link(V.tensor_copy(padded[:, :], pad_i[:, :]))
            ch.link(V.tensor_copy(ends[0][:, :], padded[:, :]))
            esrc, edst = ends
            d = 1
            while d < E:
                V.tensor_copy(edst[:, 0:d], esrc[:, 0:d])
                ch.link(V.tensor_tensor(edst[:, d:E], esrc[:, d:E], esrc[:, 0:E - d], ALU.add))
                esrc, edst, d = edst, esrc, 2 * d
            ch.link(V.tensor_tensor(base[:, :], esrc[:, :], padded[:, :], ALU.subtract))
            dve.wait_ge(counted, 3 + 1)
            ch.link(V.tensor_tensor(where[:, :, :], ps_rank[:, :].rearrange("p (t e) -> p t e", e=E),
                                    base[:, :].unsqueeze(1).broadcast_to([P, T, E]), ALU.add))
            ch.link(V.tensor_tensor(where[:, :, :], where[:, :, :], chosen[:, :].rearrange("p (t e) -> p t e", e=E),
                                    ALU.mult))
            ch.link(V.reduce_sum(slot[:, :], where[:, :, :], AX.X))
            ch.link(V.tensor_copy(ints[:, :], slot[:, :]))
            ch.link(V.tensor_scalar(ints2[:, :], ints[:, :], 7, None, ALU.logical_shift_right))
            V.tensor_copy(tile_of[:, :], ints2[:, :])
            ch.link(V.tensor_scalar(ints[:, :], ints[:, :], P - 1, None, ALU.bitwise_and))
            ch.link(V.tensor_copy(row_of[:, :], ints[:, :]))
            def one_hots(q, u):
                for j in range(NJ):
                    at = bass.ds(NJ * q + j, 1)
                    V.tensor_scalar(at_row[u][:, j, :], w["iota"][:, 0:P], row_of[:, at], None, ALU.is_equal)
                    V.tensor_scalar(hot_tile[u][:, j, :], w["iota"][:, :], tile_of[:, at], None, ALU.is_equal)
                V.tensor_scalar(at_tile[u][:, 0, NJ - 1, :], w["iota"][:, :], tile_of[:, at], w["low"][:, NJ - 1:NJ],
                                ALU.is_equal, ALU.mult).then_inc(hot, 1)

            for u in range(NU):
                one_hots(u, u)
            with dve.Fori(1, QS // NU) as i:
                for u in range(NU):
                    dve.wait_ge(used, NU * (i - 1) + u + 1 + 1)
                    one_hots(NU * i + u, u)
            ch.link(V.tensor_scalar(base[:, :], esrc[:, :], 1.0 / P, None, ALU.mult))
            ch.link(V.tensor_tensor(past[:, :, :], w["iota"][0:1, :].unsqueeze(2).broadcast_to([1, SLOTS, E]),
                                    base[0:1, :].unsqueeze(1).broadcast_to([1, SLOTS, E]), ALU.is_ge))
            ch.link(V.reduce_sum(past_sum[:, :], past[:, :, :], AX.X))
            ch.link(V.tensor_scalar(expert_at[:, :], past_sum[:, :], float(E - 1), float(D), ALU.min, ALU.mult))
            dve.wait_ge(used, QS + 1)
            ch.link(V.tensor_copy(low[:, :], ps_index[:, 0:SLOTS]))
            V.tensor_scalar(empty[:, :], low[:, :], 0.0, float(BIG), ALU.is_equal, ALU.mult)
            ch.link(V.scalar_tensor_tensor(out=low[:, :], in0=ps_index[:, SLOTS:2 * SLOTS], scalar=512.0,
                                           in1=low[:, :], op0=ALU.mult, op1=ALU.add))
            ch.link(V.scalar_tensor_tensor(out=index[:, :], in0=low[:, :], scalar=-1.0, in1=empty[:, :],
                                           op0=ALU.add, op1=ALU.add))


def expert_stage(nc, tag, w, sw_sems, calls_before, index, expert_at, src, dst):
    with ExitStack() as ctx:
        sb = lambda name, shape, dt=F32: ctx.enter_context(nc.sbuf_tensor(f"{tag}_{name}", shape, dt))
        sems = []
        sem = lambda name: sems.append(ctx.enter_context(nc.semaphore(f"{tag}_{name}"))) or sems[-1]
        NB, AHEAD, GT = EXPERT_BUFFERS, 14, 4
        ROUNDS = SLOTS // NB
        TAIL = SLOTS - NB * ROUNDS
        GR = NB // GT
        x = [sb(f"x{k}", [P, D]) for k in range(NB)]
        y = [sb(f"y{k}", [P, D]) for k in range(NB)]
        xT = [sb(f"xT{k}", [P, 2, KB, P]) for k in range(4)]
        gather_at = [sb(f"gather_at{k}", [P, 1], I32) for k in range(NB)]
        scatter_at = [sb(f"scatter_at{k}", [P, 1], I32) for k in range(NB)]
        stats, mv = sb("stats", [P, GT, 6]), sb("mv", [P, GT, 2])
        var, root, r0, tmp = (sb(k, [P, GT]) for k in ("var", "root", "r0", "tmp"))
        rstd = [sb(f"rstd{k}", [P, GT]) for k in range(2)]
        psT = [ctx.enter_context(nc.psum_tensor(f"{tag}_psT{k}", [P, 512], F32)) for k in range(4)]
        psY = [ctx.enter_context(nc.psum_tensor(f"{tag}_psY{k}", [P, 512], F32)) for k in range(4)]
        gathered, scattered = sw_sems[0:NB], sw_sems[NB:2 * NB]
        before = [calls_before * 16 * (ROUNDS + (k < TAIL)) for k in range(NB)]
        cleared, gather_at_ready, scatter_at_ready, var_ready, root_ready = (
            sem(k) for k in ("cleared", "gather_at_ready", "scatter_at_ready", "var_ready", "root_ready"))
        xT_in_psum, xT_ready, product_ready, y_ready, ln_step, turn = (
            sem(k) for k in ("xT_in_psum", "xT_ready", "product_ready", "y_ready", "ln_step", "turn"))
        start_at_one(nc, sems)
        ctx.callback(back_to_zero, nc, sems)
        block = ctx.enter_context(nc.Block())
        is_first = lambda i: isinstance(i, int) and i == 0
        exists = lambda i, k: not isinstance(i, int) or NB * i + k < SLOTS

        @block.gpsimd
        def _(pool):
            def gather(i, k):
                pool.wait_ge(gather_at_ready, NB * i + k + 1 + 1)
                pool.sem_inc(turn, 1)
                pool.indirect_dma_start(out=x[k][:, :], out_offset=None, in_=src,
                                        in_offset=bass.IndirectOffsetOnAxis(ap=gather_at[k][:, 0:1], axis=0),
                                        bounds_check=B * L - 1, oob_is_err=False).then_inc(gathered[k], 16)

            def scatter(i, k):
                pool.wait_ge(y_ready, NB * i + k + 1 + 1)
                pool.sem_inc(turn, 1)
                pool.wait_ge(scatter_at_ready, NB * i + k + 1 + 1)
                pool.sem_inc(turn, 1)
                pool.indirect_dma_start(out=dst, out_offset=bass.IndirectOffsetOnAxis(ap=scatter_at[k][:, 0:1], axis=0),
                                        in_=y[k][:, :], in_offset=None,
                                        bounds_check=B * L - 1, oob_is_err=False).then_inc(scattered[k], 16)

            def round_(i, tiles=NB, last=False):
                for k in range(tiles):
                    a = k + AHEAD
                    if a < NB:
                        if exists(i, a):
                            gather(i, a)
                    elif not last and exists(i + 1, a - NB):
                        gather(i + 1, a - NB)
                    scatter(i, k)

            for k in range(AHEAD):
                pool.wait_ge(cleared, k + 1 + 1)
                gather(0, k)
            pool.wait_ge(cleared, NB + 1)
            with pool.Fori(0, ROUNDS - 1) as i:
                round_(i)
            round_(ROUNDS - 1)
            round_(ROUNDS, TAIL, last=True)
            for k in range(NB):
                pool.wait_ge(scattered[k], before[k] + 16 * (ROUNDS + (k < TAIL)))

        @block.scalar
        def _(act):
            def place_gather(i, k):
                if not is_first(i):
                    act.wait_ge(gathered[k], before[k] + 16 * i)
                    act.sem_inc(turn, 1)
                nc.scalar.copy(gather_at[k][:, :], index[:, bass.ds(NB * i + k, 1)]).then_inc(gather_at_ready, 1)

            def place_scatter(i, k):
                if not is_first(i):
                    act.wait_ge(scattered[k], before[k] + 16 * i)
                    act.sem_inc(turn, 1)
                nc.scalar.copy(scatter_at[k][:, :], index[:, bass.ds(NB * i + k, 1)]).then_inc(scatter_at_ready, 1)

            def transposed(i, h):
                act.wait_ge(xT_in_psum, NB // 2 * i + h + 1 + 1)
                nc.scalar.copy(xT[h % 4][:, :, :, :].rearrange("p a k q -> p (a k q)"),
                               psT[h % 4][:, :]).then_inc(xT_ready, 1)

            def group_root(i, g):
                act.wait_ge(var_ready, GR * i + g + 1 + 1)
                nc.scalar.activation(root[:, :], var[:, :], ACT.Sqrt).then_inc(root_ready, 1)

            def round_(i, tiles=NB, last=False):
                for g in range(tiles // GT):
                    for k in range(GT * g, GT * (g + 1)):
                        a = k + AHEAD
                        if a < NB:
                            if exists(i, a):
                                place_gather(i, a)
                        elif not last and exists(i + 1, a - NB):
                            place_gather(i + 1, a - NB)
                        place_scatter(i, k)
                        if k % 2:
                            transposed(i, k // 2)
                            if k % GT == GT - 1:
                                if g + 1 < tiles // GT:
                                    group_root(i, g + 1)
                                elif not last:
                                    group_root(i + 1, 0)

            for k in range(AHEAD):
                place_gather(0, k)
            group_root(0, 0)
            round_(0)
            with act.Fori(1, ROUNDS - 1) as i:
                round_(i)
            round_(ROUNDS - 1)
            round_(ROUNDS, TAIL, last=True)

        @block.vector
        def _(dve):
            STEPS = 2 + 1 + 5

            def finish(i, k):
                dve.wait_ge(product_ready, NB * i + k + 1 + 1)
                if not is_first(i):
                    dve.wait_ge(scattered[k], before[k] + 16 * i)
                nc.vector.scalar_tensor_tensor(out=y[k][:, :], in0=psY[k % 4][:, 0:D],
                                               scalar=rstd[k // GT % 2][:, k % GT:k % GT + 1], in1=x[k][:, :],
                                               op0=ALU.mult, op1=ALU.add).then_inc(y_ready, 1)

            def group(i, g, fi=None, fg=None):
                at = GR * i + g
                r = rstd[g % 2][:, :]
                step = STEPS * at + 1
                done = [0]

                def finish_next():
                    if fi is not None and done[0] < GT:
                        finish(fi, GT * fg + done[0])
                        done[0] += 1

                for c in range(GT):
                    dve.wait_ge(gathered[GT * g + c], before[GT * g + c] + 16 * (i + 1))
                    ins = nc.vector.bn_stats(stats[:, c, :], x[GT * g + c][:, :])
                ins.then_inc(ln_step, 1)
                finish_next()
                dve.wait_ge(ln_step, step + 1)
                dve.sem_inc(turn, 1)
                for c in range(GT):
                    ins = nc.vector.bn_aggr(mv[:, c, :], stats[:, c, :])
                ins.then_inc(ln_step, 1)
                finish_next()
                dve.wait_ge(ln_step, step + 2)
                nc.vector.tensor_scalar(var[:, :], mv[:, :, 1], EPS, None, ALU.add).then_inc(var_ready, 1)
                finish_next()
                dve.wait_ge(root_ready, at + 1 + 1)
                nc.vector.reciprocal(r0[:, :], root[:, :]).then_inc(ln_step, 1)
                finish_next()
                dve.wait_ge(ln_step, step + 3)
                nc.vector.tensor_tensor(tmp[:, :], r0[:, :], r0[:, :], ALU.mult).then_inc(ln_step, 1)
                dve.wait_ge(ln_step, step + 4)
                nc.vector.tensor_tensor(tmp[:, :], tmp[:, :], var[:, :], ALU.mult).then_inc(ln_step, 1)
                dve.wait_ge(ln_step, step + 5)
                nc.vector.tensor_scalar(tmp[:, :], tmp[:, :], -0.5, 1.5, ALU.mult, ALU.add).then_inc(ln_step, 1)
                dve.wait_ge(ln_step, step + 6)
                nc.vector.tensor_tensor(r, r0[:, :], tmp[:, :], ALU.mult).then_inc(ln_step, 1)
                dve.wait_ge(ln_step, step + 7)
                dve.sem_inc(ln_step, 1)

            def round_(i, tiles=NB, last=False):
                n = tiles // GT
                for g in range(n):
                    if g + 1 < n:
                        group(i, g + 1, i, g)
                    elif not last:
                        group(i + 1, 0, i, g)
                    else:
                        for c in range(GT):
                            finish(i, GT * g + c)

            for k in range(NB):
                nc.vector.memset(x[k][:, :], 0.0).then_inc(cleared, 1)
            group(0, 0)
            round_(0)
            with dve.Fori(1, ROUNDS - 1) as i:
                round_(i)
            round_(ROUNDS - 1)
            round_(ROUNDS, TAIL, last=True)

        @block.tensor
        def _(pe):
            def transpose(i, h):
                for c in range(2):
                    pe.wait_ge(gathered[2 * h + c], before[2 * h + c] + 16 * (i + 1))
                    for k in range(KB):
                        ins = nc.tensor.transpose(psT[h % 4][:, (2 * c + k) * P:(2 * c + k + 1) * P],
                                                  x[2 * h + c][:, k * P:(k + 1) * P], w["ident"][:, :])
                ins.then_inc(xT_in_psum, 1)

            def product(i, h):
                pe.wait_ge(xT_ready, NB // 2 * i + h + 1 + 1)
                if not (is_first(i) and h < 2):
                    pe.wait_ge(y_ready, NB * i + 2 * h - 2 + 1)
                for c in range(2):
                    s = NB * i + 2 * h + c
                    col = pe.value_load(expert_at[0:1, bass.ds(s, 1)], min_val=0, max_val=(E - 1) * D)
                    for k in range(KB):
                        ins = nc.tensor.matmul(psY[(2 * h + c) % 4][:, 0:D], xT[h % 4][:, c, k, :],
                                               w["expert"][:, k, bass.ds(col, D)], start=(k == 0), stop=(k == KB - 1))
                    ins.then_inc(product_ready, 1)

            def round_(i, tiles=NB, last=False):
                n = tiles // 2
                for h in range(n):
                    if h + 1 < n:
                        transpose(i, h + 1)
                    elif not last:
                        transpose(i + 1, 0)
                    product(i, h)

            transpose(0, 0)
            round_(0)
            with pe.Fori(1, ROUNDS - 1) as i:
                round_(i)
            round_(ROUNDS - 1)
            round_(ROUNDS, TAIL, last=True)


def routed_experts(nc, tag, w, sw_sems, calls_before, src, dst, experts=None):
    with ExitStack() as ctx:
        index = ctx.enter_context(nc.sbuf_tensor(f"{tag}_index_of_slots", [P, SLOTS], I32))
        expert_at = ctx.enter_context(nc.sbuf_tensor(f"{tag}_expert_of_tile", [1, SLOTS], I32))
        chosen = ctx.enter_context(nc.sbuf_tensor(f"{tag}_chosen", [P, TILES * E], F16))
        score_stage(nc, tag + "s", w, src, chosen, experts)
        routing_stage(nc, tag + "r", w, chosen, index, expert_at, experts)
        expert_stage(nc, tag + "e", w, sw_sems, calls_before, index, expert_at, src, dst)


def spectra_stage(nc, w, cst, args, src, es, means, vspec):
    with ExitStack() as ctx:
        sb = lambda name, shape: ctx.enter_context(nc.sbuf_tensor(f"sp_{name}", shape, F32))
        sems = []
        sem = lambda name: sems.append(ctx.enter_context(nc.semaphore(f"sp_{name}"))) or sems[-1]
        HF = NF - 1
        x = [sb(f"x{u}", [P, 2 * NJ, D]) for u in range(2)]
        sd = sb("sd", [P, 2, NJ * D])
        stats = sb("stats", [P, 2 * NJ, 6])
        mv = sb("mv", [P, 2 * NJ, 2])
        var, root, rstd, tmp, shift = (sb(k, [P, 2 * NJ]) for k in ("var", "root", "rstd", "tmp", "shift"))
        even = sb("even", [P, KB, 512])
        X = sb("X", [P, KB, L + 4])
        XN = sb("XN", [P, KB, B])
        q = sb("q", [P, KB, L])
        sq = sb("sq", [P, KB, L])
        qk = sb("qk", [P, KB, HF])
        pair = lambda name, shape: tuple(
            ctx.enter_context(nc.sbuf_tensor(f"sp_{name}_{part}", shape, F32R)) for part in ("high", "low"))
        mag_s, qk_s = pair("mag", [P, KB, HF]), pair("qk", [P, KB, HF])
        sd_s, fwd_s = pair("sd", [P, 2, NJ * D]), pair("fwd", [P, 2 * NJ * 256])
        ind_r = ctx.enter_context(nc.sbuf_tensor("sp_ind_r", [P, KB * H], F32R))
        acc = sb("acc", [P, 2, KB])
        esb = [sb(f"es{u}", [H, 2, HF]) for u in range(2)]
        qn, magn, qkn = (sb(k, [P, KB, B]) for k in ("qn", "magn", "qkn"))
        esn = sb("esn", [H, 2, B])
        ps = [ctx.enter_context(nc.psum_tensor(f"sp_ps{i}", [P, 512], F32)) for i in range(8)]
        fwd = sd[:, :, :].rearrange("p k c -> p (k c)")
        W = {k: sb(k, [P, KB, D]) for k in ("Wq", "Wk", "Wv")}
        x_in = [sem(f"x_in{u}") for u in range(2)]
        es_out = [sem(f"es_out{u}") for u in range(2)]
        names = ("tables_in fwd_in fwd_split ind_ready var_ready root_ready shift_ready half_ready n_ready sd_high "
                 "sd_split dft_ready even_ready X_ready proj_ready q_ready v_ready k_used sq_ready mag_in mag_ready "
                 "mag_split qk_ready qk_high qk_split sums_ready es_ready ln_step nyq_ready nyq_step turn").split()
        S = {k: sem(k) for k in names}
        turn = S["turn"]
        start_at_one(nc, sems)
        ctx.callback(back_to_zero, nc, sems)
        block = ctx.enter_context(nc.Block())
        PAIRS = B // 2
        seq = src.rearrange("(b h p j) c -> b p h (j c)", b=B, h=2, j=NJ)
        es3 = es.rearrange("r (c n) -> r c n", c=2)

        @block.sync
        def _(sp):
            def load(i, u):
                sp.dma_start(x[u][:, :, :].rearrange("p (h j) c -> p h (j c)", h=2),
                             seq[bass.ds(2 * i + u, 1), :, :, :].rearrange("a p h c -> (a p) h c")).then_inc(x_in[u], 16)

            def store(i, u):
                b = 2 * i + u
                sp.wait_ge(S["es_ready"], 2 * (b + 1) + 1)
                sp.sem_inc(turn, 1)
                sp.dma_start(es3[bass.ds(b * H, H), :, 0:HF], esb[u][:, :, :]).then_inc(es_out[u], 16)

            sp.dma_start(fwd, cst["fwd"]).then_inc(S["fwd_in"], 16)
            load(0, 0)
            for k in ("Wq", "Wk", "Wv"):
                sp.dma_start(W[k][:, :, :], args["L0_attn_" + k].rearrange("(k p) n -> p k n", p=P)).then_inc(S["tables_in"], 16)
            load(0, 1)
            with sp.Fori(0, PAIRS - 1) as i:
                for u in range(2):
                    sp.wait_ge(S["n_ready"], 2 * (2 * i + u + 1) + 1)
                    sp.sem_inc(turn, 1)
                    load(i + 1, u)
                    store(i, u)
            for u in range(2):
                store(PAIRS - 1, u)
            sp.wait_ge(S["nyq_ready"], 3 + 1)
            with nc.allow_non_contiguous_dma(reason="one frequency of every row, once"):
                for c in range(2):
                    sp.dma_start(es.rearrange("(b h) n -> h b n", h=H)[:, :, c * NF + HF:c * NF + HF + 1],
                                 esn[:, c, :].unsqueeze(2)).then_inc(es_out[c], 16)
            for u in range(2):
                sp.wait_ge(es_out[u], 16 * (PAIRS + 1) + 1)

        @block.vector
        def _(dve):
            def statistics(i, b, u):
                dve.wait_ge(x_in[u], 16 * (i + 1) + 1)
                ch = Chain(dve, S["ln_step"], b * (LN_STEPS + 1))
                layer_norm_stats(nc, ch, turn, stats, mv, x[u], 2 * NJ)
                ch.link(nc.vector.tensor_scalar(var[:, :], mv[:, :, 1], EPS, None, ALU.add))
                dve.sem_inc(S["var_ready"], 1)
                return ch

            def normalise(ch, b, u):
                dve.wait_ge(S["root_ready"], b + 1 + 1)
                rsqrt_refine(nc, ch, var[:, :], root[:, :], rstd[:, :], tmp[:, :])
                nc.vector.scalar_tensor_tensor(out=shift[:, :], in0=mv[:, :, 0], scalar=-1.0, in1=rstd[:, :],
                                               op0=ALU.mult, op1=ALU.mult).then_inc(S["shift_ready"], 1)
                for r in range(NJ):
                    ins = nc.vector.tensor_scalar(x[u][:, r, :], x[u][:, r, :],
                                                  mv[:, r, 0:1], rstd[:, r:r + 1], ALU.subtract, ALU.mult)
                ch.link(ins)

            def halves(b, u):
                dve.wait_ge(S["half_ready"], b + 1 + 1)
                n = x[u][:, :, :].rearrange("p (h j) c -> p h (j c)", h=2)
                nc.vector.tensor_tensor(sd[:, 0, :], n[:, 0, :], n[:, 1, :], ALU.add).then_inc(S["n_ready"], 1)
                nc.vector.tensor_tensor(sd[:, 1, :], n[:, 0, :], n[:, 1, :], ALU.subtract).then_inc(S["n_ready"], 1)

            def sd_low(b):
                for kind in range(2):
                    dve.wait_ge(S["sd_high"], 2 * b + kind + 1 + 1)
                    ins = nc.vector.tensor_tensor(sd_s[1][:, kind, :], sd[:, kind, :], sd_s[0][:, kind, :], ALU.subtract)
                ins.then_inc(S["sd_split"], 1)

            def combine(b):
                for k in range(KB):
                    dve.wait_ge(S["even_ready"], KB * b + k + 1 + 1)
                    dve.wait_ge(S["dft_ready"], 4 * b + 2 * k + 2 + 1)
                    ev = even[:, k, :].rearrange("p (d c g) -> p c g d", d=2, c=2)
                    od = ps[2 * k + 1][:, :].rearrange("p (d c g) -> p c g d", d=2, c=2)
                    view = lambda lo, hi, step: X[:, k, lo:hi:step].rearrange("p (g d) -> p g d", d=2)
                    nc.vector.tensor_tensor(view(0, 256, 1), ev[:, 0], od[:, 0], ALU.add)
                    nc.vector.tensor_tensor(view(512, 256, -1), ev[:, 0], od[:, 0], ALU.subtract)
                    nc.vector.tensor_tensor(view(514, 770, 1), ev[:, 1], od[:, 1], ALU.add)
                    nc.vector.tensor_tensor(view(1026, 770, -1), od[:, 1], ev[:, 1], ALU.subtract)
                    nc.vector.tensor_tensor(XN[:, k, bass.ds(b, 1)], even[:, k, 0:1], ps[2 * k + 1][:, 0:1],
                                            ALU.subtract)
                    nc.vector.tensor_copy(X[:, k, 256:257], even[:, k, 128:129])
                    nc.vector.tensor_copy(X[:, k, 770:771], ps[2 * k + 1][:, 128:129]).then_inc(S["X_ready"], 1)

            def scores(b, m):
                dve.wait_ge(S["proj_ready"], 8 * b + 4 * m + 3 + 1)
                dve.wait_ge(S["q_ready"], KB * b + m + 1 + 1)
                nc.vector.scalar_tensor_tensor(out=qk[:, m, 0:1], in0=ps[6][:, 0:1], scalar=w["bias"][:, 1, m:m + 1],
                                               in1=q[:, m, 0:1], op0=ALU.add, op1=ALU.mult)
                nc.vector.tensor_tensor(qk[:, m, 1:512], ps[6][:, 1:512], q[:, m, 1:512],
                                        ALU.mult).then_inc(S["k_used"], 1)
                nc.vector.tensor_tensor(means[:, 0, m, bass.ds(b, 1)], acc[:, 0, m:m + 1], q[:, m, 0:1], ALU.add)
                nc.vector.tensor_copy(means[:, 1, m, bass.ds(b, 1)], acc[:, 1, m:m + 1]).then_inc(S["qk_ready"], 1)

            def scores_low(b):
                for m in range(KB):
                    dve.wait_ge(S["qk_high"], KB * b + m + 1 + 1)
                    nc.vector.tensor_tensor(qk_s[1][:, m, :], qk[:, m, :], qk_s[0][:, m, :],
                                            ALU.subtract).then_inc(S["qk_split"], 1)

            def turn_of(b, following):
                combine(b)
                if following:
                    normalise(statistics(*following), *following[1:])
                scores(b, 0)
                if following:
                    halves(*following[1:])
                    sd_low(following[1])
                scores(b, 1)
                scores_low(b)

            dve.wait_ge(S["fwd_split"], 1 + 1)
            nc.vector.tensor_tensor(fwd_s[1][:, :], fwd, fwd_s[0][:, :], ALU.subtract).then_inc(S["fwd_split"], 1)
            dve.wait_ge(S["fwd_split"], 2 + 1)
            ch0 = statistics(0, 0, 0)
            normalise(ch0, 0, 0)
            halves(0, 0)
            sd_low(0)
            with dve.Fori(0, PAIRS - 1) as i:
                turn_of(2 * i, (i, 2 * i + 1, 1))
                turn_of(2 * i + 1, (i + 1, 2 * i + 2, 0))
            turn_of(B - 2, (PAIRS - 1, B - 1, 1))
            turn_of(B - 1, None)
            ch = Chain(dve, S["nyq_step"], 0)
            dve.wait_ge(S["nyq_ready"], 1 + 1)
            ch.link(nc.vector.tensor_copy(qn[:, :, :], ps[0][:, 0:KB * B].rearrange("p (m b) -> p m b", m=KB)))
            nc.vector.tensor_tensor(qkn[:, :, :], ps[0][:, KB * B:2 * KB * B].rearrange("p (m b) -> p m b", m=KB),
                                    qn[:, :, :], ALU.mult)
            nc.vector.tensor_copy(vspec[:, :, HF:B * NF:NF], ps[0][:, 2 * KB * B:3 * KB * B].rearrange("p (m b) -> p m b", m=KB))
            nc.vector.tensor_tensor(means[:, 0, :, :], means[:, 0, :, :], qn[:, :, :], ALU.add)
            ch.link(nc.vector.scalar_tensor_tensor(out=magn[:, :, :], in0=qn[:, :, :], scalar=-1.0, in1=qn[:, :, :],
                                                   op0=ALU.mult, op1=ALU.max))
            dve.wait_ge(S["nyq_ready"], 2 + 1)
            nc.vector.tensor_copy(esn[:, :, :], ps[1][0:H, 0:2 * B].rearrange("p (c b) -> p c b", c=2)).then_inc(S["nyq_ready"], 1)

        @block.scalar
        def _(act):
            def even_out(b):
                for k in range(KB):
                    act.wait_ge(S["dft_ready"], 4 * b + 2 * k + 1 + 1)
                    nc.scalar.copy(even[:, k, :], ps[2 * k][:, :]).then_inc(S["even_ready"], 1)

            def ln_root(b):
                act.wait_ge(S["var_ready"], b + 1 + 1)
                nc.scalar.activation(root[:, :], var[:, :], ACT.Sqrt).then_inc(S["root_ready"], 1)

            def normalise_half(b, u):
                act.wait_ge(S["shift_ready"], b + 1 + 1)
                for r in range(NJ, 2 * NJ):
                    ins = nc.scalar.activation(x[u][:, r, :], x[u][:, r, :], ACT.Identity, bias=shift[:, r:r + 1],
                                               scale=rstd[:, r:r + 1])
                ins.then_inc(S["half_ready"], 1)

            def sd_high(b):
                for kind in range(2):
                    act.wait_ge(S["n_ready"], 2 * b + kind + 1 + 1)
                    nc.scalar.copy(sd_s[0][:, kind, :], sd[:, kind, :]).then_inc(S["sd_high"], 1)

            def project_out(b, following, u=None):
                act.wait_ge(S["qk_ready"], KB * b + 1)
                act.wait_ge(S["sq_ready"], KB * b + 1)
                if following is not None:
                    ln_root(following)
                for m in range(KB):
                    act.wait_ge(S["proj_ready"], 8 * b + 4 * m + 1 + 1)
                    nc.scalar.activation(q[:, m, 0:1], ps[4][:, 0:1], ACT.Identity, bias=w["bias"][:, 0, m:m + 1])
                    nc.scalar.activation(q[:, m, 1:512], ps[4][:, 1:512], ACT.Identity, accum_out=acc[:, 0, m:m + 1])
                    act.wait_ge(S["proj_ready"], 8 * b + 4 * m + 2 + 1)
                    nc.scalar.activation(q[:, m, 513:1024], ps[5][:, 1:512], ACT.Identity,
                                         accum_out=acc[:, 1, m:m + 1]).then_inc(S["q_ready"], 1)
                    if m == 0 and following is not None:
                        normalise_half(following, u)
                    act.wait_ge(S["proj_ready"], 8 * b + 4 * m + 4 + 1)
                    nc.scalar.activation(vspec[:, m, bass.ds(b * NF, 1)], ps[7][:, 0:1], ACT.Identity,
                                         bias=w["bias"][:, 2, m:m + 1])
                    nc.scalar.copy(vspec[:, m, bass.ds(b * NF + 1, 511)], ps[7][:, 1:512]).then_inc(S["v_ready"], 1)
                    if m == 0 and following is not None:
                        sd_high(following)
                for m in range(KB):
                    if m == 0:
                        act.wait_ge(S["sums_ready"], 2 * b + 1)
                        act.wait_ge(S["mag_split"], KB * b + 1)
                    act.wait_ge(S["qk_ready"], KB * b + m + 1 + 1)
                    nc.scalar.copy(qk_s[0][:, m, :], qk[:, m, :]).then_inc(S["qk_high"], 1)
                    act.wait_ge(S["mag_in"], KB * b + m + 1 + 1)
                    nc.scalar.activation(sq[:, m, HF:L], sq[:, m, 0:512], ACT.Sqrt)
                    nc.scalar.activation(mag_s[0][:, m, :], sq[:, m, 0:512], ACT.Sqrt).then_inc(S["mag_ready"], 1)

            def sums_out(b, i, u):
                act.wait_ge(es_out[u], 16 * i + 1)
                for r in range(2):
                    act.wait_ge(S["sums_ready"], 2 * b + r + 1 + 1)
                    nc.scalar.copy(esb[u][:, r, :], ps[5 + r][0:H, :]).then_inc(S["es_ready"], 1)

            nc.scalar.copy(ind_r[:, :], w["ind"][:, :]).then_inc(S["ind_ready"], 1)
            act.wait_ge(S["fwd_in"], 16 + 1)
            nc.scalar.copy(fwd_s[0][:, :], fwd).then_inc(S["fwd_split"], 1)
            ln_root(0)
            normalise_half(0, 0)
            sd_high(0)
            even_out(0)
            with act.Fori(0, PAIRS - 1) as i:
                for u in range(2):
                    b = 2 * i + u
                    project_out(b, b + 1, 1 - u)
                    even_out(b + 1)
                    sums_out(b, i, u)
            project_out(B - 2, B - 1, 1)
            even_out(B - 1)
            sums_out(B - 2, PAIRS - 1, 0)
            project_out(B - 1, None)
            sums_out(B - 1, PAIRS - 1, 1)

        @block.gpsimd
        def _(pool):
            def squares(b):
                for m in range(KB):
                    if m == 0:
                        pool.wait_ge(S["mag_ready"], KB * b + 1)
                    pool.wait_ge(S["q_ready"], KB * b + m + 1 + 1)
                    nc.gpsimd.tensor_tensor(sq[:, m, 0:512], q[:, m, 0:512], q[:, m, 0:512], ALU.mult)
                    nc.gpsimd.tensor_tensor(sq[:, m, 513:1024], q[:, m, 513:1024], q[:, m, 513:1024],
                                            ALU.mult).then_inc(S["sq_ready"], 1)
                    pool.wait_ge(S["sq_ready"], KB * b + m + 1 + 1)
                    nc.gpsimd.tensor_tensor(sq[:, m, 1:512], sq[:, m, 1:512], sq[:, m, 513:1024],
                                            ALU.add).then_inc(S["mag_in"], 1)
                for m in range(KB):
                    pool.wait_ge(S["mag_ready"], KB * b + m + 1 + 1)
                    nc.gpsimd.tensor_tensor(mag_s[1][:, m, :], sq[:, m, HF:L], mag_s[0][:, m, :],
                                            ALU.subtract).then_inc(S["mag_split"], 1)

            with pool.Fori(0, B) as b:
                squares(b)

        @block.tensor
        def _(pe):
            def dft(b, u):
                pe.wait_ge(S["sd_split"], b + 1 + 1)
                pe.wait_ge(S["X_ready"], KB * b + 1)
                for k in range(KB):
                    for odd in range(2):
                        for kind in range(2):
                            for c, j in enumerate((odd, odd + 2)):
                                at = (kind * NJ + j) * 256
                                ins = split_product(nc, ps[2 * k + odd][:, kind * 256:(kind + 1) * 256],
                                                    [v[:, kind, j * D + k * P:j * D + (k + 1) * P] for v in sd_s],
                                                    [v[:, at:at + 256] for v in fwd_s], c == 0, c == 1)
                        ins.then_inc(S["dft_ready"], 1)

            def project(b):
                parts = (("Wq", 0, 4), ("Wq", 514, 5), ("Wk", 0, 6), ("Wv", 0, 7))
                for m in range(KB):
                    if m == 0:
                        order = [(r, 0) for r in (0, 3, 1, 2)] + [(r, 1) for r in range(4)]
                    else:
                        order = [(r, k) for r in range(4) for k in range(KB)]
                    for r, k in order:
                        wt, lo, bank = parts[r]
                        if m == 0 and k == 0 and r == 1:
                            pe.wait_ge(S["es_ready"], 2 * b + 1)
                        if k == 0 and r < 2:
                            pe.wait_ge(S["q_ready"], KB * b + m + 1)
                        if k == 0 and r == 2:
                            pe.wait_ge(S["k_used"], KB * b + m + 1)
                        if k == 0 and r == 3:
                            pe.wait_ge(S["v_ready"], KB * b + m + 1)
                        if m == 0 and r == 0:
                            pe.wait_ge(S["X_ready"], KB * b + k + 1 + 1)
                        ins = nc.tensor.matmul(ps[bank][:, :], W[wt][:, k, m * P:(m + 1) * P], X[:, k, lo:lo + 512],
                                               start=(k == 0), stop=(k == KB - 1))
                        if k == KB - 1:
                            ins.then_inc(S["proj_ready"], 1)

            def sums(b):
                pe.wait_ge(S["qk_ready"], KB * (b + 1) + 1)
                for out, val, ready in ((ps[5], mag_s, "mag_split"), (ps[6], qk_s, "qk_split")):
                    for m in range(KB):
                        pe.wait_ge(S[ready], KB * b + m + 1 + 1)
                        for part in range(2):
                            ins = nc.tensor.matmul(out[0:H, :], ind_r[:, m * H:(m + 1) * H], val[part][:, m, :],
                                                   start=(m == 0 and part == 0), stop=(m == KB - 1 and part == 1))
                    ins.then_inc(S["sums_ready"], 1)

            pe.wait_ge(S["tables_in"], 16 * 3 + 1)
            pe.wait_ge(S["ind_ready"], 1 + 1)
            pe.wait_ge(S["fwd_split"], 2 + 1)
            dft(0, 0)
            with pe.Fori(0, PAIRS - 1) as i:
                for u in range(2):
                    project(2 * i + u)
                    dft(2 * i + u + 1, 1 - u)
                    sums(2 * i + u)
            project(B - 2)
            dft(B - 1, 1)
            sums(B - 2)
            project(B - 1)
            sums(B - 1)
            for c, wt in enumerate(("Wq", "Wk", "Wv")):
                for m in range(KB):
                    at = (c * KB + m) * B
                    for k in range(KB):
                        ins = nc.tensor.matmul(ps[0][:, at:at + B], W[wt][:, k, m * P:(m + 1) * P], XN[:, k, :],
                                               start=(k == 0), stop=(k == KB - 1))
            ins.then_inc(S["nyq_ready"], 1)
            pe.wait_ge(S["nyq_step"], 2 + 1)
            for c, val in enumerate((magn, qkn)):
                for m in range(KB):
                    ins = nc.tensor.matmul(ps[1][0:H, c * B:(c + 1) * B], w["ind"][:, m * H:(m + 1) * H], val[:, m, :],
                                           start=(m == 0), stop=(m == KB - 1))
            ins.then_inc(S["nyq_ready"], 1)


def selection_stage(nc, es, attn, outside):
    with ExitStack() as ctx:
        sb = lambda name, shape: ctx.enter_context(nc.sbuf_tensor(f"sel_{name}", shape, F32))
        sems = []
        sem = lambda name: sems.append(ctx.enter_context(nc.semaphore(f"sel_{name}"))) or sems[-1]
        G = B * H // P
        row = [sb(f"row{g}", [P, 2 * NF]) for g in range(G)]
        top = [sb(f"top{g}", [P, 8]) for g in range(G)]
        outs = [sb(f"outside{g}", [P, NF]) for g in range(G)]
        prob = [sb(f"prob{g}", [P, NF]) for g in range(G)]
        col = [sb(f"col{g}", [P, 4]) for g in range(G)]
        row_in = [sem(f"row_in{g}") for g in range(G)]
        step, max_ready, exp_ready, out_ready, stored = (sem(k) for k in ("step", "max_ready", "exp_ready", "out_ready", "stored"))
        turn = sem("turn")
        start_at_one(nc, sems)
        ctx.callback(back_to_zero, nc, sems)
        block = ctx.enter_context(nc.Block())

        @block.sync
        def _(sp):
            for g in range(G):
                sp.dma_start(row[g][:, :], es[g * P:(g + 1) * P, :]).then_inc(row_in[g], 16)
            for g in range(G):
                sp.wait_ge(out_ready, g + 1 + 1)
                sp.sem_inc(turn, 1)
                sp.dma_start(attn[g * P:(g + 1) * P, :], prob[g][:, :]).then_inc(stored, 16)
                sp.dma_start(outside[g * P:(g + 1) * P, :], outs[g][:, :]).then_inc(stored, 16)
            sp.wait_ge(stored, 32 * G + 1)
            sp.sem_inc(turn, 1)

        @block.vector
        def _(dve):
            ch = Chain(dve, step, 0)
            rows = [(row[g][:, 0:NF], row[g][:, NF:2 * NF]) for g in range(G)]
            for g in range(G):
                dve.wait_ge(row_in[g], 16 + 1)
            for turn_ in range(KTOP // 8):
                for g in range(G):
                    ch.behind(nc.vector.max(out=top[g][:, :], in_=rows[g][0]), G)
                for g in range(G):
                    ch.behind(nc.vector.match_replace(out=rows[g][0], in_to_replace=top[g][:, :], in_values=rows[g][0],
                                                      imm_value=-1.0), G)
            for g in range(G):
                ch.behind(nc.vector.tensor_scalar(outs[g][:, :], rows[g][0], 0.0, None, ALU.is_ge), G)
            for g in range(G):
                ch.behind(nc.vector.scalar_tensor_tensor(out=rows[g][1], in0=outs[g][:, :], scalar=NEG, in1=rows[g][1],
                                                         op0=ALU.mult, op1=ALU.add), G)
            for g in range(G):
                ch.behind(nc.vector.reduce_max(col[g][:, 0:1], rows[g][1], AX.X), G)
            for g in range(G):
                nc.vector.tensor_scalar(col[g][:, 1:2], col[g][:, 0:1], -1.0 / DH ** 0.5, None,
                                        ALU.mult).then_inc(max_ready, 1)
                if g + 1 < G:
                    dve.wait_ge(step, ch.k + 1)
            for g in range(G):
                dve.wait_ge(exp_ready, g + 1 + 1)
                ch.link(nc.vector.reciprocal(col[g][:, 3:4], col[g][:, 2:3]))
                nc.vector.tensor_scalar(prob[g][:, :], prob[g][:, :], col[g][:, 3:4], None,
                                        ALU.mult).then_inc(out_ready, 1)

        @block.scalar
        def _(act):
            for g in range(G):
                act.wait_ge(max_ready, g + 1 + 1)
                nc.scalar.activation(prob[g][:, :], row[g][:, NF:2 * NF], ACT.Exp, bias=col[g][:, 1:2],
                                     scale=1.0 / DH ** 0.5, accum_out=col[g][:, 2:3]).then_inc(exp_ready, 1)


def synthesis_stage(nc, w, cst, src, attn, outside, means, vspec, dst):
    with ExitStack() as ctx:
        sb = lambda name, shape, dt=F32: ctx.enter_context(nc.sbuf_tensor(f"sy_{name}", shape, dt))
        pair = lambda name, shape: tuple(sb(f"{name}_{part}", shape, F32R) for part in ("high", "low"))
        sems = []
        sem = lambda name: sems.append(ctx.enter_context(nc.semaphore(f"sy_{name}"))) or sems[-1]
        GS = 4
        R = GS * H
        G = B // GS
        x = [sb(f"x{u}", [P, 2, NJ * D]) for u in range(2)]
        at = [sb(f"at{u}", [H, NF]) for u in range(2)]
        at_s = [pair(f"at{u}", [H, 512]) for u in range(2)]
        out_rows = sb("out_rows", [R, NF])
        outT = sb("outT", [P, 4, R])
        outT_s = pair("outT", [P, 4, R])
        outT_nyq = sb("outT_nyq", [1, R])
        kc_s = pair("kc", [P, 2, 512])
        cind = sb("cind", [P, 2, KB, R])
        z = sb("z", [P, D])
        zb_s = pair("zb", [P, GS, D])
        av = sb("av", [P, KB, NF])
        av_s = pair("av", [P, KB, 512])
        avn = sb("avn", [P, KB])
        meansc = sb("meansc", [P, 2, KB, B])
        y_s = [pair(f"y{u}", [P, 5, D]) for u in range(2)]
        y0 = sb("y0", [1, D])
        rows0 = sb("rows0", [1, 2, D])
        cinv_s = pair("cinv", [P, 4 * 512])
        Wo_s = pair("Wo", [P, KB, D])
        sinv = sb("sinv", [P, 4 * 512])
        cnyq, indt, rowsel = sb("cnyq", [1, 512]), sb("indt", [H, KB * P]), sb("rowsel", [P, GS])
        cinv = x[1][:, :, :].rearrange("p h c -> p (h c)")
        small = [(t[:, :], cst[k]) for t, k in ((indt, "indt"), (rowsel, "rowsel"))]
        tables = [(cinv, cst["cinv"])] + [(t[:, :], cst[k]) for t, k in ((sinv, "sinv"), (cnyq, "cnyq"))]
        indt_r = sb("indt_r", [H, KB * P], F32R)
        ps = [ctx.enter_context(nc.psum_tensor(f"sy_ps{i}", [P, 512], F32)) for i in range(8)]
        pa, py, po, pn, pm = ps[0:2], ps[2:4], ps[4:6], ps[6], ps[7]
        x_in = [sem(f"x_in{u}") for u in range(2)]
        at_in = [sem(f"at_in{u}") for u in range(2)]
        x_out = [sem(f"x_out{u}") for u in range(2)]
        names = ("rows_in mean_ready cind_ready outT_in_psum outT_ready outT_split kc_in_psum kc_high kc_ready z_in_psum z_ready "
                 "zb_ready spread_ready av_ready av_high av_split at_high at_split y_in_psum y_high y_ready p_ready "
                 "p_used o_ready z_step row_step acc_step small_in tables_in tables_high tables_ready Wo_ready turn").split()
        S = {k: sem(k) for k in names}
        turn = S["turn"]
        start_at_one(nc, sems)
        ctx.callback(back_to_zero, nc, sems)
        block = ctx.enter_context(nc.Block())
        seq = src.rearrange("(b h p j) c -> b p h (j c)", b=B, h=2, j=NJ)
        oseq = dst.rearrange("(b h p j) c -> b p h (j c)", b=B, h=2, j=NJ)
        one = lambda ap, b: ap[bass.ds(b, 1), :, :, :].rearrange("a p h c -> (a p) h c")

        @block.sync
        def _(sp):
            def load_x(g, s):
                sp.dma_start(x[s % 2][:, :, :], one(seq, GS * g + s)).then_inc(x_in[s % 2], 16)

            def load_at(g, s):
                sp.dma_start(at[s % 2][:, :], attn[bass.ds((GS * g + s) * H, H), :]).then_inc(at_in[s % 2], 16)

            def load_rows(g):
                sp.dma_start(out_rows[:, :], outside[bass.ds(g * R, R), :]).then_inc(S["rows_in"], 16)

            def steps(g, more):
                for s in range(GS):
                    b = GS * g + s
                    if more and s == 1:
                        sp.wait_ge(S["outT_in_psum"], 5 * (g + 1) + 1)
                        sp.sem_inc(turn, 1)
                        load_rows(g + 1)
                    if more or s + 3 < GS:
                        sp.wait_ge(S["spread_ready"], 3 * (b + 2) + 1)
                        sp.sem_inc(turn, 1)
                        load_at(g + (s + 3) // GS, (s + 3) % GS)
                    sp.wait_ge(S["o_ready"], b + 1 + 1)
                    sp.sem_inc(turn, 1)
                    sp.dma_start(one(oseq, b), x[s % 2][:, :, :]).then_inc(x_out[s % 2], 16)
                    if more or s + 2 < GS:
                        sp.wait_ge(x_out[s % 2], 16 * (2 * g + s // 2 + 1) + 1)
                        sp.sem_inc(turn, 1)
                        load_x(g + (s + 2) // GS, (s + 2) % GS)

            for s in range(2):
                load_at(0, s)
            for dst_table, src_table in small:
                sp.dma_start(dst_table, src_table).then_inc(S["small_in"], 16)
            load_rows(0)
            for dst_table, src_table in tables:
                sp.dma_start(dst_table, src_table).then_inc(S["tables_in"], 16)
            load_x(0, 0)
            sp.wait_ge(S["spread_ready"], 3 + 1)
            load_at(0, 2)
            sp.wait_ge(S["tables_ready"], 1 + 1)
            load_x(0, 1)
            with sp.Fori(0, G - 1) as g:
                steps(g, True)
            steps(G - 1, False)
            for u in range(2):
                sp.wait_ge(x_out[u], 16 * (B // 2) + 1)

        @block.vector
        def _(dve):
            def spread_means(g):
                dve.wait_ge(S["z_in_psum"], g + 1)
                for c in range(2):
                    for m in range(KB):
                        ins = nc.vector.tensor_tensor(
                            cind[:, c, m, :].rearrange("p (s h) -> p s h", s=GS),
                            w["ind"][:, m * H:(m + 1) * H].unsqueeze(1).broadcast_to([P, GS, H]),
                            meansc[:, c, m, bass.ds(GS * g, GS)].unsqueeze(2).broadcast_to([P, GS, H]), ALU.mult)
                ins.then_inc(S["cind_ready"], 1)

            def rows_of_z(g):
                dve.wait_ge(S["z_ready"], g + 1 + 1)
                ch = Chain(dve, S["z_step"], g)
                for s in range(GS):
                    ins = nc.vector.tensor_scalar(zb_s[0][:, s, :], z[:, :], rowsel[:, s:s + 1], None, ALU.mult)
                ch.link(ins)
                for s in range(GS):
                    ins = nc.vector.scalar_tensor_tensor(out=zb_s[1][:, s, :], in0=z[:, :],
                                                         scalar=rowsel[:, s:s + 1], in1=zb_s[0][:, s, :],
                                                         op0=ALU.mult, op1=ALU.subtract)
                ins.then_inc(S["zb_ready"], 1)

            def rows_low(g):
                dve.wait_ge(S["outT_ready"], 3 * (g + 1) + 1)
                nc.vector.tensor_tensor(outT_s[1][:, :, :].rearrange("p i r -> p (i r)"), po[0][:, 0:4 * R],
                                        outT_s[0][:, :, :].rearrange("p i r -> p (i r)"),
                                        ALU.subtract).then_inc(S["outT_split"], 1)

            def kernels_low(g):
                for par in range(2):
                    dve.wait_ge(S["kc_high"], 2 * g + par + 1 + 1)
                    nc.vector.tensor_tensor(kc_s[1][:, par, :], po[par][:, :], kc_s[0][:, par, :],
                                            ALU.subtract).then_inc(S["kc_ready"], 1)

            def attend(b):
                dve.wait_ge(S["av_split"], b + 1)
                for m in range(KB):
                    dve.wait_ge(S["spread_ready"], 3 * b + m + 1 + 1)
                    nc.vector.tensor_tensor(av[:, m, 0:512], pa[m][:, :], vspec[:, m, bass.ds(b * NF, 512)],
                                            ALU.mult).then_inc(S["av_ready"], 1)
                dve.wait_ge(S["spread_ready"], 3 * b + 3 + 1)
                for m in range(KB):
                    ins = nc.vector.tensor_tensor(avn[:, m:m + 1], pn[:, m:m + 1],
                                                  vspec[:, m, bass.ds(b * NF + 512, 1)], ALU.mult)
                ins.then_inc(S["av_ready"], 1)

            def spectrum_low(b, u):
                hi, lo = y_s[u]
                dve.wait_ge(S["y_high"], 2 * b + 1 + 1)
                nc.vector.tensor_tensor(lo[:, 0:3:2, :], py[0][:, :].rearrange("p (a d) -> p a d", a=2),
                                        hi[:, 0:3:2, :], ALU.subtract)
                nc.vector.tensor_tensor(y0[0:1, :], py[0][0:1, 0:D], w["bo"][0:1, :], ALU.add)
                ch = Chain(dve, S["row_step"], 4 * b)
                ch.link(nc.vector.tensor_tensor(lo[:, 1, :], py[0][:, 0:D], hi[:, 1, :], ALU.subtract))
                dve.wait_ge(S["y_in_psum"], 3 * b + 2 + 1)
                nc.vector.tensor_tensor(rows0[0:1, 0, :], y0[0:1, :], pm[0:1, 0:D], ALU.add)
                ch.link(nc.vector.tensor_tensor(rows0[0:1, 1, :], y0[0:1, :], pm[0:1, 0:D], ALU.subtract))
                ch.link(nc.vector.tensor_copy(hi[0:1, 0:2, :], rows0[0:1, :, :]))
                ch.link(nc.vector.tensor_tensor(lo[0:1, 0:2, :], rows0[0:1, :, :], hi[0:1, 0:2, :], ALU.subtract))
                dve.wait_ge(S["y_high"], 2 * b + 2 + 1)
                nc.vector.tensor_tensor(lo[:, 3:5, :], py[1][:, :].rearrange("p (a d) -> p a d", a=2),
                                        hi[:, 3:5, :], ALU.subtract).then_inc(S["y_ready"], 1)

            def residual(g, b, s):
                dve.wait_ge(x_in[s % 2], 16 * (2 * g + s // 2 + 1) + 1)
                ch = Chain(dve, S["acc_step"], 4 * b)
                for jj in range(2):
                    cols = slice(jj * 512, (jj + 1) * 512)
                    x0, x1 = x[s % 2][:, 0, cols], x[s % 2][:, 1, cols]
                    dve.wait_ge(S["p_ready"], 4 * b + 2 * jj + 1 + 1)
                    nc.vector.tensor_tensor(x0, x0, po[0][:, :], ALU.add)
                    ch.link(nc.vector.tensor_tensor(x1, x1, po[0][:, :], ALU.add))
                    dve.sem_inc(S["p_used"], 1)
                    dve.wait_ge(S["p_ready"], 4 * b + 2 * jj + 2 + 1)
                    nc.vector.tensor_tensor(x0, x0, po[1][:, :], ALU.add)
                    ch.link(nc.vector.tensor_tensor(x1, x1, po[1][:, :], ALU.subtract))
                    dve.sem_inc(S["p_used"], 1)
                dve.sem_inc(S["o_ready"], 1)

            def steps(g, more):
                for s in range(GS):
                    b = GS * g + s
                    if more or s + 1 < GS:
                        spectrum_low(b + 1, (s + 1) % 2)
                    if s == 0:
                        kernels_low(g)
                    if more and s == 3:
                        rows_low(g + 1)
                    if more or s + 2 < GS:
                        attend(b + 2)
                    residual(g, b, s)
                    if more and s == 2:
                        spread_means(g + 1)
                    if more and s == 3:
                        rows_of_z(g + 1)

            nc.vector.tensor_scalar(meansc[:, :, :, :], means[:, :, :, :], 1.0 / NF, None, ALU.mult).then_inc(S["mean_ready"], 1)
            dve.wait_ge(S["mean_ready"], 1 + 1)
            spread_means(0)
            attend(0)
            rows_low(0)
            dve.wait_ge(S["small_in"], 16 * len(small) + 1)
            rows_of_z(0)
            dve.wait_ge(S["tables_high"], 3 + 1)
            nc.vector.tensor_tensor(cinv_s[1][:, :], cinv, cinv_s[0][:, :], ALU.subtract).then_inc(S["tables_ready"], 1)
            spectrum_low(0, 0)
            attend(1)
            with dve.Fori(0, G - 1) as g:
                steps(g, True)
            steps(G - 1, False)

        @block.scalar
        def _(act):
            def prepared_out(g):
                act.wait_ge(S["outT_in_psum"], 5 * g + 5 + 1)
                nc.scalar.copy(outT[:, :, :].rearrange("p i r -> p (i r)"), po[0][:, 0:4 * R]).then_inc(S["outT_ready"], 1)
                nc.scalar.copy(outT_s[0][:, :, :].rearrange("p i r -> p (i r)"),
                               po[0][:, 0:4 * R]).then_inc(S["outT_ready"], 1)
                nc.scalar.copy(outT_nyq[:, :], po[0][0:1, 4 * R:5 * R]).then_inc(S["outT_ready"], 1)
                act.wait_ge(S["zb_ready"], g + 1)
                act.wait_ge(S["z_in_psum"], g + 1 + 1)
                nc.scalar.copy(z[:, :], po[1][:, 0:D]).then_inc(S["z_ready"], 1)

            def kernels_high(g):
                for par in range(2):
                    act.wait_ge(S["kc_in_psum"], 2 * g + par + 1 + 1)
                    nc.scalar.copy(kc_s[0][:, par, :], po[par][:, :]).then_inc(S["kc_high"], 1)

            def at_high(g, s):
                act.wait_ge(at_in[s % 2], 16 * (2 * g + s // 2 + 1) + 1)
                nc.scalar.copy(at_s[s % 2][0][:, :], at[s % 2][:, 0:512]).then_inc(S["at_high"], 1)

            def av_high(b):
                for m in range(KB):
                    act.wait_ge(S["av_ready"], 3 * b + m + 1 + 1)
                    nc.scalar.copy(av_s[0][:, m, :], av[:, m, 0:512]).then_inc(S["av_high"], 1)

            def spectrum_high(b, u):
                hi = y_s[u][0]
                act.wait_ge(S["y_in_psum"], 3 * b + 1 + 1)
                nc.scalar.copy(hi[:, 0:3:2, :], py[0][:, :].rearrange("p (a d) -> p a d", a=2))
                nc.scalar.copy(hi[:, 1, :], py[0][:, 0:D]).then_inc(S["y_high"], 1)
                act.wait_ge(S["y_in_psum"], 3 * b + 3 + 1)
                nc.scalar.copy(hi[:, 3:5, :], py[1][:, :].rearrange("p (a d) -> p a d", a=2)).then_inc(S["y_high"], 1)

            def steps(g, more):
                for s in range(GS):
                    b = GS * g + s
                    if more or s + 1 < GS:
                        spectrum_high(b + 1, (s + 1) % 2)
                    if more and s == 3:
                        prepared_out(g + 1)
                    if s == 0:
                        kernels_high(g)
                    if more or s + 2 < GS:
                        av_high(b + 2)
                    if more or s + 3 < GS:
                        at_high(g + (s + 3) // GS, (s + 3) % GS)

            at_high(0, 0)
            nc.scalar.copy(Wo_s[0][:, :, :], w["Wo"][:, :, :]).then_inc(S["tables_high"], 1)
            at_high(0, 1)
            act.wait_ge(S["small_in"], 16 * len(small) + 1)
            nc.scalar.copy(indt_r[:, :], indt[:, :]).then_inc(S["tables_high"], 1)
            av_high(0)
            prepared_out(0)
            act.wait_ge(S["tables_in"], 16 * len(tables) + 1)
            nc.scalar.copy(cinv_s[0][:, :], cinv).then_inc(S["tables_high"], 1)
            spectrum_high(0, 0)
            av_high(1)
            at_high(0, 2)
            with act.Fori(0, G - 1) as g:
                steps(g, True)
            steps(G - 1, False)

        @block.gpsimd
        def _(pool):
            def at_low(b, s):
                pool.wait_ge(S["at_high"], b + 1 + 1)
                nc.gpsimd.tensor_tensor(at_s[s % 2][1][:, :], at[s % 2][:, 0:512], at_s[s % 2][0][:, :],
                                        ALU.subtract).then_inc(S["at_split"], 1)

            def av_low(b):
                for m in range(KB):
                    pool.wait_ge(S["av_high"], KB * b + m + 1 + 1)
                    ins = nc.gpsimd.tensor_tensor(av_s[1][:, m, :], av[:, m, 0:512], av_s[0][:, m, :],
                                                  ALU.subtract)
                ins.then_inc(S["av_split"], 1)

            def steps(g, more):
                for s in range(GS):
                    b = GS * g + s
                    if more or s + 2 < GS:
                        av_low(b + 2)
                    if more or s + 3 < GS:
                        at_low(b + 3, (s + 3) % GS)

            at_low(0, 0)
            pool.wait_ge(S["tables_high"], 1 + 1)
            nc.gpsimd.tensor_tensor(Wo_s[1][:, :, :], w["Wo"][:, :, :], Wo_s[0][:, :, :],
                                    ALU.subtract).then_inc(S["Wo_ready"], 1)
            at_low(1, 1)
            av_low(0)
            av_low(1)
            at_low(2, 2)
            with pool.Fori(0, G - 1) as g:
                steps(g, True)
            steps(G - 1, False)

        @block.tensor
        def _(pe):
            def prepare(g):
                pe.wait_ge(S["rows_in"], 16 * (g + 1) + 1)
                pe.sem_inc(turn, 1)
                for par in range(2):
                    for qt in range(2):
                        i = 2 * par + qt
                        lo = 256 * qt + par
                        nc.tensor.transpose(po[0][:, i * R:(i + 1) * R], out_rows[:, lo:lo + 255:2],
                                            w["ident"][0:R, 0:R]).then_inc(S["outT_in_psum"], 1)
                nc.tensor.transpose(po[0][0:1, 4 * R:5 * R], out_rows[:, 512:513],
                                    w["ident"][0:R, 0:R]).then_inc(S["outT_in_psum"], 1)
                pe.wait_ge(S["cind_ready"], g + 1 + 1)
                for c in range(2):
                    for m in range(KB):
                        ins = nc.tensor.matmul(po[1][c * R:(c + 1) * R, 0:D], cind[:, c, m, :], w["Wo"][:, m, :],
                                               start=(m == 0), stop=(m == KB - 1))
                ins.then_inc(S["z_in_psum"], 1)

            def kernels(g):
                pe.wait_ge(S["p_used"], 4 * GS * g + 1)
                pe.wait_ge(S["outT_ready"], 3 * (g + 1) + 1)
                pe.wait_ge(S["outT_split"], g + 1 + 1)
                pe.wait_ge(S["z_ready"], g + 1 + 1)
                for par in range(2):
                    for c in range(2):
                        nyq = par == 0 and c == 0
                        for qt in range(2):
                            i = 2 * par + qt
                            out, cols = po[par][c * R:(c + 1) * R, :], slice(i * 512, (i + 1) * 512)
                            if c == 0:
                                ins = split_product(nc, out, [v[:, i, :] for v in outT_s], [v[:, cols] for v in cinv_s],
                                              qt == 0, qt == 1 and not nyq)
                            else:
                                ins = nc.tensor.matmul(out, outT[:, i, :], sinv[:, cols], start=(qt == 0),
                                                       stop=(qt == 1))
                        if nyq:
                            ins = nc.tensor.matmul(po[par][0:R, :], outT_nyq[:, :], cnyq[:, :],
                                                   start=False, stop=True)
                    ins.then_inc(S["kc_in_psum"], 1)

            def spread(b, s):
                pe.wait_ge(S["at_split"], b + 1 + 1)
                pe.wait_ge(S["av_ready"], 3 * b + 1)
                for m in range(KB):
                    for part in range(2):
                        ins = nc.tensor.matmul(pa[m][:, :], indt_r[:, m * P:(m + 1) * P], at_s[s % 2][part][:, :],
                                               start=(part == 0), stop=(part == 1))
                    ins.then_inc(S["spread_ready"], 1)
                for m in range(KB):
                    ins = nc.tensor.matmul(pn[:, m:m + 1], indt[:, m * P:(m + 1) * P], at[s % 2][:, 512:513],
                                           start=True, stop=True)
                ins.then_inc(S["spread_ready"], 1)

            def project(b):
                pe.wait_ge(S["av_split"], b + 1 + 1)
                pe.wait_ge(S["av_ready"], 3 * (b + 1) + 1)
                pe.wait_ge(S["y_ready"], b + 1)
                for par in range(2):
                    for qt in range(2):
                        lo = 256 * qt + par
                        for m in range(KB):
                            ins = split_product(nc, py[par][:, qt * D:(qt + 1) * D], [v[:, m, lo:lo + 255:2] for v in av_s],
                                          [v[:, m, :] for v in Wo_s], m == 0, m == KB - 1)
                    ins.then_inc(S["y_in_psum"], 1)
                    if par == 0:
                        for m in range(KB):
                            ins = nc.tensor.matmul(pm[0:1, 0:D], avn[:, m:m + 1], w["Wo"][:, m, :],
                                                   start=(m == 0), stop=(m == KB - 1))
                        ins.then_inc(S["y_in_psum"], 1)

            def inverse(b, s):
                pe.wait_ge(S["y_ready"], b + 1 + 1)
                for jj in range(2):
                    for par in range(2):
                        if jj == 0:
                            pe.wait_ge(S["p_used"], 4 * b + 1)
                        else:
                            pe.wait_ge(S["p_used"], 4 * b + par + 1 + 1)
                        for j in (2 * jj, 2 * jj + 1):
                            out = po[par][:, (j % 2) * D:(j % 2 + 1) * D]
                            for qt in range(2):
                                i = 2 * par + qt
                                yt = 1 if (par == 0 and qt == 0 and j % 2 == 1) else (0, 2, 3, 4)[i]
                                split_product(nc, out, [v[:, i * 512 + j * P:i * 512 + (j + 1) * P] for v in cinv_s],
                                        [v[:, yt, :] for v in y_s[s % 2]], qt == 0, False)
                            ins = split_product(nc, out, [v[:, par, j * P:(j + 1) * P] for v in kc_s],
                                          [v[:, s, :] for v in zb_s], False, True)
                        ins.then_inc(S["p_ready"], 1)

            def steps(g, more):
                for s in range(GS):
                    b = GS * g + s
                    if more or s + 1 < GS:
                        project(b + 1)
                    if s == 0:
                        kernels(g)
                    if more and s == 3:
                        pe.wait_ge(S["p_used"], 4 * b + 1)
                        pe.sem_inc(turn, 1)
                        prepare(g + 1)
                    if more or s + 2 < GS:
                        spread(b + 2, (s + 2) % GS)
                    if s == 0:
                        pe.wait_ge(S["kc_ready"], 2 * (g + 1) + 1)
                        pe.wait_ge(S["zb_ready"], g + 1 + 1)
                    if more and s == 3:
                        pe.wait_ge(S["outT_ready"], 3 * (g + 2) + 1)
                        pe.wait_ge(S["outT_split"], g + 2 + 1)
                        pe.wait_ge(S["z_ready"], g + 2 + 1)
                    inverse(b, s)

            pe.wait_ge(S["tables_high"], 2 + 1)
            spread(0, 0)
            prepare(0)
            pe.wait_ge(S["Wo_ready"], 1 + 1)
            project(0)
            spread(1, 1)
            pe.wait_ge(S["tables_ready"], 1 + 1)
            pe.wait_ge(S["tables_in"], 16 * len(tables) + 1)
            with pe.Fori(0, G - 1) as g:
                steps(g, True)
            steps(G - 1, False)


def build(nc, args, cst, out):
    x1 = nc.dram_tensor("x1", (B * L, D), F32, kind="Internal").ap()
    x2 = nc.dram_tensor("x2", (B * L, D), F32, kind="Internal").ap()
    es = nc.dram_tensor("energy_score", (B * H, 2 * NF), F32, kind="Internal").ap()
    attn = nc.dram_tensor("attn", (B * H, NF), F32, kind="Internal").ap()
    outside = nc.dram_tensor("outside", (B * H, NF), F32, kind="Internal").ap()
    query = args["L0_attn_query"].rearrange("b l d -> (b l) d")
    out = out.rearrange("b l d -> (b l) d")
    with ExitStack() as ctx:
        w = {}
        for k in KEPT:
            w[k] = ctx.enter_context(nc.sbuf_tensor(f"w_{k}", list(cst[k].shape), cst[k].dtype))
        w["Wo"] = ctx.enter_context(nc.sbuf_tensor("w_Wo", [P, KB, D], F32))
        w["bias"] = ctx.enter_context(nc.sbuf_tensor("w_bias", [P, 3, KB], F32))
        w["bo"] = ctx.enter_context(nc.sbuf_tensor("w_bo", [1, D], F32))
        w["gate"] = ctx.enter_context(nc.sbuf_tensor("w_gate", [P, KB * E], F32))
        w["expert"] = ctx.enter_context(nc.sbuf_tensor("w_expert", [P, KB, E * D], F32))
        sw_sems = [ctx.enter_context(nc.semaphore(f"software_dma{k}")) for k in range(2 * EXPERT_BUFFERS)]
        with ExitStack() as first:
            experts = Experts(nc, first, w)
            setup_weights(nc, w, args, cst, experts)
            routed_experts(nc, "ffn1", w, sw_sems, 0, query, x1, experts)
        with ExitStack() as mid:
            means = mid.enter_context(nc.sbuf_tensor("means", [P, 2, KB, B], F32))
            vspec = mid.enter_context(nc.sbuf_tensor("vspec", [P, KB, B * NF], F32))
            spectra_stage(nc, w, cst, args, x1, es, means, vspec)
            selection_stage(nc, es, attn, outside)
            synthesis_stage(nc, w, cst, x1, attn, outside, means, vspec, x2)
        routed_experts(nc, "ffn2", w, sw_sems, 1, x2, out)


_INS = ["L0_attn_query", "L0_attn_Wq", "L0_attn_bq", "L0_attn_Wk", "L0_attn_bk", "L0_attn_Wv", "L0_attn_bv",
        "L0_attn_Wo", "L0_attn_bo", "L0_ffn_gate_w", "L0_ffn_expert_w"]


def kernel(**inputs):
    import concourse.bacc as bacc
    from concourse.bass_utils import run_bass_kernel_spmd

    nc = bacc.Bacc("TRN2", target_bir_lowering=False, num_devices=1)
    arrays, args, cst = {}, {}, {}
    for name in _INS:
        a = np.ascontiguousarray(inputs[name])
        arrays[name + "_dram"] = a
        args[name] = nc.dram_tensor(name + "_dram", a.shape, mybir.dt.from_np(a.dtype), kind="ExternalInput").ap()
    for name, a in constants().items():
        arrays["c_" + name] = a
        cst[name] = nc.dram_tensor("c_" + name, a.shape, mybir.dt.from_np(a.dtype), kind="ExternalInput").ap()
    out = nc.dram_tensor("out_dram", (B, L, D), F32, kind="ExternalOutput").ap()
    build(nc, args, cst, out)
    r = run_bass_kernel_spmd(nc, [arrays], core_ids=[0])
    return r.results[0]["out_dram"]
```
